# Optimizing a Trainium2 kernel written in Bass

```python
import numpy as np
import jax
import jax.numpy as jnp

def _softmax(x, axis=-1):
    return jax.nn.softmax(x, axis=axis)

def _gelu(x):
    return jax.nn.gelu(x, approximate=True)

def _silu(x):
    return jax.nn.silu(x)

def _sigmoid(x):
    return jax.nn.sigmoid(x)

def _layernorm(x, axis=-1, eps=1e-05):
    m = jnp.mean(x, axis=axis, keepdims=True)
    v = jnp.var(x, axis=axis, keepdims=True)
    return (x - m) / jnp.sqrt(v + eps)

def _scatter_add(tgt, idx, src, axis=0):
    return tgt.at[idx].add(src)

def _segment_sum(src, seg, n):
    return jax.ops.segment_sum(src, seg, n)
kernel_name = 'mk_gnn_preln_d4_gnn_r64_a08bd0'

def setup_inputs(seed: int=0):
    np.random.seed(seed)
    _w = jnp.asarray

    def _rec_inputs():
        import jax
        import jax.numpy as jnp
        _gk = jax.random.key(seed)
        x = -0.0003713 + 1 * jax.random.normal(jax.random.fold_in(_gk, 1), (50000, 128), jnp.float32)
        src = jax.random.randint(jax.random.fold_in(_gk, 2), (12500,), 0, 50000, jnp.int32)
        dst = jax.random.randint(jax.random.fold_in(_gk, 3), (12500,), 0, 50000, jnp.int32)
        _o = jnp.argsort(dst, stable=True)
        src = src[_o]
        dst = dst[_o]
        return (x, src, dst)
    x, src, dst = _rec_inputs()

    def _L0_gnn_setup():
        import jax, jax.numpy as jnp
        import numpy as np
        N_NODES = 100000
        NUM_HEADS = 8
        FOUT = 16
        FIN = 128
        N_EDGES = 25000
        ELU_ALPHA = 0.2

        def elu(x, alpha):
            return jnp.where(x > 0, x, alpha * (jnp.exp(x) - 1.0))
        key = jax.random.key(seed)
        k1, k2, k3, k4, k5 = jax.random.split(key, 5)
        x = jax.random.normal(k1, (N_NODES, FIN), dtype=jnp.float32)
        W = jax.random.normal(k2, (FIN, NUM_HEADS * FOUT), dtype=jnp.float32) * (1.0 / np.sqrt(FIN))
        source_scorer = jax.random.normal(k3, (NUM_HEADS, 1, FOUT), dtype=jnp.float32) * 0.1
        target_scorer = jax.random.normal(k4, (NUM_HEADS, 1, FOUT), dtype=jnp.float32) * 0.1
        edge_index = jax.random.randint(k5, (N_EDGES, 2), 0, N_NODES, dtype=jnp.int32)
        return {'x': x, 'W': W, 'source_scorer': source_scorer, 'target_scorer': target_scorer, 'edge_index': edge_index}
    _L0_gnn_all = _L0_gnn_setup()
    _L0_gnn_in = {k: v for k, v in _L0_gnn_all.items() if k in ('W', 'source_scorer', 'target_scorer')}
    del _L0_gnn_all

    def _L1_gnn_setup():
        import jax, jax.numpy as jnp
        import numpy as np
        N = 50000
        E = 12500
        DIN, DH, DOUT, DCTX = (128, 128, 128, 64)

        def gcn_conv(x, src, dst, W, b):
            n = x.shape[0]
            h = x @ W
            loop = jnp.arange(n, dtype=src.dtype)
            s = jnp.concatenate([src, loop])
            d = jnp.concatenate([dst, loop])
            deg = jax.ops.segment_sum(jnp.ones(s.shape, h.dtype), d, num_segments=n)
            dinv = jax.lax.rsqrt(jnp.maximum(deg, 1.0))
            norm = dinv[s] * dinv[d]
            msgs = h[s] * norm[:, None]
            return jax.ops.segment_sum(msgs, d, num_segments=n) + b
        key = jax.random.key(seed)
        ks = jax.random.split(key, 8)
        x = jax.random.normal(ks[0], (N, DIN), jnp.float32)
        edge_index = jax.random.randint(ks[1], (2, E), 0, N, dtype=jnp.int64)
        ctx = jax.random.normal(ks[2], (1, DCTX), jnp.float32)
        init = lambda k, shp, fan: jax.random.normal(k, shp, jnp.float32) / np.sqrt(fan).astype(np.float32)
        W1 = init(ks[3], (DIN, DH), DIN)
        b1 = jnp.zeros((DH,), jnp.float32)
        W2 = init(ks[4], (DH, DOUT), DH)
        b2 = jnp.zeros((DOUT,), jnp.float32)
        Wg = init(ks[5], (DCTX, DOUT), DCTX)
        bg = jnp.zeros((DOUT,), jnp.float32)
        Wb = init(ks[6], (DCTX, DOUT), DCTX)
        return {'x': x, 'ctx': ctx, 'W1': W1, 'b1': b1, 'W2': W2, 'b2': b2, 'Wg': Wg, 'bg': bg, 'Wb': Wb, 'edge_index': edge_index}
    _L1_gnn_all = _L1_gnn_setup()
    _L1_gnn_in = {k: v for k, v in _L1_gnn_all.items() if k in ('ctx', 'W1', 'b1', 'W2', 'b2', 'Wg', 'bg', 'Wb')}
    del _L1_gnn_all

    def _L2_gnn_setup():
        import jax, jax.numpy as jnp
        import numpy as np
        N_NODES = 50000
        N_EDGES = 12500
        D_H = 128
        D_MSG = 128

        def _linear_params(key, d_in, d_out):
            kw, kb = jax.random.split(key)
            bound = 1.0 / np.sqrt(d_in)
            W = jax.random.uniform(kw, (d_in, d_out), minval=-bound, maxval=bound, dtype=jnp.float32)
            b = jax.random.uniform(kb, (d_out,), minval=-bound, maxval=bound, dtype=jnp.float32)
            return (W, b)
        key = jax.random.key(seed)
        k_h, k_e, k1, k2, k3, k4 = jax.random.split(key, 6)
        h = jax.random.normal(k_h, (N_NODES, D_H), dtype=jnp.float32)
        edge_index = jax.random.randint(k_e, (2, N_EDGES), 0, N_NODES, dtype=jnp.int32)
        W_msg1, b_msg1 = _linear_params(k1, 2 * D_H, D_MSG)
        W_msg2, b_msg2 = _linear_params(k2, D_MSG, D_MSG)
        W_upd1, b_upd1 = _linear_params(k3, D_H + D_MSG, D_H)
        W_upd2, b_upd2 = _linear_params(k4, D_H, D_H)
        return {'h': h, 'edge_index': edge_index, 'W_msg1': W_msg1, 'b_msg1': b_msg1, 'W_msg2': W_msg2, 'b_msg2': b_msg2, 'W_upd1': W_upd1, 'b_upd1': b_upd1, 'W_upd2': W_upd2, 'b_upd2': b_upd2}
    _L2_gnn_all = _L2_gnn_setup()
    _L2_gnn_in = {k: v for k, v in _L2_gnn_all.items() if k in ('W_msg1', 'b_msg1', 'W_msg2', 'b_msg2', 'W_upd1', 'b_upd1', 'W_upd2', 'b_upd2')}
    del _L2_gnn_all

    def _L3_gnn_setup():
        import jax, jax.numpy as jnp
        import numpy as np
        N_NODES = 50000
        N_EDGES = 12500
        D_IN = 128
        D_HID = 256
        EPS = 0.0
        key = jax.random.key(seed)
        k1, k2, k3, k4 = jax.random.split(key, 4)
        x = jax.random.normal(k1, (N_NODES, D_IN), dtype=jnp.float32)
        edge_index = jax.random.randint(k2, (2, N_EDGES), 0, N_NODES, dtype=jnp.int64)
        W1 = jax.random.normal(k3, (D_IN, D_HID), dtype=jnp.float32) * (1.0 / np.sqrt(D_IN))
        b1 = jnp.zeros((D_HID,), dtype=jnp.float32)
        W2 = jax.random.normal(k4, (D_HID, D_IN), dtype=jnp.float32) * (1.0 / np.sqrt(D_HID))
        b2 = jnp.zeros((D_IN,), dtype=jnp.float32)
        return {'x': x, 'edge_index': edge_index, 'W1': W1, 'b1': b1, 'W2': W2, 'b2': b2}
    _L3_gnn_all = _L3_gnn_setup()
    _L3_gnn_in = {k: v for k, v in _L3_gnn_all.items() if k in ('W1', 'b1', 'W2', 'b2')}
    del _L3_gnn_all
    return {'x': x, 'src': src, 'dst': dst, 'L0_gnn_W': _L0_gnn_in['W'], 'L0_gnn_source_scorer': _L0_gnn_in['source_scorer'], 'L0_gnn_target_scorer': _L0_gnn_in['target_scorer'], 'L1_gnn_ctx': _L1_gnn_in['ctx'], 'L1_gnn_W1': _L1_gnn_in['W1'], 'L1_gnn_b1': _L1_gnn_in['b1'], 'L1_gnn_W2': _L1_gnn_in['W2'], 'L1_gnn_b2': _L1_gnn_in['b2'], 'L1_gnn_Wg': _L1_gnn_in['Wg'], 'L1_gnn_bg': _L1_gnn_in['bg'], 'L1_gnn_Wb': _L1_gnn_in['Wb'], 'L2_gnn_W_msg1': _L2_gnn_in['W_msg1'], 'L2_gnn_b_msg1': _L2_gnn_in['b_msg1'], 'L2_gnn_W_msg2': _L2_gnn_in['W_msg2'], 'L2_gnn_b_msg2': _L2_gnn_in['b_msg2'], 'L2_gnn_W_upd1': _L2_gnn_in['W_upd1'], 'L2_gnn_b_upd1': _L2_gnn_in['b_upd1'], 'L2_gnn_W_upd2': _L2_gnn_in['W_upd2'], 'L2_gnn_b_upd2': _L2_gnn_in['b_upd2'], 'L3_gnn_W1': _L3_gnn_in['W1'], 'L3_gnn_b1': _L3_gnn_in['b1'], 'L3_gnn_W2': _L3_gnn_in['W2'], 'L3_gnn_b2': _L3_gnn_in['b2']}

def reference(x, src, dst, L0_gnn_W, L0_gnn_source_scorer, L0_gnn_target_scorer, L1_gnn_ctx, L1_gnn_W1, L1_gnn_b1, L1_gnn_W2, L1_gnn_b2, L1_gnn_Wg, L1_gnn_bg, L1_gnn_Wb, L2_gnn_W_msg1, L2_gnn_b_msg1, L2_gnn_W_msg2, L2_gnn_b_msg2, L2_gnn_W_upd1, L2_gnn_b_upd1, L2_gnn_W_upd2, L2_gnn_b_upd2, L3_gnn_W1, L3_gnn_b1, L3_gnn_W2, L3_gnn_b2):
    import jax
    import jax.numpy as jnp

    def _L0_gnn_ref(x, W, source_scorer, target_scorer, edge_index):
        import jax, jax.numpy as jnp
        import numpy as np
        N_NODES = 100000
        NUM_HEADS = 8
        FOUT = 16
        FIN = 128
        N_EDGES = 25000
        ELU_ALPHA = 0.2

        def elu(x, alpha):
            return jnp.where(x > 0, x, alpha * (jnp.exp(x) - 1.0))
        N = x.shape[0]
        feats = (x @ W).reshape(NUM_HEADS, N, FOUT)
        src_score = jnp.einsum('hnf,hf->hn', feats, source_scorer[:, 0, :])
        tgt_score = jnp.einsum('hnf,hf->hn', feats, target_scorer[:, 0, :])
        src, tgt = (edge_index[:, 0], edge_index[:, 1])
        e_feats = feats[:, src, :]
        e_scores = src_score[:, src] + tgt_score[:, tgt]
        e_scores = elu(e_scores, ELU_ALPHA)
        exp_s = jnp.exp(e_scores)
        denom = jax.vmap(lambda s: jax.ops.segment_sum(s, tgt, num_segments=N))(exp_s)
        att = exp_s / denom[:, tgt]
        weighted = e_feats * att[:, :, None]
        out = jax.vmap(lambda w: jax.ops.segment_sum(w, tgt, num_segments=N))(weighted)
        return jnp.transpose(out, (1, 0, 2)).reshape(N, NUM_HEADS * FOUT)

    def _L1_gnn_ref(x, ctx, W1, b1, W2, b2, Wg, bg, Wb, edge_index):
        import jax, jax.numpy as jnp
        import numpy as np
        N = 50000
        E = 12500
        DIN, DH, DOUT, DCTX = (128, 128, 128, 64)

        def gcn_conv(x, src, dst, W, b):
            n = x.shape[0]
            h = x @ W
            loop = jnp.arange(n, dtype=src.dtype)
            s = jnp.concatenate([src, loop])
            d = jnp.concatenate([dst, loop])
            deg = jax.ops.segment_sum(jnp.ones(s.shape, h.dtype), d, num_segments=n)
            dinv = jax.lax.rsqrt(jnp.maximum(deg, 1.0))
            norm = dinv[s] * dinv[d]
            msgs = h[s] * norm[:, None]
            return jax.ops.segment_sum(msgs, d, num_segments=n) + b
        src, dst = (edge_index[0], edge_index[1])
        gate = jax.nn.sigmoid(ctx @ Wg + bg)
        bias = ctx @ Wb
        h = jax.nn.leaky_relu(gcn_conv(x, src, dst, W1, b1), negative_slope=0.2)
        out = gcn_conv(h, src, dst, W2, b2)
        return out * gate + bias

    def _L2_gnn_ref(h, edge_index, W_msg1, b_msg1, W_msg2, b_msg2, W_upd1, b_upd1, W_upd2, b_upd2):
        import jax, jax.numpy as jnp
        import numpy as np
        N_NODES = 50000
        N_EDGES = 12500
        D_H = 128
        D_MSG = 128

        def _linear_params(key, d_in, d_out):
            kw, kb = jax.random.split(key)
            bound = 1.0 / np.sqrt(d_in)
            W = jax.random.uniform(kw, (d_in, d_out), minval=-bound, maxval=bound, dtype=jnp.float32)
            b = jax.random.uniform(kb, (d_out,), minval=-bound, maxval=bound, dtype=jnp.float32)
            return (W, b)
        src, dst = (edge_index[0], edge_index[1])
        e = jnp.concatenate([h[src], h[dst]], axis=-1)
        m = jax.nn.silu(e @ W_msg1 + b_msg1) @ W_msg2 + b_msg2
        agg = jax.ops.segment_sum(m, dst, num_segments=h.shape[0])
        u = jnp.concatenate([h, agg], axis=-1)
        return jax.nn.silu(u @ W_upd1 + b_upd1) @ W_upd2 + b_upd2

    def _L3_gnn_ref(x, edge_index, W1, b1, W2, b2):
        import jax, jax.numpy as jnp
        import numpy as np
        N_NODES = 50000
        N_EDGES = 12500
        D_IN = 128
        D_HID = 256
        EPS = 0.0
        src = edge_index[0]
        dst = edge_index[1]
        agg = jax.ops.segment_sum(x[src], dst, num_segments=x.shape[0])
        h = (1.0 + EPS) * x + agg
        h = jnp.maximum(h @ W1 + b1, 0.0)
        return h @ W2 + b2
    edge_index = jnp.stack([src, dst])
    edge_index_t = jnp.stack([src, dst], axis=1)
    h = jnp.maximum(_layernorm(x, axis=-1), 0.0)
    x = x + _L0_gnn_ref(h, L0_gnn_W, L0_gnn_source_scorer, L0_gnn_target_scorer, edge_index_t)
    h = jnp.maximum(_layernorm(x, axis=-1), 0.0)
    x = x + _L1_gnn_ref(h, L1_gnn_ctx, L1_gnn_W1, L1_gnn_b1, L1_gnn_W2, L1_gnn_b2, L1_gnn_Wg, L1_gnn_bg, L1_gnn_Wb, edge_index)
    h = jnp.maximum(_layernorm(x, axis=-1), 0.0)
    x = x + _L2_gnn_ref(h, edge_index, L2_gnn_W_msg1, L2_gnn_b_msg1, L2_gnn_W_msg2, L2_gnn_b_msg2, L2_gnn_W_upd1, L2_gnn_b_upd1, L2_gnn_W_upd2, L2_gnn_b_upd2)
    h = jnp.maximum(_layernorm(x, axis=-1), 0.0)
    x = x + _L3_gnn_ref(h, edge_index, L3_gnn_W1, L3_gnn_b1, L3_gnn_W2, L3_gnn_b2)
    return x

_drawn_inputs = setup_inputs


def setup_inputs(seed=0):
    import zlib

    import numpy as np

    out = dict(_drawn_inputs(seed))
    spreads = {'L1_gnn_b1': (0.0, 0.1),
     'L1_gnn_b2': (0.0, 0.1),
     'L1_gnn_bg': (0.0, 0.8),
     'L3_gnn_b1': (0.0, 0.1),
     'L3_gnn_b2': (0.0, 0.1)}
    factors = {'L0_gnn_source_scorer': 7.489,
     'L0_gnn_target_scorer': 8.0,
     'L2_gnn_W_msg1': 8.0,
     'L2_gnn_b_msg1': 8.0,
     'L2_gnn_W_msg2': 8.0,
     'L2_gnn_b_msg2': 8.0,
     'L2_gnn_b_upd1': 7.25}
    for name, (base, spread) in spreads.items():
        noise = np.random.default_rng([zlib.crc32(name.encode()), seed]).standard_normal(out[name].shape)
        drawn = base * np.exp(spread * noise) if base else spread * noise
        out[name] = jnp.asarray(drawn.astype(out[name].dtype))
    for name, factor in factors.items():
        out[name] = (out[name] * factor).astype(out[name].dtype)
    return out
```

```python
import concourse.bass as bass
from concourse import mybir
from contextlib import ExitStack, contextmanager
from collections import namedtuple


def gnn_four_layers(nc, T, out):
    f32, i32, bf16 = mybir.dt.float32, mybir.dt.int32, mybir.dt.bfloat16
    ALU = mybir.AluOpType
    ACT = mybir.ActivationFunctionType
    AX = mybir.AxisListType

    x_in, src_in, dst_in = T["x"], T["src"], T["dst"]
    N, D = x_in.shape
    E = src_in.shape[0]
    H, F = T["L0_gnn_source_scorer"].shape[0], T["L0_gnn_source_scorer"].shape[2]
    P = 125
    TG = 4
    GR = P * TG
    NT, NG = E // P, E // GR
    ND = N // GR
    J = N // H
    NJ = J // P
    GPN = D // F
    GW = D + 2 * H
    MW = D + H + 1
    NOWHERE = 1 << 17
    EPS = 1e-5
    assert E % GR == 0 and N % GR == 0 and J % P == 0 and GPN * F == D and H * F == D

    def dram(name, shape, dt=f32):
        return nc.dram_tensor(name, shape, dt, kind="Internal").ap()

    feat_tab = dram("feat_tab", (N, GW))
    slot_of = dram("slot_of", (N, 1), i32)
    xsrc_d = dram("xsrc_d", (E, D))
    xn0_src = dram("xn0_src", (E, D))
    hid_src = dram("hid_src", (E, D))
    xn2_src = dram("xn2_src", (E, D))
    xn3_src = dram("xn3_src", (E, D))
    tab1 = dram("tab1", (E, D))
    tab2 = dram("tab2", (E, D))
    tab3 = dram("tab3", (E, D))
    tab4 = dram("tab4", (E, D))
    x1_dst = dram("x1_dst", (E, D))
    x2_dst = dram("x2_dst", (E, D))
    x3_dst = dram("x3_dst", (E, D))

    def slots(t):
        return t.rearrange("(n t p) d -> n p t d", p=P, t=TG)

    def rows(t):
        return t.rearrange("(n p t) d -> n p t d", p=P, t=TG)

    CUTS = ((0, 112), (112, P))
    DONE = 16 * len(CUTS)

    def move(eng, tile, view, sem, store=False):
        for a, z in CUTS:
            if store:
                eng.dma_start(view[a:z], tile[a:z]).then_inc(sem, 16)
            else:
                eng.dma_start(tile[a:z], view[a:z]).then_inc(sem, 16)

    def gather(gp, dst, table, index, limit, sem):
        gp.indirect_dma_start(dst, None, table, bass.IndirectOffsetOnAxis(index, 0), bounds_check=limit,
                              oob_is_err=False).then_inc(sem, 16)

    top = ExitStack()
    with top:
        def sb(name, shape, dt=f32, ctx=top):
            return ctx.enter_context(nc.sbuf_tensor(name, shape, dt))

        def sem(name, ctx):
            one = nc.alloc_semaphore(name)
            sems_of_phase.append(one)
            return one

        sems_of_phase = []

        @contextmanager
        def phase():
            with ExitStack() as ctx:
                yield ctx
            nc.clear_and_free_semaphores(sems_of_phase)
            nc.all_engine_barrier()
            sems_of_phase.clear()

        ident = sb("ident", [128, 128])
        w_feat = sb("w_feat", [128, H, GW])
        w1 = sb("w1", [128, D])
        w2g = sb("w2g", [128, D])
        wm1 = sb("wm1", [128, 2, D])
        wm2 = sb("wm2", [128, D])
        wu1 = sb("wu1", [128, 2, D])
        wu2 = sb("wu2", [128, D])
        w31 = sb("w31", [128, 2 * D])
        w32 = sb("w32", [128, 2, D])
        b1_col = sb("b1_col", [128, 1])
        bm1_col = sb("bm1_col", [128, 1])
        bu1_col = sb("bu1_col", [128, 1])
        b31_col = sb("b31_col", [128, 2])
        b1_bc = sb("b1_bc", [128, D])
        out1_bc = sb("out1_bc", [128, D])
        bias_parts = sb("bias_parts", [3, 4, TG * D], bf16)
        BIAS_OUT1, BIAS_M2, BIAS_U2, BIAS_32 = range(4)
        ones3 = sb("ones3", [3, 128], bf16)
        neghalf = sb("neghalf", [128, TG])

        nowhere = sb("nowhere", [128, 1], i32)

        idx = sb("idx", [128, 6, NT], i32)
        SRC, DST, LAST, SLOT, SRC_SLOT, DST_SLOT = range(6)
        dst_f = sb("dst_f", [128, NT])
        carry_f = sb("carry_f", [128, NT])
        islast = sb("islast", [128, NT])
        dinv = sb("dinv", [128, NT])
        dinv_last = sb("dinv_last", [128, NT])
        dst_bc = sb("dst_bc", [128, E])
        same_bc = sb("same_bc", [128, E], bf16)

        psum = top.enter_context(nc.psum_tensor("psum", [128, 8, 512], f32))

        with phase() as ctx:
            def tmp(name, shape, dt=f32):
                return sb(name, shape, dt, ctx)

            s_w = sem("s_weights_loaded", ctx)
            s_c = sem("s_ctx_loaded", ctx)
            s_e = sem("s_edges_loaded", ctx)
            s_b = sem("s_dst_broadcast_loaded", ctx)
            s_id = sem("s_identity", ctx)
            s_v = sem("s_vector_step", ctx)
            s_mm = sem("s_gate_products", ctx)
            s_sig = sem("s_gate_sigmoid", ctx)
            s_map = sem("s_map_blank", ctx)
            s_mst = sem("s_map_stored", ctx)
            s_slot = sem("s_slot_numbers", ctx)
            s_bc = sem("s_broadcast_converted", ctx)

            wsc = tmp("wsc", [128, 2, H, F])
            wtmp = tmp("wtmp", [128, 2, D])
            w2_raw = tmp("w2_raw", [128, D])
            ctx_col = tmp("ctx_col", [64, 1])
            ctx_rep = tmp("ctx_rep", [64, 128])
            wg = tmp("wg", [64, D])
            wb = tmp("wb", [64, D])
            bg_bc = tmp("bg_bc", [128, D])
            b2_bc = tmp("b2_bc", [128, D])
            gate = tmp("gate", [128, D])
            bias3 = tmp("bias3", [3, 4, D])
            part = tmp("part", [3, 3, 4, D], bf16)
            part_mask = tmp("part_mask", [3, 3])
            next_i = tmp("next_i", [128, NT], i32)
            next_f = tmp("next_f", [128, NT])
            last_f = tmp("last_f", [128, NT])
            blank = tmp("blank", [128, N // P], i32)
            CH = E // 5
            stage = tmp("stage", [128, CH], i32)
            prev_bc = tmp("prev_bc", [128, NT])

            pg, pb = psum[:, 0, 0:D], psum[:, 1, 0:D]
            W = T["L0_gnn_W"]
            blk = ctx.enter_context(nc.Block())

            n_w = [0]

            @blk.sync
            def _(sp):
                def load(dst, src):
                    n_w[0] += 16
                    sp.dma_start(dst, src).then_inc(s_w, 16)

                def edge(dst, src):
                    sp.dma_start(dst, src).then_inc(s_e, 16)

                def wide(t):
                    return t.rearrange("(a d) -> a d", a=1).broadcast_to((128, t.shape[0]))

                with nc.allow_non_contiguous_dma(reason="index columns and bias columns, once"):
                    edge(idx[0:P, SRC, :], src_in.rearrange("(t p) -> p t", p=P))
                    edge(idx[0:P, DST, :], dst_in.rearrange("(t p) -> p t", p=P))
                    edge(next_i[0:P - 1, :], dst_in.rearrange("(t p) -> p t", p=P)[1:P, :])
                    edge(next_i[P - 1:P, 0:NT - 1], dst_in.rearrange("(a t p) -> a t p", a=1, p=P)[:, 1:NT, 0])
                    load(ctx_col[:, :], T["L1_gnn_ctx"].rearrange("a c -> c a"))
                    for d, s in ((b1_col, "L1_gnn_b1"), (bm1_col, "L2_gnn_b_msg1"), (bu1_col, "L2_gnn_b_upd1")):
                        load(d[:, :], T[s].rearrange("(d a) -> d a", a=1))
                    load(b31_col[:, :], T["L3_gnn_b1"].rearrange("(a d) -> d a", d=D))
                for h in range(H):
                    load(w_feat[:, h, 0:D], W)
                for k, s in enumerate(("L0_gnn_source_scorer", "L0_gnn_target_scorer")):
                    load(wsc[:, k, :, :].rearrange("p h f -> p (h f)"),
                         T[s].rearrange("h a f -> a (h f)").broadcast_to((128, D)))
                load(wg[:, :], T["L1_gnn_Wg"])
                load(wb[:, :], T["L1_gnn_Wb"])
                load(w1[:, :], T["L1_gnn_W1"])
                load(w2_raw[:, :], T["L1_gnn_W2"])
                for c in range(2):
                    load(wm1[:, c, :], T["L2_gnn_W_msg1"][c * D:(c + 1) * D, :])
                    load(wu1[:, c, :], T["L2_gnn_W_upd1"][c * D:(c + 1) * D, :])
                    load(w32[:, c, :], T["L3_gnn_W2"][c * D:(c + 1) * D, :])
                load(wm2[:, :], T["L2_gnn_W_msg2"])
                load(wu2[:, :], T["L2_gnn_W_upd2"])
                load(w31[:, :], T["L3_gnn_W1"])
                load(b1_bc[:, :], wide(T["L1_gnn_b1"]))
                load(b2_bc[:, :], wide(T["L1_gnn_b2"]))
                load(bg_bc[:, :], wide(T["L1_gnn_bg"]))
                for k, s in ((BIAS_M2, "L2_gnn_b_msg2"), (BIAS_U2, "L2_gnn_b_upd2"), (BIAS_32, "L3_gnn_b2")):
                    load(bias3[:, k, :], T[s].rearrange("(a d) -> a d", a=1).broadcast_to((3, D)))
                for c in range(5):
                    if c:
                        sp.wait_ge(s_bc, c)
                    sp.dma_start(stage[:, :], wide(dst_in[c * CH:(c + 1) * CH])).then_inc(s_b, 16)
                sp.wait_ge(s_map, 1)
                sp.dma_start(slot_of.rearrange("(p c) a -> p (c a)", p=P), blank[0:P, :]).then_inc(s_mst, 16)
                sp.wait_ge(s_mst, 16)

            @blk.gpsimd
            def _(gp):
                gp.memset(ident[:, :], 0.0).then_inc(s_id, 1)
                gp.memset(neghalf[:, :], -0.5).then_inc(s_id, 1)
                gp.memset(ones3[:, :], 1.0).then_inc(s_id, 1)
                gp.memset(part_mask[:, :], 0.0).then_inc(s_id, 1)
                gp.wait_ge(s_id, 4)
                gp.affine_select(out=ident[:, :], in_=ident[:, :], compare_op=ALU.not_equal, fill=1.0, base=0,
                                 pattern=[[-1, 128]], channel_multiplier=1).then_inc(s_id, 1)
                gp.affine_select(out=part_mask[:, :], in_=part_mask[:, :], compare_op=ALU.not_equal, fill=1.0,
                                 base=0, pattern=[[-1, 3]], channel_multiplier=1).then_inc(s_id, 1)
                gp.memset(nowhere[:, :], NOWHERE)
                gp.memset(blank[:, :], NOWHERE).then_inc(s_map, 1)
                gp.iota(idx[0:P, SLOT, :], pattern=[[P, NT]], base=0, channel_multiplier=1).then_inc(s_slot, 1)
                gp.wait_ge(s_v, 3 * H + 3)
                gp.affine_select(out=carry_f[0:P, :], in_=carry_f[0:P, :], compare_op=ALU.is_ge, fill=-1.0,
                                 base=-(P - 1), pattern=[[0, NT]], channel_multiplier=1).then_inc(s_slot, 1)
                gp.wait_ge(s_slot, 2)

            @blk.vector
            def _(v):
                steps = [0]

                def step(ins):
                    steps[0] += 1
                    ins.then_inc(s_v, 1)
                    v.wait_ge(s_v, steps[0])

                v.wait_ge(s_w, n_w[0])
                for h in range(H):
                    for k in range(2):
                        step(v.tensor_tensor(wtmp[:, k, :].rearrange("p (g f) -> p g f", f=F),
                                             w_feat[:, h, 0:D].rearrange("p (g f) -> p g f", f=F),
                                             wsc[:, k, h, :].unsqueeze(1).broadcast_to((128, GPN, F)), ALU.mult))
                    step(v.tensor_reduce(w_feat[:, h, D:GW], wtmp[:, :, :].rearrange("p k (g f) -> p (k g) f", f=F),
                                         AX.X, ALU.add))
                v.wait_ge(s_e, 64)
                step(v.tensor_copy(dst_f[0:P, :], idx[0:P, DST, :]))
                step(v.memset(carry_f[0:P, :], -1.0))
                step(v.tensor_copy(carry_f[0:P, 1:NT], dst_f[0:P, 0:NT - 1]))
                step(v.memset(next_f[0:P, :], -1.0))
                step(v.tensor_copy(next_f[0:P - 1, :], next_i[0:P - 1, :]))
                step(v.tensor_copy(next_f[96:P, 0:NT - 1], next_i[96:P, 0:NT - 1]))
                step(v.tensor_tensor(islast[0:P, :], dst_f[0:P, :], next_f[0:P, :], ALU.not_equal))
                step(v.tensor_scalar(last_f[0:P, :], islast[0:P, :], -float(NOWHERE), float(NOWHERE), ALU.mult, ALU.add))
                step(v.tensor_tensor(idx[0:P, LAST, :], last_f[0:P, :], dst_f[0:P, :], ALU.add))
                step(v.tensor_copy(ctx_rep[:, :], ctx_col[:, :].broadcast_to((64, 128))))
                v.wait_ge(s_mm, 1)
                step(v.tensor_tensor(bg_bc[:, :], pg, bg_bc[:, :], ALU.add))
                v.wait_ge(s_sig, 1)
                step(v.tensor_tensor(w2g[:, :], w2_raw[:, :], gate[:, :], ALU.mult))
                step(v.tensor_tensor(b2_bc[:, :], b2_bc[:, :], gate[:, :], ALU.mult))
                step(v.tensor_tensor(out1_bc[:, :], pb, b2_bc[:, :], ALU.add))
                step(v.tensor_copy(bias3[:, BIAS_OUT1, :], out1_bc[0:3, :]))
                v.wait_ge(s_id, 6)
                for k in range(3):
                    step(v.tensor_copy(part[:, k, :, :], bias3[:, :, :]))
                    if k < 2:
                        step(v.tensor_tensor(bias3[:, :, :], bias3[:, :, :], part[:, k, :, :], ALU.subtract))
                step(v.tensor_scalar(part[:, 0, :, :], part[:, 0, :, :], part_mask[:, 0:1], None, ALU.mult))
                step(v.scalar_tensor_tensor(part[:, 1, :, :], part[:, 1, :, :], part_mask[:, 1:2],
                                            part[:, 0, :, :], ALU.mult, ALU.add))
                for r in range(TG):
                    step(v.scalar_tensor_tensor(bias_parts[:, :, r * D:(r + 1) * D], part[:, 2, :, :],
                                                part_mask[:, 2:3], part[:, 1, :, :], ALU.mult, ALU.add))
                for c in range(5):
                    v.wait_ge(s_b, 16 * (c + 1))
                    v.tensor_copy(dst_bc[:, c * CH:(c + 1) * CH], stage[:, :]).then_inc(s_bc, 1)
                v.wait_ge(s_bc, 5)
                step(v.memset(prev_bc[:, 0:1], -1.0))
                step(v.tensor_copy(prev_bc[:, 1:NT], dst_bc[:, :].rearrange("p (t q) -> p t q", q=P)[:, 0:NT - 1, P - 1]))
                step(v.tensor_tensor(same_bc[:, :].rearrange("p (t q) -> p t q", q=P),
                                     dst_bc[:, :].rearrange("p (t q) -> p t q", q=P),
                                     prev_bc[:, :].unsqueeze(2).broadcast_to((128, NT, P)), ALU.is_equal))

            @blk.tensor
            def _(pe):
                pe.wait_ge(s_v, 3 * H + 10)
                pe.matmul(pg, ctx_rep[:, :], wg[:, :], start=True, stop=True)
                pe.matmul(pb, ctx_rep[:, :], wb[:, :], start=True, stop=True).then_inc(s_mm, 1)

            @blk.scalar
            def _(act):
                act.wait_ge(s_v, 3 * H + 11)
                act.activation(gate[:, :], bg_bc[:, :], ACT.Sigmoid).then_inc(s_sig, 1)

        C = 4

        def counters(ctx, prefix, names):
            names = (names + " hold").split()
            return namedtuple("Counters", names)(*[sem(f"{prefix}_{n}", ctx) for n in names])

        def dma_counters(ctx, name, n):
            return [sem(f"{name}{b}", ctx) for b in range(n)]

        def start(eng, s, *dma):
            for one in s:
                eng.sem_inc(one, C)
            for many in dma:
                for one in many:
                    eng.sem_inc(one, DONE)

        def before(k):
            return DONE * k + DONE

        def landed(k):
            return DONE * k + 2 * DONE

        def count_one(gp, dst, table, sem):
            gather(gp, dst, table, nowhere[0:P, :], table.shape[0] - 1, sem)

        def ln_stats(v, x, ln, s, k):
            for t in range(TG):
                last = v.bn_stats(ln.st[0:P, t, :], x[0:P, t, :])
            last.then_inc(s.st, 1)
            v.wait_ge(s.st, k + 1 + C)
            v.sem_inc(s.hold, 1)
            for t in range(TG):
                last = v.bn_aggr(ln.mv[0:P, t, :], ln.st[0:P, t, :])
            last.then_inc(s.mv, 1)
            v.wait_ge(s.mv, k + 1 + C)
            v.tensor_scalar(ln.var[0:P, :], ln.mv[0:P, :, 1], EPS, None, ALU.add).then_inc(s.var, 1)

        def ln_power(gp, ln, s, k):
            gp.wait_ge(s.var, k + 1 + C)
            gp.sem_inc(s.order, 1)
            gp.tensor_tensor(ln.rstd[0:P, :], ln.var[0:P, :], neghalf[0:P, :], ALU.pow).then_inc(s.rstd, 1)

        def ln_apply(v, x, ln, scale, xn, done):
            for t in range(TG):
                last = v.tensor_scalar(xn[0:P, t, :], x[0:P, t, :], ln.mv[0:P, t, 0:1], scale[0:P, t:t + 1],
                                       ALU.subtract, ALU.mult)
            last.then_inc(done, 1)

        def ln_buffers(ctx, name, n):
            st = sb(f"{name}_st", [128, n, TG, 6], ctx=ctx)
            mv = sb(f"{name}_mv", [128, n, TG, 2], ctx=ctx)
            var = sb(f"{name}_var", [128, n, TG], ctx=ctx)
            rstd = sb(f"{name}_rstd", [128, n, TG], ctx=ctx)
            Norm = namedtuple("Norm", "st mv var rstd")
            return [Norm(st[:, b], mv[:, b], var[:, b], rstd[:, b]) for b in range(n)]

        def transposes(pe, ps, x):
            for t in range(TG):
                last = pe.transpose(ps[:, t * P:(t + 1) * P], x[0:P, t, :], ident[0:P, 0:P])
            return last

        def rows_times(pe, ps, cols, w, start=True, stop=True):
            for t in range(TG):
                last = pe.matmul(ps[0:P, t * D:(t + 1) * D], cols[:, t * P:(t + 1) * P], w, start=start,
                                 stop=start or (stop and t == TG - 1))
            return last

        def bias_rows(pe, ps, which):
            pe.matmul(ps[0:P, :], ones3[:, 0:P], bias_parts[:, which, :], start=True, stop=False)

        def flat(x):
            return x.rearrange("p t d -> p (t d)")

        def bank(b):
            return psum[:, b, :]

        with phase() as ctx:
            L = 4
            NI = NJ // 2
            assert NI == NG
            xr = sb("f_x", [128, L, TG, D], ctx=ctx)
            ln = ln_buffers(ctx, "f", L)
            xn = sb("f_xn", [128, L, TG, D], ctx=ctx)
            hT = sb("f_hT", [128, L, GR], ctx=ctx)
            tab = sb("f_tab", [128, 2, GPN, GW], ctx=ctx)
            xs = sb("f_xs", [128, TG, D], ctx=ctx)
            cur = sb("f_cur", [128, 4, TG], i32, ctx=ctx)

            s = counters(ctx, "f", "st mv var rstd order xn tr hT mm feat score cur")
            d_x = dma_counters(ctx, "f_x_loaded", L)
            d_tab = dma_counters(ctx, "f_table_stored", 2)
            d_map, d_xs, d_xst = sem("f_map_written", ctx), sem("f_xsrc_gathered", ctx), sem("f_xsrc_stored", ctx)

            xv = x_in.rearrange("(h j) d -> j h d", h=H)
            tabv = feat_tab.rearrange("(j g) c -> j g c", g=GPN)
            xsv = slots(xsrc_d)
            blk = ctx.enter_context(nc.Block())

            @blk.sync
            def _(sp):
                with sp.Fori(0, NI) as i:
                    for b in range(L):
                        j, q = b // 2, b % 2
                        sp.wait_ge(s.xn, L * i + b + 1 - L + C)
                        move(sp, xr[:, b], xv[bass.ds((2 * i + j) * P, P), 4 * q:4 * q + 4, :], d_x[b])
                    sp.wait_ge(d_xs, 16 * TG * (i + 1))
                    move(sp, xs, xsv[i], d_xst, store=True)
                for b in range(2):
                    sp.wait_ge(d_tab[b], before(NI))
                sp.wait_ge(d_xst, before(NI))

            @blk.vector
            def _(v):
                start(v, s, d_x, d_tab, [d_xst])
                with v.Fori(0, NI) as i:
                    for b in range(L):
                        v.wait_ge(d_x[b], landed(i))
                        ln_stats(v, xr[:, b], ln[b], s, L * i + b)
                    for b in range(L):
                        v.wait_ge(s.rstd, L * i + b + 1 + C)
                        v.wait_ge(s.tr, L * i + b + 1 - L + C)
                        ln_apply(v, xr[:, b], ln[b], ln[b].rstd, xn[:, b], s.xn)

            @blk.tensor
            def _(pe):
                with pe.Fori(0, NI) as i:
                    for b in range(L + 1):
                        if b < L:
                            pe.wait_ge(s.xn, L * i + b + 1 + C)
                            pe.wait_ge(s.hT, L * i + b - 1 + C)
                            transposes(pe, bank(b % 2), xn[:, b]).then_inc(s.tr, 1)
                        if b >= 1:
                            n, q = L * i + b - 1, (b - 1) % 2
                            pe.wait_ge(s.hT, n + 1 + C)
                            pe.wait_ge(s.score, n - 1 + C)
                            for h in range(4):
                                last = pe.matmul(psum[0:P, 2 + 2 * q + h // 2, h % 2 * 256:h % 2 * 256 + GW],
                                                 hT[:, b - 1, h * P:(h + 1) * P], w_feat[:, 4 * q + h, :],
                                                 start=True, stop=True)
                            last.then_inc(s.mm, 1)

            @blk.scalar
            def _(act):
                with act.Fori(0, NI) as i:
                    for b in range(L + 1):
                        if b < L:
                            act.wait_ge(s.tr, L * i + b + 1 + C)
                            act.wait_ge(s.mm, L * i + b + 1 - L + C)
                            act.activation(hT[:, b, :], bank(b % 2)[:, 0:GR], ACT.Relu).then_inc(s.hT, 1)
                        if b >= 1:
                            n, j, q = L * i + b - 1, (b - 1) // 2, (b - 1) % 2
                            if q == 0:
                                act.wait_ge(d_tab[j], before(i))
                            act.wait_ge(s.mm, n + 1 + C)
                            ps = psum[0:P, 2 + 2 * q:4 + 2 * q, :].rearrange("p a (h c) -> p (a h) c", h=2)
                            act.activation(
                                tab[0:P, j, :, 0:D].rearrange("p g (h f) -> p h g f", f=F)[:, 4 * q:4 * q + 4],
                                ps[:, :, 0:D].rearrange("p h (g f) -> p h g f", f=F), ACT.Copy).then_inc(s.feat, 1)
                            act.activation(
                                tab[0:P, j, :, D:GW].rearrange("p g (k h) -> p h k g", h=H)[:, 4 * q:4 * q + 4],
                                ps[:, :, D:GW].rearrange("p h (k g) -> p h k g", k=2), ACT.Copy).then_inc(s.score, 1)
                            if q == 1:
                                act.wait_ge(s.feat, n + 1 + C)
                                act.wait_ge(s.score, n + 1 + C)
                                move(act, tab[:, j], tabv[bass.ds((2 * i + j) * P, P), :, :], d_tab[j], store=True)

            @blk.gpsimd
            def _(gp):
                count_one(gp, xs[0:P, 0, :], x_in, d_map)
                with gp.Fori(0, NI) as i:
                    gp.wait_ge(d_xst, before(i))
                    gp.sem_inc(s.order, 1)
                    gp.wait_ge(d_map, 16 * TG * i + 16)
                    gp.sem_inc(s.order, 1)
                    gp.tensor_copy(cur[0:P, :, :], idx[0:P, 0:4, bass.ds(TG * i, TG)]).then_inc(s.cur, 1)
                    gp.wait_ge(s.cur, i + 1 + C)
                    gp.sem_inc(s.order, 1)
                    for t in range(TG):
                        gather(gp, xs[0:P, t, :], x_in, cur[0:P, SRC, t:t + 1], N - 1, d_xs)
                        if t % 2 == 1:
                            ln_power(gp, ln[t // 2], s, L * i + t // 2)
                    for t in range(TG):
                        gp.indirect_dma_start(slot_of, bass.IndirectOffsetOnAxis(cur[0:P, LAST, t:t + 1], 0),
                                              cur[0:P, SLOT, t:t + 1], None, bounds_check=N - 1,
                                              oob_is_err=False).then_inc(d_map, 16)
                        if t % 2 == 1:
                            ln_power(gp, ln[2 + t // 2], s, L * i + 2 + t // 2)
                gp.wait_ge(d_map, 16 * TG * NG + 16)

        def row_chain(prefix, src, groups, dst=None, taps=None, map_reads=False):
            with phase() as ctx:
                L, K = 4, 3
                KU = 3 if taps else 4
                res = sb(prefix + "_res", [128, L, TG, D], ctx=ctx)
                ln = ln_buffers(ctx, prefix, L)
                xn = sb(prefix + "_xn", [128, L, TG, D], ctx=ctx)
                hT = sb(prefix + "_hT", [128, L, GR], ctx=ctx)
                uT = sb(prefix + "_uT", [128, L, 2, GR], ctx=ctx)
                hid = sb(prefix + "_hid", [128, L, TG, D], ctx=ctx) if taps else None
                if map_reads:
                    cur = sb(prefix + "_cur", [128, L, 2, TG], i32, ctx=ctx)
                    got = sb(prefix + "_got", [128, L, 2, TG], i32, ctx=ctx)
                    d_got = dma_counters(ctx, prefix + "_slots_read", L)
                s = counters(ctx, prefix, "st mv var rstd order xn tr hT u uT leaky rows res htr hid cur got")
                d_x = dma_counters(ctx, prefix + "_x_loaded", L)
                d_out = dma_counters(ctx, prefix + "_out_stored", L)
                d_xn = dma_counters(ctx, prefix + "_xn_stored", L)
                d_hid = dma_counters(ctx, prefix + "_hid_stored", L)
                NI, REST = groups // L, groups % L
                LAYERS = 2 if taps else 3
                KU = 2 if taps else 4
                blk = ctx.enter_context(nc.Block())

                def q_of(i, k, b, nb):
                    return K * L * i + nb * k + b

                def u_of(i, k, b, nb, half):
                    return KU * L * i + nb * k + (b if k < 2 else 2 * b + half)

                def m_of(i, k, b, nb):
                    return LAYERS * L * i + nb * k + b

                def turns(eng, turn):
                    with eng.Fori(0, NI) as i:
                        turn(i, L)
                    if REST:
                        turn(NI, REST)

                def par(k, b, nb, half=0, u=False):
                    return (nb * k + (2 * b + half if u and k == 2 else b)) % 2

                @blk.sync
                def _(sp):
                    def turn(i, nb):
                        for b in range(nb):
                            if taps:
                                sp.wait_ge(s.xn, q_of(i, 0, 0, nb) + C)
                            else:
                                sp.wait_ge(d_out[b], before(i))
                            move(sp, res[:, b], src[L * i + b], d_x[b])
                        if taps:
                            for k in range(K):
                                for b in range(nb):
                                    sp.wait_ge(s.xn, q_of(i, k, b, nb) + 1 + C)
                                    move(sp, xn[:, b], taps[k][L * i + b], d_xn[b], store=True)
                                if k == 0:
                                    for b in range(nb):
                                        sp.wait_ge(s.hid, L * i + b + 1 + C)
                                        move(sp, hid[:, b], taps[3][L * i + b], d_hid[b], store=True)
                    turns(sp, turn)
                    for b in range(L):
                        t = NI + (1 if b < REST else 0)
                        if taps:
                            sp.wait_ge(d_xn[b], before(K * t))
                            sp.wait_ge(d_hid[b], before(t))
                        else:
                            sp.wait_ge(d_out[b], before(t))

                @blk.vector
                def _(v):
                    start(v, s, d_x, d_out, d_xn, d_hid)

                    def turn(i, nb):
                        for b in range(nb):
                            v.wait_ge(d_x[b], landed(i))
                            ln_stats(v, res[:, b], ln[b], s, q_of(i, 0, b, nb))
                        for k in range(K):
                            for b in range(nb):
                                v.wait_ge(s.rstd, q_of(i, k, b, nb) + 1 + C)
                                if taps:
                                    v.wait_ge(d_xn[b], before(K * i + k))
                                ln_apply(v, res[:, b], ln[b], ln[b].rstd, xn[:, b], s.xn)
                            if k >= LAYERS:
                                continue
                            for b in range(nb + 1):
                                if k == 0 and b < nb:
                                    v.wait_ge(s.uT, u_of(i, 0, b, nb, 0) + 1 + C)
                                    v.scalar_tensor_tensor(uT[:, b, 0, :], uT[:, b, 0, :], 0.2, uT[:, b, 0, :],
                                                           ALU.mult, ALU.max).then_inc(s.leaky, 1)
                                if b >= 1:
                                    c = b - 1
                                    v.wait_ge(s.rows, m_of(i, k, c, nb) + 1 + C)
                                    v.tensor_tensor(flat(res[0:P, c]), flat(res[0:P, c]), bank(4 + par(k, c, nb))[0:P],
                                                    ALU.add).then_inc(s.res, 1)
                                    if k + 1 < K:
                                        v.wait_ge(s.res, m_of(i, k, c, nb) + 1 + C)
                                        ln_stats(v, res[:, c], ln[c], s, q_of(i, k + 1, c, nb))
                    turns(v, turn)

                @blk.tensor
                def _(pe):
                    W_COL = ((w1[:, :],), (wu1[:, 0, :],), (w31[:, 0:D], w31[:, D:2 * D]))
                    W_ROW = ((w2g[:, :],), (wu2[:, :],), (w32[:, 0, :], w32[:, 1, :]))
                    BIAS = (BIAS_OUT1, BIAS_U2, BIAS_32)

                    def turn(i, nb):
                        for k in range(LAYERS):
                            for b in range(nb + 2 + (1 if taps and k == 0 else 0)):
                                if b < nb:
                                    q = q_of(i, k, b, nb)
                                    tr = m_of(i, k, b, nb)
                                    pe.wait_ge(s.xn, q + 1 + C)
                                    pe.wait_ge(s.hT, tr - 1 + C)
                                    transposes(pe, bank(par(k, b, nb)), xn[:, b]).then_inc(s.tr, 1)
                                if 1 <= b <= nb:
                                    c = b - 1
                                    pe.wait_ge(s.hT, m_of(i, k, c, nb) + 1 + C)
                                    for half, w in enumerate(W_COL[k]):
                                        pe.wait_ge(s.uT, u_of(i, k, c, nb, half) - 1 + C)
                                        pe.matmul(bank(2 + par(k, c, nb, half, True))[:, 0:GR], w, hT[:, c, :],
                                                  start=True, stop=True).then_inc(s.u, 1)
                                if 2 <= b <= nb + 1:
                                    c = b - 2
                                    m = m_of(i, k, c, nb)
                                    pe.wait_ge(s.uT, u_of(i, k, c, nb, len(W_COL[k]) - 1) + 1 + C)
                                    if k == 0:
                                        pe.wait_ge(s.leaky, L * i + c + 1 + C)
                                    pe.wait_ge(s.res, m - 1 + C)
                                    ps = bank(4 + par(k, c, nb))
                                    bias_rows(pe, ps, BIAS[k])
                                    for half, w in enumerate(W_ROW[k]):
                                        last = rows_times(pe, ps, uT[:, c, half], w, start=False,
                                                          stop=half == len(W_ROW[k]) - 1)
                                    last.then_inc(s.rows, 1)
                                if taps and k == 0 and b >= 3:
                                    c = b - 3
                                    pe.wait_ge(s.hid, L * i + c - 1 + C)
                                    for t in range(TG):
                                        last = pe.transpose(bank(6 + c % 2)[0:P, t * D:(t + 1) * D],
                                                            uT[:, c, 0, t * P:(t + 1) * P], ident[:, :])
                                    last.then_inc(s.htr, 1)
                    turns(pe, turn)

                @blk.scalar
                def _(act):
                    FUNC = ((ACT.Identity, b1_col), (ACT.Silu, bu1_col), (ACT.Relu, b31_col))

                    def turn(i, nb):
                        for k in range(LAYERS):
                            for b in range(nb + 1 + (2 if taps and k == 0 else 0)):
                                if b < nb:
                                    act.wait_ge(s.tr, m_of(i, k, b, nb) + 1 + C)
                                    act.activation(hT[:, b, :], bank(par(k, b, nb))[:, 0:GR], ACT.Relu).then_inc(s.hT, 1)
                                if 1 <= b <= nb:
                                    c = b - 1
                                    f, bias = FUNC[k]
                                    for half in range(2 if k == 2 else 1):
                                        act.wait_ge(s.u, u_of(i, k, c, nb, half) + 1 + C)
                                        act.activation(uT[:, c, half, :], bank(2 + par(k, c, nb, half, True))[:, 0:GR],
                                                       f, bias=bias[:, half:half + 1]).then_inc(s.uT, 1)
                                if taps and k == 0 and b >= 3:
                                    c = b - 3
                                    act.wait_ge(s.htr, L * i + c + 1 + C)
                                    act.wait_ge(d_hid[c], before(i))
                                    act.activation(flat(hid[0:P, c]), bank(6 + c % 2)[0:P], ACT.Copy).then_inc(s.hid, 1)
                        if dst is not None:
                            for b in range(nb):
                                act.wait_ge(s.res, m_of(i, 2, b, nb) + 1 + C)
                                move(act, res[:, b], dst[L * i + b], d_out[b], store=True)
                    turns(act, turn)

                @blk.gpsimd
                def _(gp):
                    def turn(i, nb):
                        for k in range(K):
                            for b in range(nb):
                                ln_power(gp, ln[b], s, q_of(i, k, b, nb))
                                if not map_reads:
                                    continue
                                n = L * i + b
                                if k == 0:
                                    gp.tensor_copy(cur[0:P, b], idx[0:P, SRC:DST + 1, bass.ds(TG * n, TG)]).then_inc(s.cur, 1)
                                    gp.wait_ge(s.cur, n + 1 + C)
                                    gp.sem_inc(s.order, 1)
                                if k < 2:
                                    for t in range(TG):
                                        gather(gp, got[0:P, b, k, t:t + 1], slot_of, cur[0:P, b, k, t:t + 1], N - 1, d_got[b])
                                else:
                                    gp.wait_ge(d_got[b], 16 * 2 * TG * (i + 1))
                                    gp.sem_inc(s.order, 1)
                                    gp.tensor_copy(idx[0:P, SRC_SLOT:DST_SLOT + 1, bass.ds(TG * n, TG)],
                                                   got[0:P, b]).then_inc(s.got, 1)
                    turns(gp, turn)

        row_chain("e", slots(xsrc_d), NG, taps=[slots(xn0_src), slots(xn2_src), slots(xn3_src), slots(hid_src)],
                  map_reads=True)
        row_chain("n", rows(x_in), ND, dst=rows(out))

        SL = 2
        SI, SREST = NG // SL, NG % SL

        def slot_turns(eng, turn):
            with eng.Fori(0, SI) as i:
                turn(i, range(SL))
            turn(SI, range(SREST))

        def tiles(i, b):
            return bass.ds(TG * (SL * i + b), TG)

        def select(v, which, out, i, b):
            return v.tensor_tensor(out[0:P].rearrange("p (t q) -> p t q", q=P),
                                   dst_bc[0:P, bass.ds(GR * (SL * i + b), GR)].rearrange("p (t q) -> p t q", q=P),
                                   which[0:P, tiles(i, b)].unsqueeze(2).broadcast_to((P, TG, P)), ALU.is_equal)

        def run_sums(pe, ps, m, sel):
            for t in range(TG):
                last = pe.matmul(ps[:, t * P:(t + 1) * P], m[0:P, t, :], sel[0:P, t * P:(t + 1) * P],
                                 start=True, stop=True)
            return last

        def run_carry(v, ps, sums, s, i, b):
            for t in range(TG):
                n = SL * i + b
                before_it = sums[b][:, t * P - 1:t * P] if t else sums[1 - b][:, GR - 1:GR]
                v.wait_ge(s.sum, TG * n + t + 1 + C)
                v.scalar_tensor_tensor(sums[b][:, t * P:(t + 1) * P],
                                       same_bc[:, bass.ds(GR * n + t * P, P)], before_it,
                                       ps[:, t * P:(t + 1) * P], ALU.mult, ALU.add).then_inc(s.sum, 1)

        with phase() as ctx:
            fs = sb("a_fs", [128, SL, TG, GW], ctx=ctx)
            fd = sb("a_fd", [128, SL, TG, GW], ctx=ctx)
            xd = sb("a_xd", [128, SL, TG, D], ctx=ctx)
            cur = sb("a_cur", [128, SL, 2, TG], i32, ctx=ctx)
            z = sb("a_z", [128, SL, TG, H], ctx=ctx)
            zn = sb("a_zn", [128, SL, TG, H], ctx=ctx)
            ez = sb("a_ez", [128, SL, TG, H], ctx=ctx)
            msg = sb("a_msg", [128, SL, TG, MW], ctx=ctx)
            sel = sb("a_sel", [128, SL, GR], ctx=ctx)
            selc = sb("a_selc", [128, SL, GR], ctx=ctx)
            tot = sb("a_tot", [128, SL, TG, MW], ctx=ctx)
            rw = sb("a_rw", [128, SL, TG, H], ctx=ctx)
            agg = sb("a_agg", [128, SL, TG, D], ctx=ctx)
            deg = sb("a_deg", [128, SL, TG], ctx=ctx)
            dv = sb("a_dv", [128, SL, TG], ctx=ctx)
            sc = sb("a_sc", [128, SL, TG], ctx=ctx)
            g1n = sb("a_g1n", [128, SL, TG, D], ctx=ctx)
            g1 = sb("a_g1", [128, SL, TG, D], ctx=ctx)
            ln = ln_buffers(ctx, "a", SL)
            s = counters(ctx, "a", "cur order z zn ez el w msg ones sel selc tot1 totc rw agg x1 deg dv dvs dvl st mv var rstd sc g1n g1")
            d_fs = dma_counters(ctx, "a_fs", SL)
            d_fd = dma_counters(ctx, "a_fd", SL)
            d_xd = dma_counters(ctx, "a_xd", SL)
            d_x1 = dma_counters(ctx, "a_x1_stored", SL)
            d_g1 = dma_counters(ctx, "a_g1_stored", SL)
            x1v, t1v = slots(x1_dst), slots(tab1)
            blk = ctx.enter_context(nc.Block())

            @blk.gpsimd
            def _(gp):
                def turn(i, lanes):
                    for b in lanes:
                        n = SL * i + b
                        gp.wait_ge(s.msg, n - 1 + C)
                        gp.sem_inc(s.order, 1)
                        gp.wait_ge(d_x1[b], before(i))
                        gp.sem_inc(s.order, 1)
                        gp.tensor_copy(cur[0:P, b], idx[0:P, SRC:DST + 1, tiles(i, b)]).then_inc(s.cur, 1)
                        gp.wait_ge(s.cur, n + 1 + C)
                        gp.sem_inc(s.order, 1)
                        for t in range(TG):
                            gather(gp, fs[0:P, b, t, :], feat_tab, cur[0:P, b, 0, t:t + 1], N - 1, d_fs[b])
                        for t in range(TG):
                            gather(gp, fd[0:P, b, t, :], feat_tab, cur[0:P, b, 1, t:t + 1], N - 1, d_fd[b])
                        for t in range(TG):
                            gather(gp, xd[0:P, b, t, :], x_in, cur[0:P, b, 1, t:t + 1], N - 1, d_xd[b])
                    for b in lanes:
                        gp.wait_ge(s.deg, SL * i + b + 1 + C)
                        gp.sem_inc(s.order, 1)
                        gp.tensor_tensor(dv[0:P, b], deg[0:P, b], neghalf[0:P, :], ALU.pow).then_inc(s.dv, 1)
                    for b in lanes:
                        ln_power(gp, ln[b], s, SL * i + b)
                slot_turns(gp, turn)

            @blk.vector
            def _(v):
                start(v, s)
                for one in (*d_x1, *d_g1):
                    v.sem_inc(one, DONE)
                v.memset(msg[:, :, :, D + H:MW], 1.0).then_inc(s.ones, 1)
                v.memset(tot[:, :, :, :], 0.0).then_inc(s.ones, 1)
                v.wait_ge(s.ones, 2 + C)

                def turn(i, lanes):
                    for b in lanes:
                        n = SL * i + b
                        v.wait_ge(s.tot1, TG * n - TG + C)
                        select(v, dst_f, sel[:, b], i, b).then_inc(s.sel, 1)
                        select(v, carry_f, selc[:, b], i, b).then_inc(s.selc, 1)
                    for b in lanes:
                        n = SL * i + b
                        v.wait_ge(d_fs[b], 16 * TG * (i + 1))
                        v.wait_ge(d_fd[b], 16 * TG * (i + 1))
                        v.tensor_tensor(z[0:P, b], fs[0:P, b, :, D:D + H], fd[0:P, b, :, D + H:GW], ALU.add).then_inc(s.z, 1)
                        v.wait_ge(s.z, n + 1 + C)
                        v.tensor_scalar(zn[0:P, b], z[0:P, b], 0.0, None, ALU.min).then_inc(s.zn, 1)
                    for b in lanes:
                        n = SL * i + b
                        v.wait_ge(s.ez, n + 1 + C)
                        v.tensor_scalar(ez[0:P, b], ez[0:P, b], 1.0, 0.2, ALU.subtract, ALU.mult).then_inc(s.el, 1)
                        v.wait_ge(s.el, 2 * n + 1 + C)
                        v.scalar_tensor_tensor(z[0:P, b], z[0:P, b], 0.0, ez[0:P, b], ALU.max, ALU.add).then_inc(s.el, 1)
                    for b in lanes:
                        n = SL * i + b
                        v.wait_ge(s.w, n + 1 + C)
                        v.tensor_tensor(msg[0:P, b, :, 0:D].rearrange("p t (h f) -> p t h f", f=F),
                                        fs[0:P, b, :, 0:D].rearrange("p t (h f) -> p t h f", f=F),
                                        msg[0:P, b, :, D:D + H].unsqueeze(3).broadcast_to((P, TG, H, F)), ALU.mult).then_inc(s.msg, 1)
                    for b in lanes:
                        n = SL * i + b
                        v.wait_ge(s.totc, TG * (n + 1) + C)
                        v.reciprocal(rw[0:P, b], tot[0:P, b, :, D:D + H]).then_inc(s.rw, 1)
                        v.tensor_scalar(deg[0:P, b], tot[0:P, b, :, D + H], 1.0, 1.0, ALU.add, ALU.max).then_inc(s.deg, 1)
                        v.wait_ge(s.rw, n + 1 + C)
                        v.tensor_tensor(agg[0:P, b].rearrange("p t (h f) -> p t h f", f=F),
                                        tot[0:P, b, :, 0:D].rearrange("p t (h f) -> p t h f", f=F),
                                        rw[0:P, b].unsqueeze(3).broadcast_to((P, TG, H, F)), ALU.mult).then_inc(s.agg, 1)
                        v.wait_ge(s.agg, n + 1 + C)
                        v.wait_ge(d_xd[b], 16 * TG * (i + 1))
                        v.tensor_tensor(flat(xd[0:P, b]), flat(xd[0:P, b]), flat(agg[0:P, b]), ALU.add).then_inc(s.x1, 1)
                        v.wait_ge(s.x1, n + 1 + C)
                        ln_stats(v, xd[:, b], ln[b], s, n)
                    for b in lanes:
                        n = SL * i + b
                        v.wait_ge(s.dv, n + 1 + C)
                        v.tensor_copy(dinv[0:P, tiles(i, b)], dv[0:P, b]).then_inc(s.dvs, 1)
                        v.tensor_tensor(deg[0:P, b], dv[0:P, b], islast[0:P, tiles(i, b)], ALU.mult).then_inc(s.dvl, 1)
                        v.wait_ge(s.dvl, n + 1 + C)
                        v.tensor_copy(dinv_last[0:P, tiles(i, b)], deg[0:P, b]).then_inc(s.dvs, 1)
                        v.wait_ge(s.rstd, n + 1 + C)
                        v.tensor_tensor(sc[0:P, b], ln[b].rstd[0:P], deg[0:P, b], ALU.mult).then_inc(s.sc, 1)
                        v.wait_ge(s.sc, n + 1 + C)
                        v.wait_ge(s.g1, n - 1 + C)
                        ln_apply(v, xd[:, b], ln[b], sc[:, b], g1n[:, b], s.g1n)
                slot_turns(v, turn)

            @blk.scalar
            def _(act):
                def turn(i, lanes):
                    for b in lanes:
                        act.wait_ge(s.zn, SL * i + b + 1 + C)
                        act.activation(ez[0:P, b], zn[0:P, b], ACT.Exp).then_inc(s.ez, 1)
                    for b in lanes:
                        n = SL * i + b
                        act.wait_ge(s.el, 2 * n + 2 + C)
                        act.wait_ge(s.tot1, TG * n - TG + C)
                        act.activation(msg[0:P, b, :, D:D + H], z[0:P, b], ACT.Exp).then_inc(s.w, 1)
                    for b in lanes:
                        n = SL * i + b
                        for t in range(TG):
                            act.wait_ge(s.tot1, TG * n + t + 1 + C)
                            act.activation(tot[0:P, b, t, :], bank(t % 2)[0:P, 0:MW], ACT.Copy).then_inc(s.totc, 1)
                    for b in lanes:
                        n = SL * i + b
                        act.wait_ge(s.g1n, n + 1 + C)
                        act.wait_ge(d_g1[b], before(i))
                        act.activation(flat(g1[0:P, b]), flat(g1n[0:P, b]), ACT.Relu).then_inc(s.g1, 1)
                slot_turns(act, turn)

            @blk.tensor
            def _(pe):
                def turn(i, lanes):
                    for b in lanes:
                        n = SL * i + b
                        pe.wait_ge(s.sel, n + 1 + C)
                        pe.wait_ge(s.selc, n + 1 + C)
                        pe.wait_ge(s.msg, n + 1 + C)
                        for t in range(TG):
                            ps = bank(t % 2)[0:P, 0:MW]
                            pe.wait_ge(s.totc, TG * n + t - 1 + C)
                            pe.matmul(ps, sel[0:P, b, t * P:(t + 1) * P], msg[0:P, b, t, :], start=True, stop=False)
                            pe.wait_ge(s.totc, TG * n + t + C)
                            prev = tot[0:P, b, t - 1, :] if t else tot[0:P, 1 - b, TG - 1, :]
                            pe.matmul(ps, selc[0:P, b, t * P:(t + 1) * P], prev, start=False, stop=True).then_inc(s.tot1, 1)
                slot_turns(pe, turn)

            @blk.sync
            def _(sp):
                def turn(i, lanes):
                    for b in lanes:
                        n = SL * i + b
                        sp.wait_ge(s.g1, n + 1 + C)
                        move(sp, xd[:, b], x1v[n], d_x1[b], store=True)
                        move(sp, g1[:, b], t1v[n], d_g1[b], store=True)
                slot_turns(sp, turn)
                for b in range(SL):
                    t = SI + (1 if b < SREST else 0)
                    sp.wait_ge(d_x1[b], before(t))
                    sp.wait_ge(d_g1[b], before(t))

        def convolution(prefix, first, nb_view, self_view, over_tab, x_view, out_views):
            with phase() as ctx:
                hs = sb(prefix + "_hs", [128, SL, TG, D], ctx=ctx)
                gd = sb(prefix + "_gd", [128, SL, TG, D], ctx=ctx)
                xd = sb(prefix + "_xd", [128, SL, TG, D], ctx=ctx)
                m = sb(prefix + "_m", [128, SL, TG, D], ctx=ctx)
                sel = sb(prefix + "_sel", [128, SL, GR], ctx=ctx)
                sums = sb(prefix + "_sums", [128, SL, GR], ctx=ctx)
                cur = sb(prefix + "_cur", [128, SL, TG], i32, ctx=ctx)
                u = sb(prefix + "_u", [128, SL, TG, D], ctx=ctx)
                o = sb(prefix + "_o", [128, SL, TG, D], ctx=ctx)
                dl = sb(prefix + "_dl", [128, SL, TG], ctx=ctx)
                ln = ln_buffers(ctx, prefix, SL)
                s = counters(ctx, prefix, "cur order sel m ps sum rows u dl leaky o st mv var rstd x")
                d_hs = dma_counters(ctx, prefix + "_hs", SL)
                d_gd = dma_counters(ctx, prefix + "_gd", SL)
                d_xd = dma_counters(ctx, prefix + "_xd", SL)
                d_ov = dma_counters(ctx, prefix + "_ov", SL)
                d_o = dma_counters(ctx, prefix + "_o", SL)
                d_u = dma_counters(ctx, prefix + "_u", SL)
                sums2 = [sums[:, b] for b in range(SL)]
                blk = ctx.enter_context(nc.Block())

                @blk.sync
                def _(sp):
                    def turn(i, lanes):
                        for b in lanes:
                            n = SL * i + b
                            sp.wait_ge(s.m, n - 1 + C)
                            move(sp, hs[:, b], nb_view[n], d_hs[b])
                            move(sp, gd[:, b], self_view[n], d_gd[b])
                            if not first:
                                sp.wait_ge(s.u, n - 1 + C)
                                move(sp, xd[:, b], x_view[n], d_xd[b])
                    slot_turns(sp, turn)

                @blk.gpsimd
                def _(gp):
                    def turn(i, lanes):
                        for b in lanes:
                            n = SL * i + b
                            gp.wait_ge(d_hs[b], landed(i))
                            gp.sem_inc(s.order, 1)
                            gp.tensor_copy(cur[0:P, b], idx[0:P, SRC_SLOT, tiles(i, b)]).then_inc(s.cur, 1)
                            gp.wait_ge(s.cur, n + 1 + C)
                            gp.sem_inc(s.order, 1)
                            for t in range(TG):
                                gather(gp, hs[0:P, b, t, :], over_tab, cur[0:P, b, t:t + 1], E - 1, d_ov[b])
                        if not first:
                            for b in lanes:
                                ln_power(gp, ln[b], s, SL * i + b)
                    slot_turns(gp, turn)

                @blk.vector
                def _(v):
                    start(v, s, d_hs, d_gd, d_xd, d_o, d_u)
                    v.memset(sums[:, :, :], 0.0).then_inc(s.sum, 1)
                    v.wait_ge(s.sum, 1 + C)
                    
                    def turn(i, lanes):
                        for b in lanes:
                            n = SL * i + b
                            v.wait_ge(s.ps, n - 1 + C)
                            select(v, dst_f, sel[:, b], i, b).then_inc(s.sel, 1)
                            v.wait_ge(d_hs[b], landed(i))
                            v.wait_ge(d_gd[b], landed(i))
                            v.wait_ge(d_ov[b], 16 * TG * (i + 1))
                            v.scalar_tensor_tensor(flat(m[0:P, b]), flat(hs[0:P, b]), 0.0 if first else 1.0,
                                                   flat(gd[0:P, b]), ALU.max if first else ALU.mult,
                                                   ALU.add).then_inc(s.m, 1)
                        for b in lanes:
                            n = SL * i + b
                            v.wait_ge(s.ps, n + 1 + C)
                            run_carry(v, bank(b), sums2, s, i, b)
                        for b in lanes:
                            n = SL * i + b
                            v.wait_ge(s.rows, n + 1 + C)
                            if first:
                                v.wait_ge(s.o, n - 1 + C)
                                v.tensor_copy(dl[0:P, b], dinv_last[0:P, tiles(i, b)]).then_inc(s.dl, 1)
                            else:
                                v.wait_ge(d_xd[b], landed(i))
                                v.wait_ge(d_u[b], before(i))
                            for t in range(TG):
                                last = v.scalar_tensor_tensor(u[0:P, b, t, :], bank(4 + b)[0:P, t * D:(t + 1) * D],
                                                              dinv[0:P, bass.ds(TG * n + t, 1)],
                                                              b1_bc[0:P, :] if first else xd[0:P, b, t, :],
                                                              ALU.mult, ALU.add)
                            last.then_inc(s.u, 1)
                            if first:
                                v.wait_ge(s.u, n + 1 + C)
                                v.scalar_tensor_tensor(flat(u[0:P, b]), flat(u[0:P, b]), 0.2, flat(u[0:P, b]),
                                                       ALU.mult, ALU.max).then_inc(s.leaky, 1)
                            else:
                                v.wait_ge(s.u, n + 1 + C)
                                v.tensor_tensor(u[0:P, b], u[0:P, b], out1_bc[0:P, :].unsqueeze(1).broadcast_to((P, TG, D)),
                                                ALU.add).then_inc(s.x, 1)
                                v.wait_ge(s.x, n + 1 + C)
                                ln_stats(v, u[:, b], ln[b], s, n)
                        if not first:
                            for b in lanes:
                                v.wait_ge(s.rstd, SL * i + b + 1 + C)
                                v.wait_ge(d_o[b], before(i))
                                ln_apply(v, u[:, b], ln[b], ln[b].rstd, o[:, b], s.o)
                    slot_turns(v, turn)

                @blk.tensor
                def _(pe):
                    def turn(i, lanes):
                        for b in lanes:
                            n = SL * i + b
                            pe.wait_ge(s.sel, n + 1 + C)
                            pe.wait_ge(s.m, n + 1 + C)
                            pe.wait_ge(s.sum, TG * (n - 1) + 1 + C)
                            run_sums(pe, bank(b), m[:, b], sel[:, b]).then_inc(s.ps, 1)
                        for b in lanes:
                            n = SL * i + b
                            pe.wait_ge(s.sum, TG * (n + 1) + 1 + C)
                            pe.wait_ge(s.u, n - 1 + C)
                            rows_times(pe, bank(4 + b), sums2[b], w1[:, :] if first else w2g[:, :]).then_inc(s.rows, 1)
                    slot_turns(pe, turn)

                @blk.scalar
                def _(act):
                    def turn(i, lanes):
                        for b in lanes:
                            n = SL * i + b
                            if first:
                                act.wait_ge(s.leaky, n + 1 + C)
                                act.wait_ge(s.dl, n + 1 + C)
                                act.wait_ge(d_o[b], before(i))
                                for t in range(TG):
                                    last = act.activation(o[0:P, b, t, :], u[0:P, b, t, :], ACT.Copy,
                                                          scale=dl[0:P, b, t:t + 1])
                                last.then_inc(s.o, 1)
                            act.wait_ge(s.o, n + 1 + C)
                            move(act, o[:, b], out_views[0][n], d_o[b], store=True)
                            if not first:
                                move(act, u[:, b], out_views[1][n], d_u[b], store=True)
                    slot_turns(act, turn)
                    for b in range(SL):
                        t = SI + (1 if b < SREST else 0)
                        act.wait_ge(d_o[b], before(t))
                        if not first:
                            act.wait_ge(d_u[b], before(t))

        def message_layer():
            with phase() as ctx:
                hs = sb("m_hs", [128, SL, TG, D], ctx=ctx)
                hd = sb("m_hd", [128, SL, TG, D], ctx=ctx)
                xd = sb("m_xd", [128, SL, TG, D], ctx=ctx)
                cur = sb("m_cur", [128, SL, 2, TG], i32, ctx=ctx)
                sT = sb("m_sT", [128, SL, GR], ctx=ctx)
                dT = sb("m_dT", [128, SL, GR], ctx=ctx)
                vT = sb("m_vT", [128, SL, GR], ctx=ctx)
                wT = sb("m_wT", [128, SL, GR], ctx=ctx)
                m = sb("m_m", [128, SL, TG, D], ctx=ctx)
                sel = sb("m_sel", [128, SL, GR], ctx=ctx)
                sums = sb("m_sums", [128, SL, GR], ctx=ctx)
                gn = sb("m_gn", [128, SL, TG, D], ctx=ctx)
                g = sb("m_g", [128, SL, TG, D], ctx=ctx)
                sc = sb("m_sc", [128, SL, TG], ctx=ctx)
                ln = ln_buffers(ctx, "m", SL)
                s = counters(ctx, "m", "cur order trs sT trd dT u v rows m sel ps sum u2 w rows2 x st mv var rstd sc gn g")
                d_hs = dma_counters(ctx, "m_hs", SL)
                d_xd = dma_counters(ctx, "m_xd", SL)
                d_ov = dma_counters(ctx, "m_ov", SL)
                d_hd = dma_counters(ctx, "m_hd", SL)
                d_x3 = dma_counters(ctx, "m_x3", SL)
                d_g = dma_counters(ctx, "m_g", SL)
                sums2 = [sums[:, b] for b in range(SL)]
                hsv, xdv, x3v, t4v = slots(xn2_src), slots(x2_dst), slots(x3_dst), slots(tab4)
                blk = ctx.enter_context(nc.Block())

                @blk.sync
                def _(sp):
                    def turn(i, lanes):
                        for b in lanes:
                            n = SL * i + b
                            sp.wait_ge(s.trs, n - 1 + C)
                            move(sp, hs[:, b], hsv[n], d_hs[b])
                            sp.wait_ge(d_x3[b], before(i))
                            move(sp, xd[:, b], xdv[n], d_xd[b])
                    slot_turns(sp, turn)

                @blk.gpsimd
                def _(gp):
                    def turn(i, lanes):
                        for b in lanes:
                            n = SL * i + b
                            gp.wait_ge(d_hs[b], landed(i))
                            gp.sem_inc(s.order, 1)
                            gp.wait_ge(s.trd, n - 1 + C)
                            gp.sem_inc(s.order, 1)
                            gp.tensor_copy(cur[0:P, b], idx[0:P, SRC_SLOT:DST_SLOT + 1, tiles(i, b)]).then_inc(s.cur, 1)
                            gp.wait_ge(s.cur, n + 1 + C)
                            gp.sem_inc(s.order, 1)
                            for t in range(TG):
                                gather(gp, hs[0:P, b, t, :], tab3, cur[0:P, b, 0, t:t + 1], E - 1, d_ov[b])
                            for t in range(TG):
                                gather(gp, hd[0:P, b, t, :], tab3, cur[0:P, b, 1, t:t + 1], E - 1, d_hd[b])
                        for b in lanes:
                            ln_power(gp, ln[b], s, SL * i + b)
                    slot_turns(gp, turn)

                @blk.vector
                def _(v):
                    start(v, s, d_hs, d_xd, d_x3, d_g)
                    v.memset(sums[:, :, :], 0.0).then_inc(s.sum, 1)
                    v.wait_ge(s.sum, 1 + C)

                    def turn(i, lanes):
                        for b in lanes:
                            v.wait_ge(s.ps, SL * i + b - 1 + C)
                            select(v, dst_f, sel[:, b], i, b).then_inc(s.sel, 1)
                        for b in lanes:
                            v.wait_ge(s.rows, SL * i + b + 1 + C)
                            v.tensor_copy(flat(m[0:P, b]), bank(4 + b)[0:P]).then_inc(s.m, 1)
                        for b in lanes:
                            v.wait_ge(s.ps, SL * i + b + 1 + C)
                            run_carry(v, bank(6 + b), sums2, s, i, b)
                        for b in lanes:
                            n = SL * i + b
                            v.wait_ge(s.rows2, n + 1 + C)
                            v.wait_ge(d_xd[b], landed(i))
                            v.tensor_tensor(flat(xd[0:P, b]), flat(xd[0:P, b]), bank(4 + b)[0:P], ALU.add).then_inc(s.x, 1)
                            v.wait_ge(s.x, n + 1 + C)
                            ln_stats(v, xd[:, b], ln[b], s, n)
                        for b in lanes:
                            n = SL * i + b
                            v.wait_ge(s.rstd, n + 1 + C)
                            v.tensor_tensor(sc[0:P, b], ln[b].rstd[0:P], islast[0:P, tiles(i, b)], ALU.mult).then_inc(s.sc, 1)
                            v.wait_ge(s.sc, n + 1 + C)
                            v.wait_ge(s.g, n - 1 + C)
                            ln_apply(v, xd[:, b], ln[b], sc[:, b], gn[:, b], s.gn)
                    slot_turns(v, turn)

                @blk.tensor
                def _(pe):
                    def turn(i, lanes):
                        for b in lanes:
                            n = SL * i + b
                            pe.wait_ge(d_hs[b], landed(i))
                            pe.wait_ge(d_ov[b], 16 * TG * (i + 1))
                            pe.wait_ge(s.sT, n - 1 + C)
                            transposes(pe, bank(b), hs[:, b]).then_inc(s.trs, 1)
                            pe.wait_ge(d_hd[b], 16 * TG * (i + 1))
                            pe.wait_ge(s.w, n - 1 + C)
                            transposes(pe, bank(2 + b), hd[:, b]).then_inc(s.trd, 1)
                        for b in lanes:
                            n = SL * i + b
                            pe.wait_ge(s.sT, n + 1 + C)
                            pe.matmul(bank(b)[:, 0:GR], wm1[:, 0, :], sT[:, b, :], start=True, stop=False)
                            pe.wait_ge(s.dT, n + 1 + C)
                            pe.matmul(bank(b)[:, 0:GR], wm1[:, 1, :], dT[:, b, :], start=False, stop=True).then_inc(s.u, 1)
                        for b in lanes:
                            n = SL * i + b
                            pe.wait_ge(s.v, n + 1 + C)
                            pe.wait_ge(s.x, n - 1 + C)
                            bias_rows(pe, bank(4 + b), BIAS_M2)
                            rows_times(pe, bank(4 + b), vT[:, b], wm2[:, :], start=False).then_inc(s.rows, 1)
                        for b in lanes:
                            n = SL * i + b
                            pe.wait_ge(s.sel, n + 1 + C)
                            pe.wait_ge(s.m, n + 1 + C)
                            pe.wait_ge(s.sum, TG * (n - 1) + 1 + C)
                            run_sums(pe, bank(6 + b), m[:, b], sel[:, b]).then_inc(s.ps, 1)
                        for b in lanes:
                            n = SL * i + b
                            pe.matmul(bank(2 + b)[:, 0:GR], wu1[:, 0, :], dT[:, b, :], start=True, stop=False)
                            pe.wait_ge(s.sum, TG * (n + 1) + 1 + C)
                            pe.matmul(bank(2 + b)[:, 0:GR], wu1[:, 1, :], sums[:, b, :], start=False, stop=True).then_inc(s.u2, 1)
                        for b in lanes:
                            n = SL * i + b
                            pe.wait_ge(s.w, n + 1 + C)
                            bias_rows(pe, bank(4 + b), BIAS_U2)
                            rows_times(pe, bank(4 + b), wT[:, b], wu2[:, :], start=False).then_inc(s.rows2, 1)
                    slot_turns(pe, turn)

                @blk.scalar
                def _(act):
                    def turn(i, lanes):
                        for b in lanes:
                            n = SL * i + b
                            act.wait_ge(s.trs, n + 1 + C)
                            act.activation(sT[:, b, :], bank(b)[:, 0:GR], ACT.Relu).then_inc(s.sT, 1)
                            act.wait_ge(s.trd, n + 1 + C)
                            act.activation(dT[:, b, :], bank(2 + b)[:, 0:GR], ACT.Relu).then_inc(s.dT, 1)
                        for b in lanes:
                            n = SL * i + b
                            act.wait_ge(s.u, n + 1 + C)
                            act.activation(vT[:, b, :], bank(b)[:, 0:GR], ACT.Silu, bias=bm1_col[:, 0:1]).then_inc(s.v, 1)
                        for b in lanes:
                            n = SL * i + b
                            act.wait_ge(s.u2, n + 1 + C)
                            act.activation(wT[:, b, :], bank(2 + b)[:, 0:GR], ACT.Silu, bias=bu1_col[:, 0:1]).then_inc(s.w, 1)
                        for b in lanes:
                            n = SL * i + b
                            act.wait_ge(s.gn, n + 1 + C)
                            act.wait_ge(d_g[b], before(i))
                            act.activation(flat(g[0:P, b]), flat(gn[0:P, b]), ACT.Relu).then_inc(s.g, 1)
                            act.wait_ge(s.g, n + 1 + C)
                            move(act, g[:, b], t4v[n], d_g[b], store=True)
                            move(act, xd[:, b], x3v[n], d_x3[b], store=True)
                    slot_turns(act, turn)
                    for b in range(SL):
                        t = SI + (1 if b < SREST else 0)
                        act.wait_ge(d_g[b], before(t))
                        act.wait_ge(d_x3[b], before(t))

        def isomorphism_layer():
            with phase() as ctx:
                hs = sb("g_hs", [128, SL, TG, D], ctx=ctx)
                gd = sb("g_gd", [128, SL, TG, D], ctx=ctx)
                xd = sb("g_xd", [128, SL, TG, D], ctx=ctx)
                cur = sb("g_cur", [128, SL, 2, TG], i32, ctx=ctx)
                m = sb("g_m", [128, SL, TG, D], ctx=ctx)
                sel = sb("g_sel", [128, SL, GR], ctx=ctx)
                sums = sb("g_sums", [128, SL, GR], ctx=ctx)
                hT = sb("g_hT", [128, SL, 2, GR], ctx=ctx)
                s = counters(ctx, "g", "cur order sel m ps sum u h rows x")
                d_hs = dma_counters(ctx, "g_hs", SL)
                d_gd = dma_counters(ctx, "g_gd", SL)
                d_xd = dma_counters(ctx, "g_xd", SL)
                d_ov = dma_counters(ctx, "g_ov", SL)
                d_out = dma_counters(ctx, "g_out", SL)
                sums2 = [sums[:, b] for b in range(SL)]
                hsv, xdv, gdv = slots(xn3_src), slots(x3_dst), slots(tab4)
                blk = ctx.enter_context(nc.Block())

                @blk.sync
                def _(sp):
                    def turn(i, lanes):
                        for b in lanes:
                            n = SL * i + b
                            sp.wait_ge(s.m, n - 1 + C)
                            move(sp, hs[:, b], hsv[n], d_hs[b])
                            move(sp, gd[:, b], gdv[n], d_gd[b])
                            sp.wait_ge(d_out[b], 16 * TG * i + 16)
                            move(sp, xd[:, b], xdv[n], d_xd[b])
                    slot_turns(sp, turn)

                @blk.gpsimd
                def _(gp):
                    def turn(i, lanes):
                        for b in lanes:
                            n = SL * i + b
                            gp.wait_ge(d_hs[b], landed(i))
                            gp.sem_inc(s.order, 1)
                            gp.wait_ge(d_out[b], 16 * TG * i + 16)
                            gp.sem_inc(s.order, 1)
                            gp.tensor_copy(cur[0:P, b, 0], idx[0:P, SRC_SLOT, tiles(i, b)]).then_inc(s.cur, 1)
                            gp.tensor_copy(cur[0:P, b, 1], idx[0:P, LAST, tiles(i, b)]).then_inc(s.cur, 1)
                            gp.wait_ge(s.cur, 2 * n + 2 + C)
                            gp.sem_inc(s.order, 1)
                            for t in range(TG):
                                gather(gp, hs[0:P, b, t, :], tab4, cur[0:P, b, 0, t:t + 1], E - 1, d_ov[b])
                        for b in lanes:
                            gp.wait_ge(s.x, SL * i + b + 1 + C)
                            gp.sem_inc(s.order, 1)
                            for t in range(TG):
                                gp.indirect_dma_start(out, bass.IndirectOffsetOnAxis(cur[0:P, b, 1, t:t + 1], 0),
                                                      xd[0:P, b, t, :], None, bounds_check=N - 1,
                                                      oob_is_err=False).then_inc(d_out[b], 16)
                    for b in range(SL):
                        count_one(gp, xd[0:P, b, 0, :], tab4, d_out[b])
                    slot_turns(gp, turn)
                    for b in range(SL):
                        gp.wait_ge(d_out[b], 16 * TG * (SI + (1 if b < SREST else 0)) + 16)

                @blk.vector
                def _(v):
                    start(v, s, d_hs, d_gd, d_xd)
                    v.memset(sums[:, :, :], 0.0).then_inc(s.sum, 1)
                    v.wait_ge(s.sum, 1 + C)

                    def turn(i, lanes):
                        for b in lanes:
                            n = SL * i + b
                            v.wait_ge(s.ps, n - 1 + C)
                            select(v, dst_f, sel[:, b], i, b).then_inc(s.sel, 1)
                            v.wait_ge(d_hs[b], landed(i))
                            v.wait_ge(d_gd[b], landed(i))
                            v.wait_ge(d_ov[b], 16 * TG * (i + 1))
                            v.scalar_tensor_tensor(flat(m[0:P, b]), flat(hs[0:P, b]), 0.0, flat(gd[0:P, b]),
                                                   ALU.max, ALU.add).then_inc(s.m, 1)
                        for b in lanes:
                            v.wait_ge(s.ps, SL * i + b + 1 + C)
                            run_carry(v, bank(b), sums2, s, i, b)
                        for b in lanes:
                            n = SL * i + b
                            v.wait_ge(s.rows, n + 1 + C)
                            v.wait_ge(d_xd[b], landed(i))
                            v.tensor_tensor(flat(xd[0:P, b]), flat(xd[0:P, b]), bank(4 + b)[0:P], ALU.add).then_inc(s.x, 1)
                    slot_turns(v, turn)

                @blk.tensor
                def _(pe):
                    def turn(i, lanes):
                        for b in lanes:
                            n = SL * i + b
                            pe.wait_ge(s.sel, n + 1 + C)
                            pe.wait_ge(s.m, n + 1 + C)
                            pe.wait_ge(s.sum, TG * (n - 1) + 1 + C)
                            run_sums(pe, bank(b), m[:, b], sel[:, b]).then_inc(s.ps, 1)
                        for b in lanes:
                            n = SL * i + b
                            pe.wait_ge(s.sum, TG * (n + 1) + 1 + C)
                            for half in range(2):
                                pe.wait_ge(s.h, 2 * n + half - 1 + C)
                                pe.matmul(bank(2 + half)[:, 0:GR], w31[:, half * D:(half + 1) * D], sums[:, b, :],
                                          start=True, stop=True).then_inc(s.u, 1)
                        for b in lanes:
                            n = SL * i + b
                            pe.wait_ge(s.x, n - 1 + C)
                            bias_rows(pe, bank(4 + b), BIAS_32)
                            for half in range(2):
                                pe.wait_ge(s.h, 2 * n + half + 1 + C)
                                last = rows_times(pe, bank(4 + b), hT[:, b, half], w32[:, half, :], start=False, stop=half == 1)
                            last.then_inc(s.rows, 1)
                    slot_turns(pe, turn)

                @blk.scalar
                def _(act):
                    def turn(i, lanes):
                        for b in lanes:
                            n = SL * i + b
                            act.wait_ge(s.rows, n - 1 + C)
                            for half in range(2):
                                act.wait_ge(s.u, 2 * n + half + 1 + C)
                                act.activation(hT[:, b, half, :], bank(2 + half)[:, 0:GR], ACT.Relu,
                                               bias=b31_col[:, half:half + 1]).then_inc(s.h, 1)
                    slot_turns(act, turn)

        convolution("c", True, slots(xn0_src), slots(tab1), tab1, None, [slots(tab2)])
        convolution("d", False, slots(hid_src), slots(tab2), tab2, slots(x1_dst), [slots(tab3), slots(x2_dst)])
        message_layer()
        isomorphism_layer()


_INS = ['x', 'src', 'dst', 'L0_gnn_W', 'L0_gnn_source_scorer', 'L0_gnn_target_scorer', 'L1_gnn_ctx', 'L1_gnn_W1',
        'L1_gnn_b1', 'L1_gnn_W2', 'L1_gnn_b2', 'L1_gnn_Wg', 'L1_gnn_bg', 'L1_gnn_Wb', 'L2_gnn_W_msg1',
        'L2_gnn_b_msg1', 'L2_gnn_W_msg2', 'L2_gnn_b_msg2', 'L2_gnn_W_upd1', 'L2_gnn_b_upd1', 'L2_gnn_W_upd2',
        'L2_gnn_b_upd2', 'L3_gnn_W1', 'L3_gnn_b1', 'L3_gnn_W2', 'L3_gnn_b2']


def kernel(**inputs):
    import numpy as _np
    import concourse.bacc as _bacc
    from concourse import mybir as _mybir
    from concourse.bass_utils import run_bass_kernel_spmd as _run

    nc = _bacc.Bacc("TRN2", target_bir_lowering=False, num_devices=1)
    arrays, tensors = {}, {}
    for name in _INS:
        a = _np.ascontiguousarray(inputs[name])
        arrays[f"in_{name}"] = a
        tensors[name] = nc.dram_tensor(f"in_{name}", a.shape, _mybir.dt.from_np(a.dtype), kind="ExternalInput").ap()
    shape = tuple(inputs["x"].shape)
    out = nc.dram_tensor("out_x", shape, _mybir.dt.float32, kind="ExternalOutput").ap()
    gnn_four_layers(nc, tensors, out)
    r = _run(nc, [arrays], core_ids=[0])
    return r.results[0]["out_x"]
```

```python
import concourse.bass as bass
from concourse import mybir
from contextlib import ExitStack, contextmanager
from collections import namedtuple


def gnn_four_layers(nc, T, out):
    f32, i32, bf16 = mybir.dt.float32, mybir.dt.int32, mybir.dt.bfloat16
    ALU = mybir.AluOpType
    ACT = mybir.ActivationFunctionType
    AX = mybir.AxisListType

    x_in, src_in, dst_in = T["x"], T["src"], T["dst"]
    N, D = x_in.shape
    E = src_in.shape[0]
    H, F = T["L0_gnn_source_scorer"].shape[0], T["L0_gnn_source_scorer"].shape[2]
    P = 125
    TG = 4
    GR = P * TG
    NT, NG = E // P, E // GR
    ND = N // GR
    J = N // H
    NJ = J // P
    GPN = D // F
    GW = D + 2 * H
    MW = D + H + 1
    NOWHERE = 1 << 17
    EPS = 1e-5
    assert E % GR == 0 and N % GR == 0 and J % P == 0 and GPN * F == D and H * F == D

    def dram(name, shape, dt=f32):
        return nc.dram_tensor(name, shape, dt, kind="Internal").ap()

    feat_tab = dram("feat_tab", (N, GW))
    slot_of = dram("slot_of", (N, 1), i32)
    xsrc_d = dram("xsrc_d", (E, D))
    xn0_src = dram("xn0_src", (E, D))
    hid_src = dram("hid_src", (E, D))
    xn2_src = dram("xn2_src", (E, D))
    xn3_src = dram("xn3_src", (E, D))
    tab1 = dram("tab1", (E, D))
    tab2 = dram("tab2", (E, D))
    tab3 = dram("tab3", (E, D))
    tab4 = dram("tab4", (E, D))
    x1_dst = dram("x1_dst", (E, D))
    x2_dst = dram("x2_dst", (E, D))
    x3_dst = dram("x3_dst", (E, D))

    def slots(t):
        return t.rearrange("(n t p) d -> n p t d", p=P, t=TG)

    def rows(t):
        return t.rearrange("(n p t) d -> n p t d", p=P, t=TG)

    CUTS = ((0, 112), (112, P))
    DONE = 16 * len(CUTS)

    def move(eng, tile, view, sem, store=False):
        for a, z in CUTS:
            if store:
                eng.dma_start(view[a:z], tile[a:z]).then_inc(sem, 16)
            else:
                eng.dma_start(tile[a:z], view[a:z]).then_inc(sem, 16)

    def gather(gp, dst, table, index, limit, sem):
        gp.indirect_dma_start(dst, None, table, bass.IndirectOffsetOnAxis(index, 0), bounds_check=limit,
                              oob_is_err=False).then_inc(sem, 16)

    top = ExitStack()
    with top:
        def sb(name, shape, dt=f32, ctx=top):
            return ctx.enter_context(nc.sbuf_tensor(name, shape, dt))

        def sem(name, ctx):
            one = nc.alloc_semaphore(name)
            sems_of_phase.append(one)
            return one

        sems_of_phase = []

        @contextmanager
        def phase():
            with ExitStack() as ctx:
                yield ctx
            nc.clear_and_free_semaphores(sems_of_phase)
            nc.all_engine_barrier()
            sems_of_phase.clear()

        ident = sb("ident", [128, 128])
        w_feat = sb("w_feat", [128, H, GW])
        w1 = sb("w1", [128, D])
        w2g = sb("w2g", [128, D])
        wm1 = sb("wm1", [128, 2, D])
        wm2 = sb("wm2", [128, D])
        wu1 = sb("wu1", [128, 2, D])
        wu2 = sb("wu2", [128, D])
        w31 = sb("w31", [128, 2 * D])
        w32 = sb("w32", [128, 2, D])
        b1_col = sb("b1_col", [128, 1])
        bm1_col = sb("bm1_col", [128, 1])
        bu1_col = sb("bu1_col", [128, 1])
        b31_col = sb("b31_col", [128, 2])
        b1_bc = sb("b1_bc", [128, D])
        out1_bc = sb("out1_bc", [128, D])
        bias_parts = sb("bias_parts", [3, 4, TG * D], bf16)
        BIAS_OUT1, BIAS_M2, BIAS_U2, BIAS_32 = range(4)
        ones3 = sb("ones3", [3, 128], bf16)
        neghalf = sb("neghalf", [128, TG])

        nowhere = sb("nowhere", [128, 1], i32)

        idx = sb("idx", [128, 6, NT], i32)
        SRC, DST, LAST, SLOT, SRC_SLOT, DST_SLOT = range(6)
        dst_f = sb("dst_f", [128, NT])
        carry_f = sb("carry_f", [128, NT])
        islast = sb("islast", [128, NT])
        dinv = sb("dinv", [128, NT])
        dinv_last = sb("dinv_last", [128, NT])
        dst_bc = sb("dst_bc", [128, E])
        same_bc = sb("same_bc", [128, E], bf16)

        psum = top.enter_context(nc.psum_tensor("psum", [128, 8, 512], f32))

        with phase() as ctx:
            def tmp(name, shape, dt=f32):
                return sb(name, shape, dt, ctx)

            s_w = sem("s_weights_loaded", ctx)
            s_c = sem("s_ctx_loaded", ctx)
            s_e = sem("s_edges_loaded", ctx)
            s_b = sem("s_dst_broadcast_loaded", ctx)
            s_id = sem("s_identity", ctx)
            s_v = sem("s_vector_step", ctx)
            s_mm = sem("s_gate_products", ctx)
            s_sig = sem("s_gate_sigmoid", ctx)
            s_map = sem("s_map_blank", ctx)
            s_mst = sem("s_map_stored", ctx)
            s_slot = sem("s_slot_numbers", ctx)
            s_bc = sem("s_broadcast_converted", ctx)

            wsc = tmp("wsc", [128, 2, H, F])
            wtmp = tmp("wtmp", [128, 2, D])
            w2_raw = tmp("w2_raw", [128, D])
            ctx_col = tmp("ctx_col", [64, 1])
            ctx_rep = tmp("ctx_rep", [64, 128])
            wg = tmp("wg", [64, D])
            wb = tmp("wb", [64, D])
            bg_bc = tmp("bg_bc", [128, D])
            b2_bc = tmp("b2_bc", [128, D])
            gate = tmp("gate", [128, D])
            bias3 = tmp("bias3", [3, 4, D])
            part = tmp("part", [3, 3, 4, D], bf16)
            part_mask = tmp("part_mask", [3, 3])
            next_i = tmp("next_i", [128, NT], i32)
            next_f = tmp("next_f", [128, NT])
            last_f = tmp("last_f", [128, NT])
            blank = tmp("blank", [128, N // P], i32)
            CH = E // 5
            stage = tmp("stage", [128, CH], i32)
            prev_bc = tmp("prev_bc", [128, NT])

            pg, pb = psum[:, 0, 0:D], psum[:, 1, 0:D]
            W = T["L0_gnn_W"]
            blk = ctx.enter_context(nc.Block())

            n_w = [0]

            @blk.sync
            def _(sp):
                def load(dst, src):
                    n_w[0] += 16
                    sp.dma_start(dst, src).then_inc(s_w, 16)

                def edge(dst, src):
                    sp.dma_start(dst, src).then_inc(s_e, 16)

                def wide(t):
                    return t.rearrange("(a d) -> a d", a=1).broadcast_to((128, t.shape[0]))

                with nc.allow_non_contiguous_dma(reason="index columns and bias columns, once"):
                    edge(idx[0:P, SRC, :], src_in.rearrange("(t p) -> p t", p=P))
                    edge(idx[0:P, DST, :], dst_in.rearrange("(t p) -> p t", p=P))
                    edge(next_i[0:P - 1, :], dst_in.rearrange("(t p) -> p t", p=P)[1:P, :])
                    edge(next_i[P - 1:P, 0:NT - 1], dst_in.rearrange("(a t p) -> a t p", a=1, p=P)[:, 1:NT, 0])
                    load(ctx_col[:, :], T["L1_gnn_ctx"].rearrange("a c -> c a"))
                    for d, s in ((b1_col, "L1_gnn_b1"), (bm1_col, "L2_gnn_b_msg1"), (bu1_col, "L2_gnn_b_upd1")):
                        load(d[:, :], T[s].rearrange("(d a) -> d a", a=1))
                    load(b31_col[:, :], T["L3_gnn_b1"].rearrange("(a d) -> d a", d=D))
                for h in range(H):
                    load(w_feat[:, h, 0:D], W)
                for k, s in enumerate(("L0_gnn_source_scorer", "L0_gnn_target_scorer")):
                    load(wsc[:, k, :, :].rearrange("p h f -> p (h f)"),
                         T[s].rearrange("h a f -> a (h f)").broadcast_to((128, D)))
                load(wg[:, :], T["L1_gnn_Wg"])
                load(wb[:, :], T["L1_gnn_Wb"])
                load(w1[:, :], T["L1_gnn_W1"])
                load(w2_raw[:, :], T["L1_gnn_W2"])
                for c in range(2):
                    load(wm1[:, c, :], T["L2_gnn_W_msg1"][c * D:(c + 1) * D, :])
                    load(wu1[:, c, :], T["L2_gnn_W_upd1"][c * D:(c + 1) * D, :])
                    load(w32[:, c, :], T["L3_gnn_W2"][c * D:(c + 1) * D, :])
                load(wm2[:, :], T["L2_gnn_W_msg2"])
                load(wu2[:, :], T["L2_gnn_W_upd2"])
                load(w31[:, :], T["L3_gnn_W1"])
                load(b1_bc[:, :], wide(T["L1_gnn_b1"]))
                load(b2_bc[:, :], wide(T["L1_gnn_b2"]))
                load(bg_bc[:, :], wide(T["L1_gnn_bg"]))
                for k, s in ((BIAS_M2, "L2_gnn_b_msg2"), (BIAS_U2, "L2_gnn_b_upd2"), (BIAS_32, "L3_gnn_b2")):
                    load(bias3[:, k, :], T[s].rearrange("(a d) -> a d", a=1).broadcast_to((3, D)))
                for c in range(5):
                    if c:
                        sp.wait_ge(s_bc, c)
                    sp.dma_start(stage[:, :], wide(dst_in[c * CH:(c + 1) * CH])).then_inc(s_b, 16)
                sp.wait_ge(s_map, 1)
                sp.dma_start(slot_of.rearrange("(p c) a -> p (c a)", p=P), blank[0:P, :]).then_inc(s_mst, 16)
                sp.wait_ge(s_mst, 16)

            @blk.gpsimd
            def _(gp):
                gp.memset(ident[:, :], 0.0).then_inc(s_id, 1)
                gp.memset(neghalf[:, :], -0.5).then_inc(s_id, 1)
                gp.memset(ones3[:, :], 1.0).then_inc(s_id, 1)
                gp.memset(part_mask[:, :], 0.0).then_inc(s_id, 1)
                gp.wait_ge(s_id, 4)
                gp.affine_select(out=ident[:, :], in_=ident[:, :], compare_op=ALU.not_equal, fill=1.0, base=0,
                                 pattern=[[-1, 128]], channel_multiplier=1).then_inc(s_id, 1)
                gp.affine_select(out=part_mask[:, :], in_=part_mask[:, :], compare_op=ALU.not_equal, fill=1.0,
                                 base=0, pattern=[[-1, 3]], channel_multiplier=1).then_inc(s_id, 1)
                gp.memset(nowhere[:, :], NOWHERE)
                gp.memset(blank[:, :], NOWHERE).then_inc(s_map, 1)
                gp.iota(idx[0:P, SLOT, :], pattern=[[P, NT]], base=0, channel_multiplier=1).then_inc(s_slot, 1)
                gp.wait_ge(s_v, 3 * H + 3)
                gp.affine_select(out=carry_f[0:P, :], in_=carry_f[0:P, :], compare_op=ALU.is_ge, fill=-1.0,
                                 base=-(P - 1), pattern=[[0, NT]], channel_multiplier=1).then_inc(s_slot, 1)
                gp.wait_ge(s_slot, 2)

            @blk.vector
            def _(v):
                steps = [0]

                def step(ins):
                    steps[0] += 1
                    ins.then_inc(s_v, 1)
                    v.wait_ge(s_v, steps[0])

                v.wait_ge(s_w, n_w[0])
                for h in range(H):
                    for k in range(2):
                        step(v.tensor_tensor(wtmp[:, k, :].rearrange("p (g f) -> p g f", f=F),
                                             w_feat[:, h, 0:D].rearrange("p (g f) -> p g f", f=F),
                                             wsc[:, k, h, :].unsqueeze(1).broadcast_to((128, GPN, F)), ALU.mult))
                    step(v.tensor_reduce(w_feat[:, h, D:GW], wtmp[:, :, :].rearrange("p k (g f) -> p (k g) f", f=F),
                                         AX.X, ALU.add))
                v.wait_ge(s_e, 64)
                step(v.tensor_copy(dst_f[0:P, :], idx[0:P, DST, :]))
                step(v.memset(carry_f[0:P, :], -1.0))
                step(v.tensor_copy(carry_f[0:P, 1:NT], dst_f[0:P, 0:NT - 1]))
                step(v.memset(next_f[0:P, :], -1.0))
                step(v.tensor_copy(next_f[0:P - 1, :], next_i[0:P - 1, :]))
                step(v.tensor_copy(next_f[96:P, 0:NT - 1], next_i[96:P, 0:NT - 1]))
                step(v.tensor_tensor(islast[0:P, :], dst_f[0:P, :], next_f[0:P, :], ALU.not_equal))
                step(v.tensor_scalar(last_f[0:P, :], islast[0:P, :], -float(NOWHERE), float(NOWHERE), ALU.mult, ALU.add))
                step(v.tensor_tensor(idx[0:P, LAST, :], last_f[0:P, :], dst_f[0:P, :], ALU.add))
                step(v.tensor_copy(ctx_rep[:, :], ctx_col[:, :].broadcast_to((64, 128))))
                v.wait_ge(s_mm, 1)
                step(v.tensor_tensor(bg_bc[:, :], pg, bg_bc[:, :], ALU.add))
                v.wait_ge(s_sig, 1)
                step(v.tensor_tensor(w2g[:, :], w2_raw[:, :], gate[:, :], ALU.mult))
                step(v.tensor_tensor(b2_bc[:, :], b2_bc[:, :], gate[:, :], ALU.mult))
                step(v.tensor_tensor(out1_bc[:, :], pb, b2_bc[:, :], ALU.add))
                step(v.tensor_copy(bias3[:, BIAS_OUT1, :], out1_bc[0:3, :]))
                v.wait_ge(s_id, 6)
                for k in range(3):
                    step(v.tensor_copy(part[:, k, :, :], bias3[:, :, :]))
                    if k < 2:
                        step(v.tensor_tensor(bias3[:, :, :], bias3[:, :, :], part[:, k, :, :], ALU.subtract))
                step(v.tensor_scalar(part[:, 0, :, :], part[:, 0, :, :], part_mask[:, 0:1], None, ALU.mult))
                step(v.scalar_tensor_tensor(part[:, 1, :, :], part[:, 1, :, :], part_mask[:, 1:2],
                                            part[:, 0, :, :], ALU.mult, ALU.add))
                for r in range(TG):
                    step(v.scalar_tensor_tensor(bias_parts[:, :, r * D:(r + 1) * D], part[:, 2, :, :],
                                                part_mask[:, 2:3], part[:, 1, :, :], ALU.mult, ALU.add))
                for c in range(5):
                    v.wait_ge(s_b, 16 * (c + 1))
                    v.tensor_copy(dst_bc[:, c * CH:(c + 1) * CH], stage[:, :]).then_inc(s_bc, 1)
                v.wait_ge(s_bc, 5)
                step(v.memset(prev_bc[:, 0:1], -1.0))
                step(v.tensor_copy(prev_bc[:, 1:NT], dst_bc[:, :].rearrange("p (t q) -> p t q", q=P)[:, 0:NT - 1, P - 1]))
                step(v.tensor_tensor(same_bc[:, :].rearrange("p (t q) -> p t q", q=P),
                                     dst_bc[:, :].rearrange("p (t q) -> p t q", q=P),
                                     prev_bc[:, :].unsqueeze(2).broadcast_to((128, NT, P)), ALU.is_equal))

            @blk.tensor
            def _(pe):
                pe.wait_ge(s_v, 3 * H + 10)
                pe.matmul(pg, ctx_rep[:, :], wg[:, :], start=True, stop=True)
                pe.matmul(pb, ctx_rep[:, :], wb[:, :], start=True, stop=True).then_inc(s_mm, 1)

            @blk.scalar
            def _(act):
                act.wait_ge(s_v, 3 * H + 11)
                act.activation(gate[:, :], bg_bc[:, :], ACT.Sigmoid).then_inc(s_sig, 1)

        C = 20

        def counters(ctx, prefix, names):
            names = (names + " hold").split()
            return namedtuple("Counters", names)(*[sem(f"{prefix}_{n}", ctx) for n in names])

        def dma_counters(ctx, name, n):
            return [sem(f"{name}{b}", ctx) for b in range(n)]

        def start(eng, s, *dma):
            for one in s:
                eng.sem_inc(one, C)
            for many in dma:
                for one in many:
                    eng.sem_inc(one, DONE)

        def before(k):
            return DONE * k + DONE

        def landed(k):
            return DONE * k + 2 * DONE

        def count_one(gp, dst, table, sem):
            gather(gp, dst, table, nowhere[0:P, :], table.shape[0] - 1, sem)

        def ln_stats(v, x, ln, s, k):
            for t in range(TG):
                last = v.bn_stats(ln.st[0:P, t, :], x[0:P, t, :])
            last.then_inc(s.st, 1)
            v.wait_ge(s.st, k + 1 + C)
            v.sem_inc(s.hold, 1)
            for t in range(TG):
                last = v.bn_aggr(ln.mv[0:P, t, :], ln.st[0:P, t, :])
            last.then_inc(s.mv, 1)
            v.wait_ge(s.mv, k + 1 + C)
            v.tensor_scalar(ln.var[0:P, :], ln.mv[0:P, :, 1], EPS, None, ALU.add).then_inc(s.var, 1)

        def ln_power(gp, ln, s, k):
            gp.wait_ge(s.var, k + 1 + C)
            gp.sem_inc(s.order, 1)
            gp.tensor_tensor(ln.rstd[0:P, :], ln.var[0:P, :], neghalf[0:P, :], ALU.pow).then_inc(s.rstd, 1)

        def ln_apply(v, x, ln, scale, xn, done):
            for t in range(TG):
                last = v.tensor_scalar(xn[0:P, t, :], x[0:P, t, :], ln.mv[0:P, t, 0:1], scale[0:P, t:t + 1],
                                       ALU.subtract, ALU.mult)
            last.then_inc(done, 1)

        TV = TG // 2

        def ln_apply_first(v, x, ln, xn, done, shifted):
            v.scalar_tensor_tensor(ln.shift[0:P, TV:TG], ln.mv[0:P, TV:TG, 0], -1.0, ln.rstd[0:P, TV:TG],
                                   ALU.mult, ALU.mult).then_inc(shifted, 1)
            for t in range(TV):
                last = v.tensor_scalar(xn[0:P, t, :], x[0:P, t, :], ln.mv[0:P, t, 0:1], ln.rstd[0:P, t:t + 1],
                                       ALU.subtract, ALU.mult)
            last.then_inc(done, 1)

        def ln_apply_rest(act, x, ln, xn, done):
            for t in range(TV, TG):
                last = act.activation(xn[0:P, t, :], x[0:P, t, :], ACT.Identity, bias=ln.shift[0:P, t:t + 1],
                                      scale=ln.rstd[0:P, t:t + 1])
            last.then_inc(done, 1)

        def ln_buffers(ctx, name, n):
            st = sb(f"{name}_st", [128, n, TG, 6], ctx=ctx)
            mv = sb(f"{name}_mv", [128, n, TG, 2], ctx=ctx)
            var = sb(f"{name}_var", [128, n, TG], ctx=ctx)
            rstd = sb(f"{name}_rstd", [128, n, TG], ctx=ctx)
            shift = sb(f"{name}_shift", [128, n, TG], ctx=ctx)
            Norm = namedtuple("Norm", "st mv var rstd shift")
            return [Norm(st[:, b], mv[:, b], var[:, b], rstd[:, b], shift[:, b]) for b in range(n)]

        def transposes(pe, ps, x):
            for t in range(TG):
                last = pe.transpose(ps[:, t * P:(t + 1) * P], x[0:P, t, :], ident[0:P, 0:P])
            return last

        def rows_times(pe, ps, cols, w, start=True, stop=True):
            for t in range(TG):
                last = pe.matmul(ps[0:P, t * D:(t + 1) * D], cols[:, t * P:(t + 1) * P], w, start=start,
                                 stop=start or (stop and t == TG - 1))
            return last

        def bias_rows(pe, ps, which):
            pe.matmul(ps[0:P, :], ones3[:, 0:P], bias_parts[:, which, :], start=True, stop=False)

        def flat(x):
            return x.rearrange("p t d -> p (t d)")

        def bank(b):
            return psum[:, b, :]

        with phase() as ctx:
            L = 4
            NI = NJ // 2
            assert NI == NG
            xr = sb("f_x", [128, L, TG, D], ctx=ctx)
            ln = ln_buffers(ctx, "f", L)
            xn = sb("f_xn", [128, L, TG, D], ctx=ctx)
            hT = sb("f_hT", [128, L, GR], ctx=ctx)
            tab = sb("f_tab", [128, 2, GPN, GW], ctx=ctx)
            xs = sb("f_xs", [128, TG, D], ctx=ctx)
            cur = sb("f_cur", [128, 4, TG], i32, ctx=ctx)

            s = counters(ctx, "f", "st mv var rstd order xn tr hT mm feat score cur")
            d_x = dma_counters(ctx, "f_x_loaded", L)
            d_tab = dma_counters(ctx, "f_table_stored", 2)
            d_map, d_xs, d_xst = sem("f_map_written", ctx), sem("f_xsrc_gathered", ctx), sem("f_xsrc_stored", ctx)

            xv = x_in.rearrange("(h j) d -> j h d", h=H)
            tabv = feat_tab.rearrange("(j g) c -> j g c", g=GPN)
            xsv = slots(xsrc_d)
            blk = ctx.enter_context(nc.Block())

            @blk.sync
            def _(sp):
                with sp.Fori(0, NI) as i:
                    for b in range(L):
                        j, q = b // 2, b % 2
                        sp.wait_ge(s.xn, L * i + b + 1 - L + C)
                        move(sp, xr[:, b], xv[bass.ds((2 * i + j) * P, P), 4 * q:4 * q + 4, :], d_x[b])
                    sp.wait_ge(d_xs, 16 * TG * (i + 1))
                    move(sp, xs, xsv[i], d_xst, store=True)
                for b in range(2):
                    sp.wait_ge(d_tab[b], before(NI))
                sp.wait_ge(d_xst, before(NI))

            @blk.vector
            def _(v):
                start(v, s, d_x, d_tab, [d_xst])
                with v.Fori(0, NI) as i:
                    for b in range(L):
                        v.wait_ge(d_x[b], landed(i))
                        ln_stats(v, xr[:, b], ln[b], s, L * i + b)
                    for b in range(L):
                        v.wait_ge(s.rstd, L * i + b + 1 + C)
                        v.wait_ge(s.tr, L * i + b + 1 - L + C)
                        ln_apply(v, xr[:, b], ln[b], ln[b].rstd, xn[:, b], s.xn)

            @blk.tensor
            def _(pe):
                with pe.Fori(0, NI) as i:
                    for b in range(L + 1):
                        if b < L:
                            pe.wait_ge(s.xn, L * i + b + 1 + C)
                            pe.wait_ge(s.hT, L * i + b - 1 + C)
                            transposes(pe, bank(b % 2), xn[:, b]).then_inc(s.tr, 1)
                        if b >= 1:
                            n, q = L * i + b - 1, (b - 1) % 2
                            pe.wait_ge(s.hT, n + 1 + C)
                            pe.wait_ge(s.score, n - 1 + C)
                            for h in range(4):
                                last = pe.matmul(psum[0:P, 2 + 2 * q + h // 2, h % 2 * 256:h % 2 * 256 + GW],
                                                 hT[:, b - 1, h * P:(h + 1) * P], w_feat[:, 4 * q + h, :],
                                                 start=True, stop=True)
                            last.then_inc(s.mm, 1)

            @blk.scalar
            def _(act):
                with act.Fori(0, NI) as i:
                    for b in range(L + 1):
                        if b < L:
                            act.wait_ge(s.tr, L * i + b + 1 + C)
                            act.wait_ge(s.mm, L * i + b + 1 - L + C)
                            act.activation(hT[:, b, :], bank(b % 2)[:, 0:GR], ACT.Relu).then_inc(s.hT, 1)
                        if b >= 1:
                            n, j, q = L * i + b - 1, (b - 1) // 2, (b - 1) % 2
                            if q == 0:
                                act.wait_ge(d_tab[j], before(i))
                            act.wait_ge(s.mm, n + 1 + C)
                            ps = psum[0:P, 2 + 2 * q:4 + 2 * q, :].rearrange("p a (h c) -> p (a h) c", h=2)
                            act.activation(
                                tab[0:P, j, :, 0:D].rearrange("p g (h f) -> p h g f", f=F)[:, 4 * q:4 * q + 4],
                                ps[:, :, 0:D].rearrange("p h (g f) -> p h g f", f=F), ACT.Copy).then_inc(s.feat, 1)
                            act.activation(
                                tab[0:P, j, :, D:GW].rearrange("p g (k h) -> p h k g", h=H)[:, 4 * q:4 * q + 4],
                                ps[:, :, D:GW].rearrange("p h (k g) -> p h k g", k=2), ACT.Copy).then_inc(s.score, 1)
                            if q == 1:
                                act.wait_ge(s.feat, n + 1 + C)
                                act.wait_ge(s.score, n + 1 + C)
                                move(act, tab[:, j], tabv[bass.ds((2 * i + j) * P, P), :, :], d_tab[j], store=True)

            @blk.gpsimd
            def _(gp):
                count_one(gp, xs[0:P, 0, :], x_in, d_map)
                with gp.Fori(0, NI) as i:
                    gp.wait_ge(d_xst, before(i))
                    gp.sem_inc(s.order, 1)
                    gp.wait_ge(d_map, 16 * TG * i + 16)
                    gp.sem_inc(s.order, 1)
                    gp.tensor_copy(cur[0:P, :, :], idx[0:P, 0:4, bass.ds(TG * i, TG)]).then_inc(s.cur, 1)
                    gp.wait_ge(s.cur, i + 1 + C)
                    gp.sem_inc(s.order, 1)
                    for t in range(TG):
                        gather(gp, xs[0:P, t, :], x_in, cur[0:P, SRC, t:t + 1], N - 1, d_xs)
                        if t % 2 == 1:
                            ln_power(gp, ln[t // 2], s, L * i + t // 2)
                    for t in range(TG):
                        gp.indirect_dma_start(slot_of, bass.IndirectOffsetOnAxis(cur[0:P, LAST, t:t + 1], 0),
                                              cur[0:P, SLOT, t:t + 1], None, bounds_check=N - 1,
                                              oob_is_err=False).then_inc(d_map, 16)
                        if t % 2 == 1:
                            ln_power(gp, ln[2 + t // 2], s, L * i + 2 + t // 2)
                gp.wait_ge(d_map, 16 * TG * NG + 16)

        def row_chain(prefix, src, groups, L, dst=None, taps=None, map_reads=False):
            with phase() as ctx:
                K = 3
                LAYERS = 2 if taps else 3
                KU = 2 if taps else 4
                R = 5
                NI = groups // L
                TASKS, PRODUCTS = K * L, LAYERS * L
                assert groups % L == 0 and PRODUCTS % R == 0 and PRODUCTS % 2 == 0 and L >= 5
                res = sb(prefix + "_res", [128, L, TG, D], ctx=ctx)
                ln = ln_buffers(ctx, prefix, L)
                xn = sb(prefix + "_xn", [128, L, TG, D], ctx=ctx)
                hT = sb(prefix + "_hT", [128, 2, GR], ctx=ctx)
                uT = sb(prefix + "_uT", [128, R, 2, GR], ctx=ctx)
                hid = sb(prefix + "_hid", [128, L, TG, D], ctx=ctx) if taps else None
                if map_reads:
                    cur = sb(prefix + "_cur", [128, L, 2, TG], i32, ctx=ctx)
                    got = sb(prefix + "_got", [128, L, 2, TG], i32, ctx=ctx)
                    d_got = dma_counters(ctx, prefix + "_slots_read", L)
                s = counters(ctx, prefix, "st mv var rstd order shift xn xa tr hT u uT leaky rows res htr hid cur got")
                d_x = dma_counters(ctx, prefix + "_x_loaded", L)
                d_out = dma_counters(ctx, prefix + "_out_stored", L)
                d_xn = dma_counters(ctx, prefix + "_xn_stored", L)
                d_hid = dma_counters(ctx, prefix + "_hid_stored", L)
                blk = ctx.enter_context(nc.Block())

                def norm_of(i, t):
                    return TASKS * i + t

                def row_of(i, t):
                    return PRODUCTS * i + t

                def col_of(i, t, half=0):
                    return KU * L * i + (t if t < 2 * L else 2 * L + 2 * (t - 2 * L) + half)

                def col_bank(t, half=0):
                    return bank(2 + (t if t < 2 * L else half) % 2)

                def halves(t):
                    return 2 if t >= 2 * L else 1

                @blk.sync
                def _(sp):
                    with sp.Fori(0, NI) as i:
                        for b in range(L):
                            if taps:
                                sp.wait_ge(s.xn, norm_of(i, b - L) + 1 + C)
                                sp.wait_ge(s.xa, norm_of(i, b - L) + 1 + C)
                            else:
                                sp.wait_ge(d_out[b], before(i))
                            move(sp, res[:, b], src[L * i + b], d_x[b])
                        if taps:
                            for t in range(TASKS + 4):
                                if t < TASKS:
                                    sp.wait_ge(s.xn, norm_of(i, t) + 1 + C)
                                    sp.wait_ge(s.xa, norm_of(i, t) + 1 + C)
                                    move(sp, xn[:, t % L], taps[t // L][L * i + t % L], d_xn[t % L], store=True)
                                if 0 <= t - 4 < L:
                                    b = t - 4
                                    sp.wait_ge(s.hid, L * i + b + 1 + C)
                                    move(sp, hid[:, b], taps[3][L * i + b], d_hid[b], store=True)
                    for b in range(L):
                        if taps:
                            sp.wait_ge(d_xn[b], before(K * NI))
                            sp.wait_ge(d_hid[b], before(NI))
                        else:
                            sp.wait_ge(d_out[b], before(NI))

                @blk.vector
                def _(v):
                    start(v, s, d_x, d_out, d_xn, d_hid)
                    with v.Fori(0, NI) as i:
                        for t in range(-1, PRODUCTS + 3):
                            if 0 <= t - 2 < L:
                                r = t - 2
                                v.wait_ge(s.uT, col_of(i, r) + 1 + C)
                                v.scalar_tensor_tensor(uT[:, r % R, 0, :], uT[:, r % R, 0, :], 0.2, uT[:, r % R, 0, :],
                                                       ALU.mult, ALU.max).then_inc(s.leaky, 1)
                            for b in range(4 * t + 4, min(L, 4 * t + 8)):
                                v.wait_ge(d_x[b], landed(i))
                                ln_stats(v, res[:, b], ln[b], s, norm_of(i, b))
                            if t + 1 < TASKS:
                                q = t + 1
                                v.wait_ge(s.rstd, norm_of(i, q) + 1 + C)
                                if taps:
                                    v.wait_ge(d_xn[q % L], before(K * i + q // L))
                                ln_apply_first(v, res[:, q % L], ln[q % L], xn[:, q % L], s.xn, s.shift)
                            if t >= 3:
                                r, b = t - 3, (t - 3) % L
                                v.wait_ge(s.rows, row_of(i, r) + 1 + C)
                                v.tensor_tensor(flat(res[0:P, b]), flat(res[0:P, b]), bank(4 + r % 2)[0:P],
                                                ALU.add).then_inc(s.res, 1)
                                if r + L < TASKS:
                                    v.wait_ge(s.res, row_of(i, r) + 1 + C)
                                    ln_stats(v, res[:, b], ln[b], s, norm_of(i, r + L))
                        for q in range(PRODUCTS + 4, TASKS):
                            v.wait_ge(s.rstd, norm_of(i, q) + 1 + C)
                            v.wait_ge(d_xn[q % L], before(K * i + q // L))
                            ln_apply_first(v, res[:, q % L], ln[q % L], xn[:, q % L], s.xn, s.shift)

                @blk.gpsimd
                def _(gp):
                    with gp.Fori(0, NI) as i:
                        for t in range(TASKS):
                            b = t % L
                            n = L * i + b
                            ln_power(gp, ln[b], s, norm_of(i, t))
                            if not map_reads:
                                continue
                            if t < L:
                                gp.tensor_copy(cur[0:P, b], idx[0:P, SRC:DST + 1, bass.ds(TG * n, TG)]).then_inc(s.cur, 1)
                                gp.wait_ge(s.cur, n + 1 + C)
                                gp.sem_inc(s.order, 1)
                            if t < 2 * L:
                                k = t // L
                                for c in range(TG):
                                    gather(gp, got[0:P, b, k, c:c + 1], slot_of, cur[0:P, b, k, c:c + 1], N - 1, d_got[b])
                            else:
                                gp.wait_ge(d_got[b], 16 * 2 * TG * (i + 1))
                                gp.sem_inc(s.order, 1)
                                gp.tensor_copy(idx[0:P, SRC_SLOT:DST_SLOT + 1, bass.ds(TG * n, TG)],
                                               got[0:P, b]).then_inc(s.got, 1)

                @blk.tensor
                def _(pe):
                    W_COL = ((w1[:, :],), (wu1[:, 0, :],), (w31[:, 0:D], w31[:, D:2 * D]))
                    W_ROW = ((w2g[:, :],), (wu2[:, :],), (w32[:, 0, :], w32[:, 1, :]))
                    BIAS = (BIAS_OUT1, BIAS_U2, BIAS_32)
                    with pe.Fori(0, NI) as i:
                        for t in range(PRODUCTS + 2):
                            if 0 <= t - 1 < PRODUCTS:
                                c = t - 1
                                pe.wait_ge(s.hT, row_of(i, c) + 1 + C)
                                for half, w in enumerate(W_COL[c // L]):
                                    pe.wait_ge(s.uT, col_of(i, c, half) - 1 + C)
                                    pe.matmul(col_bank(c, half)[:, 0:GR], w, hT[:, c % 2, :],
                                              start=True, stop=True).then_inc(s.u, 1)
                            if t < PRODUCTS:
                                pe.wait_ge(s.xn, norm_of(i, t) + 1 + C)
                                pe.wait_ge(s.xa, norm_of(i, t) + 1 + C)
                                pe.wait_ge(s.hT, row_of(i, t) - 1 + C)
                                transposes(pe, bank(t % 2), xn[:, t % L]).then_inc(s.tr, 1)
                            if t >= 2:
                                r, k = t - 2, (t - 2) // L
                                pe.wait_ge(s.uT, col_of(i, r, halves(r) - 1) + 1 + C)
                                if k == 0:
                                    pe.wait_ge(s.leaky, L * i + r + 1 + C)
                                pe.wait_ge(s.res, row_of(i, r) - 1 + C)
                                ps = bank(4 + r % 2)
                                bias_rows(pe, ps, BIAS[k])
                                for half, w in enumerate(W_ROW[k]):
                                    last = rows_times(pe, ps, uT[:, r % R, half], w, start=False,
                                                      stop=half == len(W_ROW[k]) - 1)
                                last.then_inc(s.rows, 1)
                                if taps and k == 0:
                                    pe.wait_ge(s.hid, L * i + r - 1 + C)
                                    for c in range(TG):
                                        last = pe.transpose(bank(6 + r % 2)[0:P, c * D:(c + 1) * D],
                                                            uT[:, r % R, 0, c * P:(c + 1) * P], ident[:, :])
                                    last.then_inc(s.htr, 1)

                @blk.scalar
                def _(act):
                    FUNC = ((ACT.Identity, b1_col), (ACT.Silu, bu1_col), (ACT.Relu, b31_col))
                    with act.Fori(0, NI) as i:
                        for t in range(-1, TASKS + 4):
                            if 0 <= t - 1 < PRODUCTS:
                                c = t - 1
                                f, bias = FUNC[c // L]
                                for half in range(halves(c)):
                                    act.wait_ge(s.u, col_of(i, c, half) + 1 + C)
                                    act.activation(uT[:, c % R, half, :], col_bank(c, half)[:, 0:GR],
                                                   f, bias=bias[:, half:half + 1]).then_inc(s.uT, 1)
                            if 0 <= t < PRODUCTS:
                                act.wait_ge(s.tr, row_of(i, t) + 1 + C)
                                act.activation(hT[:, t % 2, :], bank(t % 2)[:, 0:GR], ACT.Relu).then_inc(s.hT, 1)
                            if t + 1 < TASKS:
                                q = t + 1
                                act.wait_ge(s.shift, norm_of(i, q) + 1 + C)
                                if taps:
                                    act.wait_ge(d_xn[q % L], before(K * i + q // L))
                                ln_apply_rest(act, res[:, q % L], ln[q % L], xn[:, q % L], s.xa)
                            if taps and 0 <= t - 3 < L:
                                b = t - 3
                                act.wait_ge(s.htr, L * i + b + 1 + C)
                                act.wait_ge(d_hid[b], before(i))
                                act.activation(flat(hid[0:P, b]), bank(6 + b % 2)[0:P], ACT.Copy).then_inc(s.hid, 1)
                            if dst is not None and 0 <= t - 4 - 2 * L < L:
                                b = t - 4 - 2 * L
                                act.wait_ge(s.res, row_of(i, 2 * L + b) + 1 + C)
                                move(act, res[:, b], dst[L * i + b], d_out[b], store=True)

        row_chain("e", slots(xsrc_d), NG, 5, taps=[slots(xn0_src), slots(xn2_src), slots(xn3_src), slots(hid_src)],
                  map_reads=True)
        row_chain("n", rows(x_in), ND, 10, dst=rows(out))

        SL = 5
        SI = NG // SL
        assert NG % SL == 0

        def in_order(eng, turn):
            with eng.Fori(0, SI) as i:
                for b in range(SL):
                    turn(i, b, SL * i + b)

        def staggered(eng, step):
            def run(i, t, turn=None):
                def late(k):
                    c, b = divmod(t - k, SL)
                    if turn is None or 0 <= SL * (turn + c) + b < NG:
                        yield i + c, b, SL * (i + c) + b
                step(late)

            for t in range(SL):
                run(0, t, 0)
            if SI > 1:
                with eng.Fori(1, SI) as i:
                    for t in range(SL):
                        run(i, t)
            for t in range(SL + 1):
                run(SI, t, SI)

        def reused(n):
            return n - SL + 1 + C

        def tiles(n):
            return bass.ds(TG * n, TG)

        def select(v, which, out, n):
            return v.tensor_tensor(out[0:P].rearrange("p (t q) -> p t q", q=P),
                                   dst_bc[0:P, bass.ds(GR * n, GR)].rearrange("p (t q) -> p t q", q=P),
                                   which[0:P, tiles(n)].unsqueeze(2).broadcast_to((P, TG, P)), ALU.is_equal)

        def run_sums(pe, ps, m, sel):
            for t in range(TG):
                last = pe.matmul(ps[:, t * P:(t + 1) * P], m[0:P, t, :], sel[0:P, t * P:(t + 1) * P],
                                 start=True, stop=True)
            return last

        def run_carry(v, ps, sums, s, b, n):
            for t in range(TG):
                before_it = sums[:, b, t * P - 1:t * P] if t else sums[:, (b - 1) % SL, GR - 1:GR]
                v.wait_ge(s.sum, TG * n + t + 1 + C)
                v.scalar_tensor_tensor(sums[:, b, t * P:(t + 1) * P],
                                       same_bc[:, bass.ds(GR * n + t * P, P)], before_it,
                                       ps[:, t * P:(t + 1) * P], ALU.mult, ALU.add).then_inc(s.sum, 1)

        def stage_indices(gp, cur, which, s, n, k=1):
            gp.tensor_copy(cur, idx[0:P, which, tiles(n)]).then_inc(s.cur, 1)
            gp.wait_ge(s.cur, k * (n + 1) + C)
            gp.sem_inc(s.order, 1)

        with phase() as ctx:
            fs = sb("a_fs", [128, SL, TG, GW], ctx=ctx)
            fd = sb("a_fd", [128, SL, TG, GW], ctx=ctx)
            xd = sb("a_xd", [128, SL, TG, D], ctx=ctx)
            cur = sb("a_cur", [128, SL, 2, TG], i32, ctx=ctx)
            z = sb("a_z", [128, SL, TG, H], ctx=ctx)
            zn = sb("a_zn", [128, SL, TG, H], ctx=ctx)
            ez = sb("a_ez", [128, SL, TG, H], ctx=ctx)
            msg = sb("a_msg", [128, SL, TG, MW], ctx=ctx)
            sel = sb("a_sel", [128, SL, GR], ctx=ctx)
            selc = sb("a_selc", [128, SL, GR], ctx=ctx)
            tot = sb("a_tot", [128, SL, TG, MW], ctx=ctx)
            rw = sb("a_rw", [128, SL, TG, H], ctx=ctx)
            agg = sb("a_agg", [128, SL, TG, D], ctx=ctx)
            deg = sb("a_deg", [128, SL, TG], ctx=ctx)
            dv = sb("a_dv", [128, SL, TG], ctx=ctx)
            sc = sb("a_sc", [128, SL, TG], ctx=ctx)
            ln = ln_buffers(ctx, "a", SL)
            s = counters(ctx, "a", "cur order z zn ez el w msg ones sel selc tot1 totc rw agg x1 deg dv dvs dvl st mv var rstd sc g1n g1")
            d_fs = dma_counters(ctx, "a_fs", SL)
            d_fd = dma_counters(ctx, "a_fd", SL)
            d_xd = dma_counters(ctx, "a_xd", SL)
            d_x1 = dma_counters(ctx, "a_x1_stored", SL)
            d_g1 = dma_counters(ctx, "a_g1_stored", SL)
            x1v, t1v = slots(x1_dst), slots(tab1)
            blk = ctx.enter_context(nc.Block())

            @blk.gpsimd
            def _(gp):
                def step(late):
                    for i, b, n in late(0):
                        gp.wait_ge(s.msg, reused(n))
                        gp.sem_inc(s.order, 1)
                        gp.wait_ge(d_x1[b], before(i))
                        gp.sem_inc(s.order, 1)
                        stage_indices(gp, cur[0:P, b], slice(SRC, DST + 1), s, n)
                        for t in range(TG):
                            gather(gp, fs[0:P, b, t, :], feat_tab, cur[0:P, b, 0, t:t + 1], N - 1, d_fs[b])
                        for t in range(TG):
                            gather(gp, fd[0:P, b, t, :], feat_tab, cur[0:P, b, 1, t:t + 1], N - 1, d_fd[b])
                        for t in range(TG):
                            gather(gp, xd[0:P, b, t, :], x_in, cur[0:P, b, 1, t:t + 1], N - 1, d_xd[b])
                    for i, b, n in late(2):
                        gp.wait_ge(s.deg, n + 1 + C)
                        gp.sem_inc(s.order, 1)
                        gp.tensor_tensor(dv[0:P, b], deg[0:P, b], neghalf[0:P, :], ALU.pow).then_inc(s.dv, 1)
                        ln_power(gp, ln[b], s, n)
                staggered(gp, step)

            @blk.vector
            def _(v):
                start(v, s)
                for one in (*d_x1, *d_g1):
                    v.sem_inc(one, DONE)
                v.memset(msg[:, :, :, D + H:MW], 1.0).then_inc(s.ones, 1)
                v.memset(tot[:, :, :, :], 0.0).then_inc(s.ones, 1)
                v.wait_ge(s.ones, 2 + C)

                def step(late):
                    for i, b, n in late(3):
                        v.wait_ge(s.dv, n + 1 + C)
                        v.tensor_copy(dinv[0:P, tiles(n)], dv[0:P, b]).then_inc(s.dvs, 1)
                        v.tensor_tensor(deg[0:P, b], dv[0:P, b], islast[0:P, tiles(n)], ALU.mult).then_inc(s.dvl, 1)
                        v.wait_ge(s.dvl, n + 1 + C)
                        v.tensor_copy(dinv_last[0:P, tiles(n)], deg[0:P, b]).then_inc(s.dvs, 1)
                        v.wait_ge(s.rstd, n + 1 + C)
                        v.tensor_tensor(sc[0:P, b], ln[b].rstd[0:P], deg[0:P, b], ALU.mult).then_inc(s.sc, 1)
                        v.wait_ge(s.sc, n + 1 + C)
                        ln_apply(v, xd[:, b], ln[b], sc[:, b], agg[:, b], s.g1n)
                    for i, b, n in late(0):
                        v.wait_ge(s.tot1, TG * reused(n) - TG * C + C)
                        select(v, dst_f, sel[:, b], n).then_inc(s.sel, 1)
                        select(v, carry_f, selc[:, b], n).then_inc(s.selc, 1)
                        v.wait_ge(d_fs[b], 16 * TG * (i + 1))
                        v.wait_ge(d_fd[b], 16 * TG * (i + 1))
                        v.tensor_tensor(z[0:P, b], fs[0:P, b, :, D:D + H], fd[0:P, b, :, D + H:GW], ALU.add).then_inc(s.z, 1)
                        v.wait_ge(s.z, n + 1 + C)
                        v.tensor_scalar(zn[0:P, b], z[0:P, b], 0.0, None, ALU.min).then_inc(s.zn, 1)
                    for i, b, n in late(1):
                        v.wait_ge(s.totc, TG * (n + 1) + C)
                        v.reciprocal(rw[0:P, b], tot[0:P, b, :, D:D + H]).then_inc(s.rw, 1)
                        v.tensor_scalar(deg[0:P, b], tot[0:P, b, :, D + H], 1.0, 1.0, ALU.add, ALU.max).then_inc(s.deg, 1)
                        v.wait_ge(s.rw, n + 1 + C)
                        v.wait_ge(d_g1[b], before(i))
                        v.tensor_tensor(agg[0:P, b].rearrange("p t (h f) -> p t h f", f=F),
                                        tot[0:P, b, :, 0:D].rearrange("p t (h f) -> p t h f", f=F),
                                        rw[0:P, b].unsqueeze(3).broadcast_to((P, TG, H, F)), ALU.mult).then_inc(s.agg, 1)
                    for i, b, n in late(0):
                        v.wait_ge(s.ez, n + 1 + C)
                        v.tensor_scalar(ez[0:P, b], ez[0:P, b], 1.0, 0.2, ALU.subtract, ALU.mult).then_inc(s.el, 1)
                        v.wait_ge(s.el, 2 * n + 1 + C)
                        v.scalar_tensor_tensor(z[0:P, b], z[0:P, b], 0.0, ez[0:P, b], ALU.max, ALU.add).then_inc(s.el, 1)
                    for i, b, n in late(1):
                        v.wait_ge(s.agg, n + 1 + C)
                        v.wait_ge(d_xd[b], 16 * TG * (i + 1))
                        v.tensor_tensor(flat(xd[0:P, b]), flat(xd[0:P, b]), flat(agg[0:P, b]), ALU.add).then_inc(s.x1, 1)
                    for i, b, n in late(0):
                        v.wait_ge(s.w, n + 1 + C)
                        v.tensor_tensor(msg[0:P, b, :, 0:D].rearrange("p t (h f) -> p t h f", f=F),
                                        fs[0:P, b, :, 0:D].rearrange("p t (h f) -> p t h f", f=F),
                                        msg[0:P, b, :, D:D + H].unsqueeze(3).broadcast_to((P, TG, H, F)), ALU.mult).then_inc(s.msg, 1)
                    for i, b, n in late(1):
                        v.wait_ge(s.x1, n + 1 + C)
                        ln_stats(v, xd[:, b], ln[b], s, n)
                staggered(v, step)

            @blk.scalar
            def _(act):
                def step(late):
                    for i, b, n in late(0):
                        act.wait_ge(s.zn, n + 1 + C)
                        act.activation(ez[0:P, b], zn[0:P, b], ACT.Exp).then_inc(s.ez, 1)
                    for i, b, n in late(3):
                        act.wait_ge(s.g1n, n + 1 + C)
                        act.activation(flat(agg[0:P, b]), flat(agg[0:P, b]), ACT.Relu).then_inc(s.g1, 1)
                    for i, b, n in late(0):
                        act.wait_ge(s.el, 2 * n + 2 + C)
                        act.activation(msg[0:P, b, :, D:D + H], z[0:P, b], ACT.Exp).then_inc(s.w, 1)
                        for t in range(TG):
                            act.wait_ge(s.tot1, TG * n + t + 1 + C)
                            act.activation(tot[0:P, b, t, :], bank(t % 2)[0:P, 0:MW], ACT.Copy).then_inc(s.totc, 1)
                staggered(act, step)

            @blk.tensor
            def _(pe):
                def turn(i, b, n):
                    pe.wait_ge(s.sel, n + 1 + C)
                    pe.wait_ge(s.selc, n + 1 + C)
                    pe.wait_ge(s.msg, n + 1 + C)
                    for t in range(TG):
                        ps = bank(t % 2)[0:P, 0:MW]
                        pe.wait_ge(s.totc, TG * n + t - 1 + C)
                        pe.matmul(ps, sel[0:P, b, t * P:(t + 1) * P], msg[0:P, b, t, :], start=True, stop=False)
                        pe.wait_ge(s.totc, TG * n + t + C)
                        prev = tot[0:P, b, t - 1, :] if t else tot[0:P, (b - 1) % SL, TG - 1, :]
                        pe.matmul(ps, selc[0:P, b, t * P:(t + 1) * P], prev, start=False, stop=True).then_inc(s.tot1, 1)
                in_order(pe, turn)

            @blk.sync
            def _(sp):
                def turn(i, b, n):
                    sp.wait_ge(s.g1, n + 1 + C)
                    move(sp, xd[:, b], x1v[n], d_x1[b], store=True)
                    move(sp, agg[:, b], t1v[n], d_g1[b], store=True)
                in_order(sp, turn)
                for b in range(SL):
                    sp.wait_ge(d_x1[b], before(SI))
                    sp.wait_ge(d_g1[b], before(SI))

        def convolution(prefix, first, nb_view, self_view, over_tab, x_view, out_views):
            with phase() as ctx:
                hs = sb(prefix + "_hs", [128, SL, TG, D], ctx=ctx)
                gd = sb(prefix + "_gd", [128, SL, TG, D], ctx=ctx)
                xd = None if first else sb(prefix + "_xd", [128, SL, TG, D], ctx=ctx)
                m = sb(prefix + "_m", [128, SL, TG, D], ctx=ctx)
                sel = sb(prefix + "_sel", [128, SL, GR], ctx=ctx)
                sums = sb(prefix + "_sums", [128, SL, GR], ctx=ctx)
                cur = sb(prefix + "_cur", [128, SL, TG], i32, ctx=ctx)
                u = sb(prefix + "_u", [128, SL, TG, D], ctx=ctx)
                o = sb(prefix + "_o", [128, SL, TG, D], ctx=ctx)
                dl = sb(prefix + "_dl", [128, SL, TG], ctx=ctx)
                ln = ln_buffers(ctx, prefix, SL)
                s = counters(ctx, prefix, "cur order sel m ps sum rows u dl leaky o st mv var rstd x")
                d_hs = dma_counters(ctx, prefix + "_hs", SL)
                d_gd = dma_counters(ctx, prefix + "_gd", SL)
                d_xd = dma_counters(ctx, prefix + "_xd", SL)
                d_ov = dma_counters(ctx, prefix + "_ov", SL)
                d_o = dma_counters(ctx, prefix + "_o", SL)
                d_u = dma_counters(ctx, prefix + "_u", SL)
                blk = ctx.enter_context(nc.Block())

                @blk.sync
                def _(sp):
                    def turn(i, b, n):
                        sp.wait_ge(s.m, reused(n))
                        move(sp, hs[:, b], nb_view[n], d_hs[b])
                        move(sp, gd[:, b], self_view[n], d_gd[b])
                        if not first:
                            sp.wait_ge(s.u, reused(n))
                            move(sp, xd[:, b], x_view[n], d_xd[b])
                    in_order(sp, turn)

                @blk.gpsimd
                def _(gp):
                    def step(late):
                        for i, b, n in late(0):
                            gp.wait_ge(d_hs[b], landed(i))
                            gp.sem_inc(s.order, 1)
                            stage_indices(gp, cur[0:P, b], SRC_SLOT, s, n)
                            for t in range(TG):
                                gather(gp, hs[0:P, b, t, :], over_tab, cur[0:P, b, t:t + 1], E - 1, d_ov[b])
                        if not first:
                            for i, b, n in late(3):
                                ln_power(gp, ln[b], s, n)
                    staggered(gp, step)

                @blk.vector
                def _(v):
                    start(v, s, d_hs, d_gd, d_xd, d_o, d_u)
                    v.memset(sums[:, :, :], 0.0).then_inc(s.sum, 1)
                    v.wait_ge(s.sum, 1 + C)

                    def step(late):
                        for i, b, n in late(0):
                            v.wait_ge(s.ps, reused(n))
                            select(v, dst_f, sel[:, b], n).then_inc(s.sel, 1)
                            v.wait_ge(d_hs[b], landed(i))
                            v.wait_ge(d_gd[b], landed(i))
                            v.wait_ge(d_ov[b], 16 * TG * (i + 1))
                            v.scalar_tensor_tensor(flat(m[0:P, b]), flat(hs[0:P, b]), 0.0 if first else 1.0,
                                                   flat(gd[0:P, b]), ALU.max if first else ALU.mult,
                                                   ALU.add).then_inc(s.m, 1)
                        for i, b, n in late(1):
                            v.wait_ge(s.rows, n + 1 + C)
                            if first:
                                v.wait_ge(s.o, reused(n))
                                v.tensor_copy(dl[0:P, b], dinv_last[0:P, tiles(n)]).then_inc(s.dl, 1)
                            else:
                                v.wait_ge(d_xd[b], landed(i))
                                v.wait_ge(d_u[b], before(i))
                            for t in range(TG):
                                last = v.scalar_tensor_tensor(u[0:P, b, t, :], bank(2)[0:P, t * D:(t + 1) * D],
                                                              dinv[0:P, bass.ds(TG * n + t, 1)],
                                                              b1_bc[0:P, :] if first else xd[0:P, b, t, :],
                                                              ALU.mult, ALU.add)
                            last.then_inc(s.u, 1)
                        for i, b, n in late(0):
                            v.wait_ge(s.ps, n + 1 + C)
                            run_carry(v, bank(0), sums, s, b, n)
                        for i, b, n in late(1):
                            v.wait_ge(s.u, n + 1 + C)
                            if first:
                                v.scalar_tensor_tensor(flat(u[0:P, b]), flat(u[0:P, b]), 0.2, flat(u[0:P, b]),
                                                       ALU.mult, ALU.max).then_inc(s.leaky, 1)
                            else:
                                v.tensor_tensor(u[0:P, b], u[0:P, b], out1_bc[0:P, :].unsqueeze(1).broadcast_to((P, TG, D)),
                                                ALU.add).then_inc(s.x, 1)
                                v.wait_ge(s.x, n + 1 + C)
                                ln_stats(v, u[:, b], ln[b], s, n)
                        if not first:
                            for i, b, n in late(4):
                                v.wait_ge(s.rstd, n + 1 + C)
                                v.wait_ge(d_o[b], before(i))
                                ln_apply(v, u[:, b], ln[b], ln[b].rstd, o[:, b], s.o)
                    staggered(v, step)

                @blk.tensor
                def _(pe):
                    def step(late):
                        for i, b, n in late(1):
                            pe.wait_ge(s.sum, TG * (n + 1) + 1 + C)
                            pe.wait_ge(s.u, n + C)
                            rows_times(pe, bank(2), sums[:, b], w1[:, :] if first else w2g[:, :]).then_inc(s.rows, 1)
                        for i, b, n in late(0):
                            pe.wait_ge(s.sel, n + 1 + C)
                            pe.wait_ge(s.m, n + 1 + C)
                            pe.wait_ge(s.sum, TG * n + 1 + C)
                            run_sums(pe, bank(0), m[:, b], sel[:, b]).then_inc(s.ps, 1)
                    staggered(pe, step)

                @blk.scalar
                def _(act):
                    def turn(i, b, n):
                        if first:
                            act.wait_ge(s.leaky, n + 1 + C)
                            act.wait_ge(s.dl, n + 1 + C)
                            act.wait_ge(d_o[b], before(i))
                            for t in range(TG):
                                last = act.activation(o[0:P, b, t, :], u[0:P, b, t, :], ACT.Copy,
                                                      scale=dl[0:P, b, t:t + 1])
                            last.then_inc(s.o, 1)
                        act.wait_ge(s.o, n + 1 + C)
                        move(act, o[:, b], out_views[0][n], d_o[b], store=True)
                        if not first:
                            move(act, u[:, b], out_views[1][n], d_u[b], store=True)
                    in_order(act, turn)
                    for b in range(SL):
                        act.wait_ge(d_o[b], before(SI))
                        if not first:
                            act.wait_ge(d_u[b], before(SI))

        def message_layer():
            with phase() as ctx:
                hs = sb("m_hs", [128, SL, TG, D], ctx=ctx)
                hd = sb("m_hd", [128, SL, TG, D], ctx=ctx)
                xd = sb("m_xd", [128, SL, TG, D], ctx=ctx)
                cur = sb("m_cur", [128, SL, 2, TG], i32, ctx=ctx)
                sT = sb("m_sT", [128, SL, GR], ctx=ctx)
                dT = sb("m_dT", [128, SL, GR], ctx=ctx)
                vT = sb("m_vT", [128, SL, GR], ctx=ctx)
                m = sb("m_m", [128, SL, TG, D], ctx=ctx)
                sel = sb("m_sel", [128, SL, GR], ctx=ctx)
                sums = sb("m_sums", [128, SL, GR], ctx=ctx)
                sc = sb("m_sc", [128, SL, TG], ctx=ctx)
                ln = ln_buffers(ctx, "m", SL)
                s = counters(ctx, "m", "cur order trs sT trd dT u v rows m sel ps sum u2 w rows2 x st mv var rstd sc gn g")
                d_hs = dma_counters(ctx, "m_hs", SL)
                d_xd = dma_counters(ctx, "m_xd", SL)
                d_ov = dma_counters(ctx, "m_ov", SL)
                d_hd = dma_counters(ctx, "m_hd", SL)
                d_x3 = dma_counters(ctx, "m_x3", SL)
                d_g = dma_counters(ctx, "m_g", SL)
                hsv, xdv, x3v, t4v = slots(xn2_src), slots(x2_dst), slots(x3_dst), slots(tab4)
                PS_S, PS_D, PS_U, PS_MSG, PS_SUM, PS_U2, PS_UPD = range(7)
                blk = ctx.enter_context(nc.Block())

                @blk.sync
                def _(sp):
                    def turn(i, b, n):
                        sp.wait_ge(s.trs, reused(n))
                        move(sp, hs[:, b], hsv[n], d_hs[b])
                        sp.wait_ge(d_x3[b], before(i))
                        move(sp, xd[:, b], xdv[n], d_xd[b])
                    in_order(sp, turn)

                @blk.gpsimd
                def _(gp):
                    def step(late):
                        for i, b, n in late(0):
                            gp.wait_ge(d_hs[b], landed(i))
                            gp.sem_inc(s.order, 1)
                            gp.wait_ge(s.trd, reused(n))
                            gp.sem_inc(s.order, 1)
                            stage_indices(gp, cur[0:P, b], slice(SRC_SLOT, DST_SLOT + 1), s, n)
                            for t in range(TG):
                                gather(gp, hs[0:P, b, t, :], tab3, cur[0:P, b, 0, t:t + 1], E - 1, d_ov[b])
                            for t in range(TG):
                                gather(gp, hd[0:P, b, t, :], tab3, cur[0:P, b, 1, t:t + 1], E - 1, d_hd[b])
                        for i, b, n in late(4):
                            ln_power(gp, ln[b], s, n)
                    staggered(gp, step)

                @blk.vector
                def _(v):
                    start(v, s, d_hs, d_xd, d_x3, d_g)
                    v.memset(sums[:, :, :], 0.0).then_inc(s.sum, 1)
                    v.wait_ge(s.sum, 1 + C)

                    def step(late):
                        for i, b, n in late(5):
                            v.wait_ge(s.rstd, n + 1 + C)
                            v.tensor_tensor(sc[0:P, b], ln[b].rstd[0:P], islast[0:P, tiles(n)], ALU.mult).then_inc(s.sc, 1)
                            v.wait_ge(s.sc, n + 1 + C)
                            ln_apply(v, xd[:, b], ln[b], sc[:, b], m[:, b], s.gn)
                        for i, b, n in late(0):
                            v.wait_ge(s.ps, reused(n))
                            select(v, dst_f, sel[:, b], n).then_inc(s.sel, 1)
                        for i, b, n in late(1):
                            v.wait_ge(s.rows, n + 1 + C)
                            v.wait_ge(d_g[b], before(i))
                            v.tensor_copy(flat(m[0:P, b]), bank(PS_MSG)[0:P]).then_inc(s.m, 1)
                        for i, b, n in late(2):
                            v.wait_ge(s.rows2, n + 1 + C)
                            v.wait_ge(d_xd[b], landed(i))
                            v.tensor_tensor(flat(xd[0:P, b]), flat(xd[0:P, b]), bank(PS_UPD)[0:P], ALU.add).then_inc(s.x, 1)
                        for i, b, n in late(1):
                            v.wait_ge(s.ps, n + 1 + C)
                            run_carry(v, bank(PS_SUM), sums, s, b, n)
                        for i, b, n in late(2):
                            v.wait_ge(s.x, n + 1 + C)
                            ln_stats(v, xd[:, b], ln[b], s, n)
                    staggered(v, step)

                @blk.tensor
                def _(pe):
                    def step(late):
                        for i, b, n in late(2):
                            pe.wait_ge(s.w, n + C)
                            pe.matmul(bank(PS_U2)[:, 0:GR], wu1[:, 0, :], dT[:, b, :], start=True, stop=False)
                            pe.wait_ge(s.sum, TG * (n + 1) + 1 + C)
                            pe.matmul(bank(PS_U2)[:, 0:GR], wu1[:, 1, :], sums[:, b, :], start=False, stop=True).then_inc(s.u2, 1)
                        for i, b, n in late(1):
                            pe.wait_ge(s.v, n + 1 + C)
                            pe.wait_ge(s.m, n + C)
                            bias_rows(pe, bank(PS_MSG), BIAS_M2)
                            rows_times(pe, bank(PS_MSG), vT[:, b], wm2[:, :], start=False).then_inc(s.rows, 1)
                        for i, b, n in late(2):
                            pe.wait_ge(s.w, n + 1 + C)
                            pe.wait_ge(s.x, n + C)
                            bias_rows(pe, bank(PS_UPD), BIAS_U2)
                            rows_times(pe, bank(PS_UPD), vT[:, b], wu2[:, :], start=False).then_inc(s.rows2, 1)
                        for i, b, n in late(1):
                            pe.wait_ge(s.sel, n + 1 + C)
                            pe.wait_ge(s.m, n + 1 + C)
                            pe.wait_ge(s.sum, TG * n + 1 + C)
                            run_sums(pe, bank(PS_SUM), m[:, b], sel[:, b]).then_inc(s.ps, 1)
                        for i, b, n in late(0):
                            pe.wait_ge(d_hs[b], landed(i))
                            pe.wait_ge(d_ov[b], 16 * TG * (i + 1))
                            pe.wait_ge(s.sT, n + C)
                            transposes(pe, bank(PS_S), hs[:, b]).then_inc(s.trs, 1)
                            pe.wait_ge(d_hd[b], 16 * TG * (i + 1))
                            pe.wait_ge(s.dT, n + C)
                            transposes(pe, bank(PS_D), hd[:, b]).then_inc(s.trd, 1)
                            pe.wait_ge(s.sT, n + 1 + C)
                            pe.wait_ge(s.v, n + C)
                            pe.matmul(bank(PS_U)[:, 0:GR], wm1[:, 0, :], sT[:, b, :], start=True, stop=False)
                            pe.wait_ge(s.dT, n + 1 + C)
                            pe.matmul(bank(PS_U)[:, 0:GR], wm1[:, 1, :], dT[:, b, :], start=False, stop=True).then_inc(s.u, 1)
                    staggered(pe, step)

                @blk.scalar
                def _(act):
                    def step(late):
                        for i, b, n in late(5):
                            act.wait_ge(s.gn, n + 1 + C)
                            act.activation(flat(m[0:P, b]), flat(m[0:P, b]), ACT.Relu).then_inc(s.g, 1)
                        for i, b, n in late(2):
                            act.wait_ge(s.u2, n + 1 + C)
                            act.activation(vT[:, b, :], bank(PS_U2)[:, 0:GR], ACT.Silu, bias=bu1_col[:, 0:1]).then_inc(s.w, 1)
                        for i, b, n in late(0):
                            act.wait_ge(s.trs, n + 1 + C)
                            act.activation(sT[:, b, :], bank(PS_S)[:, 0:GR], ACT.Relu).then_inc(s.sT, 1)
                            act.wait_ge(s.trd, n + 1 + C)
                            act.activation(dT[:, b, :], bank(PS_D)[:, 0:GR], ACT.Relu).then_inc(s.dT, 1)
                            act.wait_ge(s.u, n + 1 + C)
                            act.activation(vT[:, b, :], bank(PS_U)[:, 0:GR], ACT.Silu, bias=bm1_col[:, 0:1]).then_inc(s.v, 1)
                        for i, b, n in late(5):
                            act.wait_ge(s.g, n + 1 + C)
                            move(act, m[:, b], t4v[n], d_g[b], store=True)
                            move(act, xd[:, b], x3v[n], d_x3[b], store=True)
                    staggered(act, step)
                    for b in range(SL):
                        act.wait_ge(d_g[b], before(SI))
                        act.wait_ge(d_x3[b], before(SI))

        def isomorphism_layer():
            with phase() as ctx:
                hs = sb("g_hs", [128, SL, TG, D], ctx=ctx)
                gd = sb("g_gd", [128, SL, TG, D], ctx=ctx)
                xd = sb("g_xd", [128, SL, TG, D], ctx=ctx)
                cur = sb("g_cur", [128, SL, TG], i32, ctx=ctx)
                at = sb("g_at", [128, SL, TG], i32, ctx=ctx)
                m = sb("g_m", [128, SL, TG, D], ctx=ctx)
                sel = sb("g_sel", [128, SL, GR], ctx=ctx)
                sums = sb("g_sums", [128, SL, GR], ctx=ctx)
                hT = sb("g_hT", [128, SL, 2, GR], ctx=ctx)
                s = counters(ctx, "g", "cur at order sel m ps sum u h rows x")
                d_hs = dma_counters(ctx, "g_hs", SL)
                d_gd = dma_counters(ctx, "g_gd", SL)
                d_xd = dma_counters(ctx, "g_xd", SL)
                d_ov = dma_counters(ctx, "g_ov", SL)
                d_out = dma_counters(ctx, "g_out", SL)
                hsv, xdv, gdv = slots(xn3_src), slots(x3_dst), slots(tab4)
                PS_SUM, PS_H, PS_OUT = 0, 2, 4
                blk = ctx.enter_context(nc.Block())

                @blk.sync
                def _(sp):
                    def turn(i, b, n):
                        sp.wait_ge(s.m, reused(n))
                        move(sp, hs[:, b], hsv[n], d_hs[b])
                        move(sp, gd[:, b], gdv[n], d_gd[b])
                        sp.wait_ge(d_out[b], 16 * TG * i + 16)
                        move(sp, xd[:, b], xdv[n], d_xd[b])
                    in_order(sp, turn)

                @blk.gpsimd
                def _(gp):
                    def step(late):
                        for i, b, n in late(0):
                            gp.wait_ge(d_hs[b], landed(i))
                            gp.sem_inc(s.order, 1)
                            stage_indices(gp, cur[0:P, b], SRC_SLOT, s, n)
                            for t in range(TG):
                                gather(gp, hs[0:P, b, t, :], tab4, cur[0:P, b, t:t + 1], E - 1, d_ov[b])
                        for i, b, n in late(3):
                            gp.wait_ge(d_out[b], 16 * TG * i + 16)
                            gp.sem_inc(s.order, 1)
                            gp.tensor_copy(at[0:P, b], idx[0:P, LAST, tiles(n)]).then_inc(s.at, 1)
                            gp.wait_ge(s.at, n + 1 + C)
                            gp.sem_inc(s.order, 1)
                            gp.wait_ge(s.x, n + 1 + C)
                            gp.sem_inc(s.order, 1)
                            for t in range(TG):
                                gp.indirect_dma_start(out, bass.IndirectOffsetOnAxis(at[0:P, b, t:t + 1], 0),
                                                      xd[0:P, b, t, :], None, bounds_check=N - 1,
                                                      oob_is_err=False).then_inc(d_out[b], 16)
                    for b in range(SL):
                        count_one(gp, xd[0:P, b, 0, :], tab4, d_out[b])
                    staggered(gp, step)
                    for b in range(SL):
                        gp.wait_ge(d_out[b], 16 * TG * SI + 16)

                @blk.vector
                def _(v):
                    start(v, s, d_hs, d_gd, d_xd)
                    v.memset(sums[:, :, :], 0.0).then_inc(s.sum, 1)
                    v.wait_ge(s.sum, 1 + C)

                    def step(late):
                        for i, b, n in late(0):
                            v.wait_ge(s.ps, reused(n))
                            select(v, dst_f, sel[:, b], n).then_inc(s.sel, 1)
                            v.wait_ge(d_hs[b], landed(i))
                            v.wait_ge(d_gd[b], landed(i))
                            v.wait_ge(d_ov[b], 16 * TG * (i + 1))
                            v.scalar_tensor_tensor(flat(m[0:P, b]), flat(hs[0:P, b]), 0.0, flat(gd[0:P, b]),
                                                   ALU.max, ALU.add).then_inc(s.m, 1)
                            v.wait_ge(s.ps, n + 1 + C)
                            run_carry(v, bank(PS_SUM), sums, s, b, n)
                        for i, b, n in late(1):
                            v.wait_ge(s.rows, n + 1 + C)
                            v.wait_ge(d_xd[b], landed(i))
                            v.tensor_tensor(flat(xd[0:P, b]), flat(xd[0:P, b]), bank(PS_OUT)[0:P], ALU.add).then_inc(s.x, 1)
                    staggered(v, step)

                @blk.tensor
                def _(pe):
                    def step(late):
                        for i, b, n in late(1):
                            pe.wait_ge(s.sum, TG * (n + 1) + 1 + C)
                            for half in range(2):
                                pe.wait_ge(s.h, 2 * n + half - 1 + C)
                                pe.matmul(bank(PS_H + half)[:, 0:GR], w31[:, half * D:(half + 1) * D], sums[:, b, :],
                                          start=True, stop=True).then_inc(s.u, 1)
                        for i, b, n in late(0):
                            pe.wait_ge(s.sel, n + 1 + C)
                            pe.wait_ge(s.m, n + 1 + C)
                            pe.wait_ge(s.sum, TG * n + 1 + C)
                            run_sums(pe, bank(PS_SUM), m[:, b], sel[:, b]).then_inc(s.ps, 1)
                        for i, b, n in late(1):
                            pe.wait_ge(s.x, n + C)
                            bias_rows(pe, bank(PS_OUT), BIAS_32)
                            for half in range(2):
                                pe.wait_ge(s.h, 2 * n + half + 1 + C)
                                last = rows_times(pe, bank(PS_OUT), hT[:, b, half], w32[:, half, :], start=False, stop=half == 1)
                            last.then_inc(s.rows, 1)
                    staggered(pe, step)

                @blk.scalar
                def _(act):
                    def turn(i, b, n):
                        for half in range(2):
                            act.wait_ge(s.rows, reused(n))
                            act.wait_ge(s.u, 2 * n + half + 1 + C)
                            act.activation(hT[:, b, half, :], bank(PS_H + half)[:, 0:GR], ACT.Relu,
                                           bias=b31_col[:, half:half + 1]).then_inc(s.h, 1)
                    in_order(act, turn)

        convolution("c", True, slots(xn0_src), slots(tab1), tab1, None, [slots(tab2)])
        convolution("d", False, slots(hid_src), slots(tab2), tab2, slots(x1_dst), [slots(tab3), slots(x2_dst)])
        message_layer()
        isomorphism_layer()


_INS = ['x', 'src', 'dst', 'L0_gnn_W', 'L0_gnn_source_scorer', 'L0_gnn_target_scorer', 'L1_gnn_ctx', 'L1_gnn_W1',
        'L1_gnn_b1', 'L1_gnn_W2', 'L1_gnn_b2', 'L1_gnn_Wg', 'L1_gnn_bg', 'L1_gnn_Wb', 'L2_gnn_W_msg1',
        'L2_gnn_b_msg1', 'L2_gnn_W_msg2', 'L2_gnn_b_msg2', 'L2_gnn_W_upd1', 'L2_gnn_b_upd1', 'L2_gnn_W_upd2',
        'L2_gnn_b_upd2', 'L3_gnn_W1', 'L3_gnn_b1', 'L3_gnn_W2', 'L3_gnn_b2']


def kernel(**inputs):
    import numpy as _np
    import concourse.bacc as _bacc
    from concourse import mybir as _mybir
    from concourse.bass_utils import run_bass_kernel_spmd as _run

    nc = _bacc.Bacc("TRN2", target_bir_lowering=False, num_devices=1)
    arrays, tensors = {}, {}
    for name in _INS:
        a = _np.ascontiguousarray(inputs[name])
        arrays[f"in_{name}"] = a
        tensors[name] = nc.dram_tensor(f"in_{name}", a.shape, _mybir.dt.from_np(a.dtype), kind="ExternalInput").ap()
    shape = tuple(inputs["x"].shape)
    out = nc.dram_tensor("out_x", shape, _mybir.dt.float32, kind="ExternalOutput").ap()
    gnn_four_layers(nc, tensors, out)
    r = _run(nc, [arrays], core_ids=[0])
    return r.results[0]["out_x"]
```

```python
import concourse.bass as bass
from concourse import mybir
from contextlib import ExitStack, contextmanager
from collections import namedtuple


def gnn_four_layers(nc, T, out):
    f32, i32, bf16 = mybir.dt.float32, mybir.dt.int32, mybir.dt.bfloat16
    ALU = mybir.AluOpType
    ACT = mybir.ActivationFunctionType
    AX = mybir.AxisListType

    x_in, src_in, dst_in = T["x"], T["src"], T["dst"]
    N, D = x_in.shape
    E = src_in.shape[0]
    H, F = T["L0_gnn_source_scorer"].shape[0], T["L0_gnn_source_scorer"].shape[2]
    P = 125
    TG = 4
    GR = P * TG
    NT, NG = E // P, E // GR
    ND = N // GR
    J = N // H
    NJ = J // P
    GPN = D // F
    GW = D + 2 * H
    FW = H + D
    MW = D + H + 1
    NOWHERE = 1 << 17
    EPS = 1e-5
    assert E % GR == 0 and N % GR == 0 and J % P == 0 and GPN * F == D and H * F == D

    def dram(name, shape, dt=f32):
        return nc.dram_tensor(name, shape, dt, kind="Internal").ap()

    feat_tab = dram("feat_tab", (N, FW))
    tgt_tab = dram("tgt_tab", (N, H))
    slot_of = dram("slot_of", (N, 1), i32)
    xsrc_d = dram("xsrc_d", (E, D))
    xn0_src = dram("xn0_src", (E, D))
    hid_src = dram("hid_src", (E, D))
    xn2_src = dram("xn2_src", (E, D))
    xn3_src = dram("xn3_src", (E, D))
    tab1 = dram("tab1", (E, D))
    tab2 = dram("tab2", (E, D))
    tab3 = dram("tab3", (E, D))
    tab4 = dram("tab4", (E, D))
    x1_dst = dram("x1_dst", (E, D))
    x2_dst = dram("x2_dst", (E, D))
    x3_dst = dram("x3_dst", (E, D))

    def slots(t):
        return t.rearrange("(n t p) d -> n p t d", p=P, t=TG)

    def rows(t):
        return t.rearrange("(n p t) d -> n p t d", p=P, t=TG)

    CUTS = ((0, 112), (112, P))
    DONE = 16 * len(CUTS)

    def move(eng, tile, view, sem, store=False):
        for a, z in CUTS:
            if store:
                eng.dma_start(view[a:z], tile[a:z]).then_inc(sem, 16)
            else:
                eng.dma_start(tile[a:z], view[a:z]).then_inc(sem, 16)

    def gather(gp, dst, table, index, limit, sem):
        gp.indirect_dma_start(dst, None, table, bass.IndirectOffsetOnAxis(index, 0), bounds_check=limit,
                              oob_is_err=False).then_inc(sem, 16)

    top = ExitStack()
    with top:
        def sb(name, shape, dt=f32, ctx=top):
            return ctx.enter_context(nc.sbuf_tensor(name, shape, dt))

        def sem(name, ctx):
            one = nc.alloc_semaphore(name)
            sems_of_phase.append(one)
            return one

        sems_of_phase = []

        @contextmanager
        def phase():
            with ExitStack() as ctx:
                yield ctx
            nc.clear_and_free_semaphores(sems_of_phase)
            nc.all_engine_barrier()
            sems_of_phase.clear()

        ident = sb("ident", [128, 128])
        w_feat = sb("w_feat", [128, H, GW])
        w1 = sb("w1", [128, D])
        w2g = sb("w2g", [128, D])
        wm1 = sb("wm1", [128, 2, D])
        wm2 = sb("wm2", [128, D])
        wu1 = sb("wu1", [128, 2, D])
        wu2 = sb("wu2", [128, D])
        w31 = sb("w31", [128, 2 * D])
        w32 = sb("w32", [128, 2, D])
        b1_col = sb("b1_col", [128, 1])
        bm1_col = sb("bm1_col", [128, 1])
        bu1_col = sb("bu1_col", [128, 1])
        b31_col = sb("b31_col", [128, 2])
        b1_bc = sb("b1_bc", [128, D])
        out1_bc = sb("out1_bc", [128, D])
        bias_parts = sb("bias_parts", [3, 4, TG * D], bf16)
        BIAS_OUT1, BIAS_M2, BIAS_U2, BIAS_32 = range(4)
        ones3 = sb("ones3", [3, 128], bf16)
        neghalf = sb("neghalf", [128, TG])

        nowhere = sb("nowhere", [128, 1], i32)

        idx = sb("idx", [128, 6, NT], i32)
        SRC, DST, LAST, SLOT, SRC_SLOT, DST_SLOT = range(6)
        dst_f = sb("dst_f", [128, NT])
        carry_f = sb("carry_f", [128, NT])
        islast = sb("islast", [128, NT])
        dinv = sb("dinv", [128, NT])
        dinv_last = sb("dinv_last", [128, NT])
        dst_bc = sb("dst_bc", [128, E])
        same_bc = sb("same_bc", [128, E], bf16)

        psum = top.enter_context(nc.psum_tensor("psum", [128, 8, 512], f32))

        with phase() as ctx:
            def tmp(name, shape, dt=f32):
                return sb(name, shape, dt, ctx)

            s_w = sem("s_weights_loaded", ctx)
            s_c = sem("s_ctx_loaded", ctx)
            s_e = sem("s_edges_loaded", ctx)
            s_b = sem("s_dst_broadcast_loaded", ctx)
            s_id = sem("s_identity", ctx)
            s_v = sem("s_vector_step", ctx)
            s_mm = sem("s_gate_products", ctx)
            s_sig = sem("s_gate_sigmoid", ctx)
            s_map = sem("s_map_blank", ctx)
            s_mst = sem("s_map_stored", ctx)
            s_slot = sem("s_slot_numbers", ctx)
            s_bc = sem("s_broadcast_converted", ctx)

            wsc = tmp("wsc", [128, 2, H, F])
            wtmp = tmp("wtmp", [128, 2, D])
            w2_raw = tmp("w2_raw", [128, D])
            ctx_col = tmp("ctx_col", [64, 1])
            ctx_rep = tmp("ctx_rep", [64, 128])
            wg = tmp("wg", [64, D])
            wb = tmp("wb", [64, D])
            bg_bc = tmp("bg_bc", [128, D])
            b2_bc = tmp("b2_bc", [128, D])
            gate = tmp("gate", [128, D])
            bias3 = tmp("bias3", [3, 4, D])
            part = tmp("part", [3, 3, 4, D], bf16)
            part_mask = tmp("part_mask", [3, 3])
            next_i = tmp("next_i", [128, NT], i32)
            next_f = tmp("next_f", [128, NT])
            last_f = tmp("last_f", [128, NT])
            blank = tmp("blank", [128, N // P], i32)
            CH = E // 5
            stage = tmp("stage", [128, CH], i32)
            prev_bc = tmp("prev_bc", [128, NT])

            pg, pb = psum[:, 0, 0:D], psum[:, 1, 0:D]
            W = T["L0_gnn_W"]
            blk = ctx.enter_context(nc.Block())

            n_w = [0]

            @blk.sync
            def _(sp):
                def load(dst, src):
                    n_w[0] += 16
                    sp.dma_start(dst, src).then_inc(s_w, 16)

                def edge(dst, src):
                    sp.dma_start(dst, src).then_inc(s_e, 16)

                def wide(t):
                    return t.rearrange("(a d) -> a d", a=1).broadcast_to((128, t.shape[0]))

                with nc.allow_non_contiguous_dma(reason="index columns and bias columns, once"):
                    edge(idx[0:P, SRC, :], src_in.rearrange("(t p) -> p t", p=P))
                    edge(idx[0:P, DST, :], dst_in.rearrange("(t p) -> p t", p=P))
                    edge(next_i[0:P - 1, :], dst_in.rearrange("(t p) -> p t", p=P)[1:P, :])
                    edge(next_i[P - 1:P, 0:NT - 1], dst_in.rearrange("(a t p) -> a t p", a=1, p=P)[:, 1:NT, 0])
                    load(ctx_col[:, :], T["L1_gnn_ctx"].rearrange("a c -> c a"))
                    for d, s in ((b1_col, "L1_gnn_b1"), (bm1_col, "L2_gnn_b_msg1"), (bu1_col, "L2_gnn_b_upd1")):
                        load(d[:, :], T[s].rearrange("(d a) -> d a", a=1))
                    load(b31_col[:, :], T["L3_gnn_b1"].rearrange("(a d) -> d a", d=D))
                for h in range(H):
                    load(w_feat[:, h, 0:D], W)
                for k, s in enumerate(("L0_gnn_target_scorer", "L0_gnn_source_scorer")):
                    load(wsc[:, k, :, :].rearrange("p h f -> p (h f)"),
                         T[s].rearrange("h a f -> a (h f)").broadcast_to((128, D)))
                load(wg[:, :], T["L1_gnn_Wg"])
                load(wb[:, :], T["L1_gnn_Wb"])
                load(w1[:, :], T["L1_gnn_W1"])
                load(w2_raw[:, :], T["L1_gnn_W2"])
                for c in range(2):
                    load(wm1[:, c, :], T["L2_gnn_W_msg1"][c * D:(c + 1) * D, :])
                    load(wu1[:, c, :], T["L2_gnn_W_upd1"][c * D:(c + 1) * D, :])
                    load(w32[:, c, :], T["L3_gnn_W2"][c * D:(c + 1) * D, :])
                load(wm2[:, :], T["L2_gnn_W_msg2"])
                load(wu2[:, :], T["L2_gnn_W_upd2"])
                load(w31[:, :], T["L3_gnn_W1"])
                load(b1_bc[:, :], wide(T["L1_gnn_b1"]))
                load(b2_bc[:, :], wide(T["L1_gnn_b2"]))
                load(bg_bc[:, :], wide(T["L1_gnn_bg"]))
                for k, s in ((BIAS_M2, "L2_gnn_b_msg2"), (BIAS_U2, "L2_gnn_b_upd2"), (BIAS_32, "L3_gnn_b2")):
                    load(bias3[:, k, :], T[s].rearrange("(a d) -> a d", a=1).broadcast_to((3, D)))
                for c in range(5):
                    if c:
                        sp.wait_ge(s_bc, c)
                    sp.dma_start(stage[:, :], wide(dst_in[c * CH:(c + 1) * CH])).then_inc(s_b, 16)
                sp.wait_ge(s_map, 1)
                sp.dma_start(slot_of.rearrange("(p c) a -> p (c a)", p=P), blank[0:P, :]).then_inc(s_mst, 16)
                sp.wait_ge(s_mst, 16)

            @blk.gpsimd
            def _(gp):
                gp.memset(ident[:, :], 0.0).then_inc(s_id, 1)
                gp.memset(neghalf[:, :], -0.5).then_inc(s_id, 1)
                gp.memset(ones3[:, :], 1.0).then_inc(s_id, 1)
                gp.memset(part_mask[:, :], 0.0).then_inc(s_id, 1)
                gp.wait_ge(s_id, 4)
                gp.affine_select(out=ident[:, :], in_=ident[:, :], compare_op=ALU.not_equal, fill=1.0, base=0,
                                 pattern=[[-1, 128]], channel_multiplier=1).then_inc(s_id, 1)
                gp.affine_select(out=part_mask[:, :], in_=part_mask[:, :], compare_op=ALU.not_equal, fill=1.0,
                                 base=0, pattern=[[-1, 3]], channel_multiplier=1).then_inc(s_id, 1)
                gp.memset(nowhere[:, :], NOWHERE)
                gp.memset(blank[:, :], NOWHERE).then_inc(s_map, 1)
                gp.iota(idx[0:P, SLOT, :], pattern=[[P, NT]], base=0, channel_multiplier=1).then_inc(s_slot, 1)
                gp.wait_ge(s_v, 3 * H + 3)
                gp.affine_select(out=carry_f[0:P, :], in_=carry_f[0:P, :], compare_op=ALU.is_ge, fill=-1.0,
                                 base=-(P - 1), pattern=[[0, NT]], channel_multiplier=1).then_inc(s_slot, 1)
                gp.wait_ge(s_slot, 2)

            @blk.vector
            def _(v):
                steps = [0]

                def step(ins):
                    steps[0] += 1
                    ins.then_inc(s_v, 1)
                    v.wait_ge(s_v, steps[0])

                v.wait_ge(s_w, n_w[0])
                for h in range(H):
                    for k in range(2):
                        step(v.tensor_tensor(wtmp[:, k, :].rearrange("p (g f) -> p g f", f=F),
                                             w_feat[:, h, 0:D].rearrange("p (g f) -> p g f", f=F),
                                             wsc[:, k, h, :].unsqueeze(1).broadcast_to((128, GPN, F)), ALU.mult))
                    step(v.tensor_reduce(w_feat[:, h, D:GW], wtmp[:, :, :].rearrange("p k (g f) -> p (k g) f", f=F),
                                         AX.X, ALU.add))
                v.wait_ge(s_e, 64)
                step(v.tensor_copy(dst_f[0:P, :], idx[0:P, DST, :]))
                step(v.memset(carry_f[0:P, :], -1.0))
                step(v.tensor_copy(carry_f[0:P, 1:NT], dst_f[0:P, 0:NT - 1]))
                step(v.memset(next_f[0:P, :], -1.0))
                step(v.tensor_copy(next_f[0:P - 1, :], next_i[0:P - 1, :]))
                step(v.tensor_copy(next_f[96:P, 0:NT - 1], next_i[96:P, 0:NT - 1]))
                step(v.tensor_tensor(islast[0:P, :], dst_f[0:P, :], next_f[0:P, :], ALU.not_equal))
                step(v.tensor_scalar(last_f[0:P, :], islast[0:P, :], -float(NOWHERE), float(NOWHERE), ALU.mult, ALU.add))
                step(v.tensor_tensor(idx[0:P, LAST, :], last_f[0:P, :], dst_f[0:P, :], ALU.add))
                step(v.tensor_copy(ctx_rep[:, :], ctx_col[:, :].broadcast_to((64, 128))))
                v.wait_ge(s_mm, 1)
                step(v.tensor_tensor(bg_bc[:, :], pg, bg_bc[:, :], ALU.add))
                v.wait_ge(s_sig, 1)
                step(v.tensor_tensor(w2g[:, :], w2_raw[:, :], gate[:, :], ALU.mult))
                step(v.tensor_tensor(b2_bc[:, :], b2_bc[:, :], gate[:, :], ALU.mult))
                step(v.tensor_tensor(out1_bc[:, :], pb, b2_bc[:, :], ALU.add))
                step(v.tensor_copy(bias3[:, BIAS_OUT1, :], out1_bc[0:3, :]))
                v.wait_ge(s_id, 6)
                for k in range(3):
                    step(v.tensor_copy(part[:, k, :, :], bias3[:, :, :]))
                    if k < 2:
                        step(v.tensor_tensor(bias3[:, :, :], bias3[:, :, :], part[:, k, :, :], ALU.subtract))
                step(v.tensor_scalar(part[:, 0, :, :], part[:, 0, :, :], part_mask[:, 0:1], None, ALU.mult))
                step(v.scalar_tensor_tensor(part[:, 1, :, :], part[:, 1, :, :], part_mask[:, 1:2],
                                            part[:, 0, :, :], ALU.mult, ALU.add))
                for r in range(TG):
                    step(v.scalar_tensor_tensor(bias_parts[:, :, r * D:(r + 1) * D], part[:, 2, :, :],
                                                part_mask[:, 2:3], part[:, 1, :, :], ALU.mult, ALU.add))
                for c in range(5):
                    v.wait_ge(s_b, 16 * (c + 1))
                    v.tensor_copy(dst_bc[:, c * CH:(c + 1) * CH], stage[:, :]).then_inc(s_bc, 1)
                v.wait_ge(s_bc, 5)
                step(v.memset(prev_bc[:, 0:1], -1.0))
                step(v.tensor_copy(prev_bc[:, 1:NT], dst_bc[:, :].rearrange("p (t q) -> p t q", q=P)[:, 0:NT - 1, P - 1]))
                step(v.tensor_tensor(same_bc[:, :].rearrange("p (t q) -> p t q", q=P),
                                     dst_bc[:, :].rearrange("p (t q) -> p t q", q=P),
                                     prev_bc[:, :].unsqueeze(2).broadcast_to((128, NT, P)), ALU.is_equal))

            @blk.tensor
            def _(pe):
                pe.wait_ge(s_v, 3 * H + 10)
                pe.matmul(pg, ctx_rep[:, :], wg[:, :], start=True, stop=True)
                pe.matmul(pb, ctx_rep[:, :], wb[:, :], start=True, stop=True).then_inc(s_mm, 1)

            @blk.scalar
            def _(act):
                act.wait_ge(s_v, 3 * H + 11)
                act.activation(gate[:, :], bg_bc[:, :], ACT.Sigmoid).then_inc(s_sig, 1)

        C = 20

        def counters(ctx, prefix, names):
            names = (names + " hold").split()
            return namedtuple("Counters", names)(*[sem(f"{prefix}_{n}", ctx) for n in names])

        def dma_counters(ctx, name, n):
            return [sem(f"{name}{b}", ctx) for b in range(n)]

        def start(eng, s, *dma):
            for one in s:
                eng.sem_inc(one, C)
            for many in dma:
                for one in many:
                    eng.sem_inc(one, DONE)

        def before(k):
            return DONE * k + DONE

        def landed(k):
            return DONE * k + 2 * DONE

        def count_one(gp, dst, table, sem):
            gather(gp, dst, table, nowhere[0:P, :], table.shape[0] - 1, sem)

        SL = 5
        SI = NG // SL
        assert NG % SL == 0 and ND % SL == 0

        def in_order(eng, turn, groups=NG):
            with eng.Fori(0, groups // SL) as i:
                for b in range(SL):
                    turn(i, b, SL * i + b)

        def staggered(eng, step, most, groups=NG, size=SL):
            def run(i, t, turn=None):
                def late(k):
                    c, b = divmod(t - k, size)
                    if turn is None or 0 <= size * (turn + c) + b < groups:
                        yield i + c, b, size * (i + c) + b
                step(late)

            whole = groups // size
            peeled = min(whole, -(-most // size))
            for turn in range(peeled):
                for t in range(size):
                    run(turn, t, turn)
            if whole > peeled:
                with eng.Fori(peeled, whole) as i:
                    for t in range(size):
                        run(i, t)
            for t in range(most):
                run(whole, t, whole)

        def reused(n):
            return n - SL + 1 + C

        def tiles(n):
            return bass.ds(TG * n, TG)

        def stage_indices(gp, cur, which, s, n, k=1):
            gp.tensor_copy(cur, idx[0:P, which, tiles(n)]).then_inc(s.cur, 1)
            gp.wait_ge(s.cur, k * (n + 1) + C)
            gp.sem_inc(s.order, 1)

        def ln_stats(v, x, ln, s, k):
            for t in range(TG):
                last = v.bn_stats(ln.st[0:P, t, :], x[0:P, t, :])
            last.then_inc(s.st, 1)
            v.wait_ge(s.st, k + 1 + C)
            v.sem_inc(s.hold, 1)
            for t in range(TG):
                last = v.bn_aggr(ln.mv[0:P, t, :], ln.st[0:P, t, :])
            last.then_inc(s.mv, 1)
            v.wait_ge(s.mv, k + 1 + C)
            v.tensor_scalar(ln.var[0:P, :], ln.mv[0:P, :, 1], EPS, None, ALU.add).then_inc(s.var, 1)

        def ln_power(gp, ln, s, k):
            gp.wait_ge(s.var, k + 1 + C)
            gp.sem_inc(s.order, 1)
            gp.tensor_tensor(ln.rstd[0:P, :], ln.var[0:P, :], neghalf[0:P, :], ALU.pow).then_inc(s.rstd, 1)

        def ln_apply(v, x, ln, scale, xn, done):
            for t in range(TG):
                last = v.tensor_scalar(xn[0:P, t, :], x[0:P, t, :], ln.mv[0:P, t, 0:1], scale[0:P, t:t + 1],
                                       ALU.subtract, ALU.mult)
            last.then_inc(done, 1)

        TV = TG // 2

        def ln_apply_first(v, x, ln, xn, done, shifted):
            v.scalar_tensor_tensor(ln.shift[0:P, TV:TG], ln.mv[0:P, TV:TG, 0], -1.0, ln.rstd[0:P, TV:TG],
                                   ALU.mult, ALU.mult).then_inc(shifted, 1)
            for t in range(TV):
                last = v.tensor_scalar(xn[0:P, t, :], x[0:P, t, :], ln.mv[0:P, t, 0:1], ln.rstd[0:P, t:t + 1],
                                       ALU.subtract, ALU.mult)
            last.then_inc(done, 1)

        def ln_apply_rest(act, x, ln, xn, done):
            for t in range(TV, TG):
                last = act.activation(xn[0:P, t, :], x[0:P, t, :], ACT.Identity, bias=ln.shift[0:P, t:t + 1],
                                      scale=ln.rstd[0:P, t:t + 1])
            last.then_inc(done, 1)

        def ln_buffers(ctx, name, n):
            st = sb(f"{name}_st", [128, n, TG, 6], ctx=ctx)
            mv = sb(f"{name}_mv", [128, n, TG, 2], ctx=ctx)
            var = sb(f"{name}_var", [128, n, TG], ctx=ctx)
            rstd = sb(f"{name}_rstd", [128, n, TG], ctx=ctx)
            shift = sb(f"{name}_shift", [128, n, TG], ctx=ctx)
            Norm = namedtuple("Norm", "st mv var rstd shift")
            return [Norm(st[:, b], mv[:, b], var[:, b], rstd[:, b], shift[:, b]) for b in range(n)]

        def transposes(pe, ps, x):
            for t in range(TG):
                last = pe.transpose(ps[:, t * P:(t + 1) * P], x[0:P, t, :], ident[0:P, 0:P])
            return last

        def rows_times(pe, ps, cols, w, start=True, stop=True):
            for t in range(TG):
                last = pe.matmul(ps[0:P, t * D:(t + 1) * D], cols[:, t * P:(t + 1) * P], w, start=start,
                                 stop=start or (stop and t == TG - 1))
            return last

        def bias_rows(pe, ps, which):
            pe.matmul(ps[0:P, :], ones3[:, 0:P], bias_parts[:, which, :], start=True, stop=False)

        def flat(x):
            return x.rearrange("p t d -> p (t d)")

        def bank(b):
            return psum[:, b, :]

        with phase() as ctx:
            L = 4
            UNITS = NJ * 2
            assert UNITS // L == NG
            xr = sb("f_x", [128, L, TG, D], ctx=ctx)
            ln = ln_buffers(ctx, "f", L)
            xn = sb("f_xn", [128, L, TG, D], ctx=ctx)
            hT = sb("f_hT", [128, L, GR], ctx=ctx)
            tab = sb("f_tab", [128, 2, GPN, FW], ctx=ctx)
            tgt = sb("f_tgt", [128, 2, GPN, H], ctx=ctx)
            xs = sb("f_xs", [128, TG, D], ctx=ctx)
            cur_src = sb("f_cur_src", [128, TG], i32, ctx=ctx)
            cur_map = sb("f_cur_map", [128, 2, TG], i32, ctx=ctx)

            s = counters(ctx, "f", "st mv var rstd order xn tr hT mm feat score cur")
            d_x = dma_counters(ctx, "f_x_loaded", L)
            d_tab = dma_counters(ctx, "f_table_stored", 2)
            d_tgt = dma_counters(ctx, "f_targets_stored", 2)
            d_map, d_xs, d_xst = sem("f_map_written", ctx), sem("f_xsrc_gathered", ctx), sem("f_xsrc_stored", ctx)

            xv = x_in.rearrange("(h j) d -> j h d", h=H)
            tabv = feat_tab.rearrange("(j g) c -> j g c", g=GPN)
            tgtv = tgt_tab.rearrange("(j g) h -> j g h", g=GPN)
            xsv = slots(xsrc_d)
            blk = ctx.enter_context(nc.Block())

            @blk.sync
            def _(sp):
                with sp.Fori(0, NG) as i:
                    for b in range(L):
                        j, q = b // 2, b % 2
                        sp.wait_ge(s.xn, L * i + b + 1 - L + C)
                        move(sp, xr[:, b], xv[bass.ds((2 * i + j) * P, P), 4 * q:4 * q + 4, :], d_x[b])
                    sp.wait_ge(d_xs, 16 * TG * (i + 1))
                    move(sp, xs, xsv[i], d_xst, store=True)
                for b in range(2):
                    sp.wait_ge(d_tab[b], before(NG))
                    sp.wait_ge(d_tgt[b], before(NG))
                sp.wait_ge(d_xst, before(NG))

            @blk.vector
            def _(v):
                start(v, s, d_x, d_tab, d_tgt, [d_xst])

                def step(late):
                    for i, b, n in late(2):
                        v.wait_ge(s.rstd, n + 1 + C)
                        v.wait_ge(s.tr, n + 1 - L + C)
                        ln_apply(v, xr[:, b], ln[b], ln[b].rstd, xn[:, b], s.xn)
                    for i, b, n in late(0):
                        v.wait_ge(d_x[b], landed(i))
                        ln_stats(v, xr[:, b], ln[b], s, n)
                staggered(v, step, 2, UNITS, L)

            @blk.tensor
            def _(pe):
                def step(late):
                    for i, b, n in late(0):
                        pe.wait_ge(s.xn, n + 1 + C)
                        pe.wait_ge(s.hT, n - 1 + C)
                        transposes(pe, bank(b % 2), xn[:, b]).then_inc(s.tr, 1)
                    for i, b, n in late(1):
                        q = b % 2
                        pe.wait_ge(s.hT, n + 1 + C)
                        pe.wait_ge(s.score, n - 1 + C)
                        for h in range(4):
                            last = pe.matmul(psum[0:P, 2 + 2 * q + h // 2, h % 2 * 256:h % 2 * 256 + GW],
                                             hT[:, b, h * P:(h + 1) * P], w_feat[:, 4 * q + h, :],
                                             start=True, stop=True)
                        last.then_inc(s.mm, 1)
                staggered(pe, step, 1, UNITS, L)

            @blk.scalar
            def _(act):
                def step(late):
                    for i, b, n in late(0):
                        act.wait_ge(s.tr, n + 1 + C)
                        act.wait_ge(s.mm, n + 1 - L + C)
                        act.activation(hT[:, b, :], bank(b % 2)[:, 0:GR], ACT.Relu).then_inc(s.hT, 1)
                    for i, b, n in late(1):
                        j, q = b // 2, b % 2
                        if q == 0:
                            act.wait_ge(d_tab[j], before(i))
                            act.wait_ge(d_tgt[j], before(i))
                        act.wait_ge(s.mm, n + 1 + C)
                        ps = psum[0:P, 2 + 2 * q:4 + 2 * q, :].rearrange("p a (h c) -> p (a h) c", h=2)
                        act.activation(
                            tab[0:P, j, :, H:FW].rearrange("p g (h f) -> p h g f", f=F)[:, 4 * q:4 * q + 4],
                            ps[:, :, 0:D].rearrange("p h (g f) -> p h g f", f=F), ACT.Copy).then_inc(s.feat, 1)
                        act.activation(
                            tab[0:P, j, :, 4 * q:4 * q + 4].rearrange("p g h -> p h g"),
                            ps[:, :, D + H:GW], ACT.Copy).then_inc(s.feat, 1)
                        act.activation(
                            tgt[0:P, j, :, 4 * q:4 * q + 4].rearrange("p g h -> p h g"),
                            ps[:, :, D:D + H], ACT.Copy).then_inc(s.score, 1)
                        if q == 1:
                            act.wait_ge(s.feat, 2 * n + 2 + C)
                            act.wait_ge(s.score, n + 1 + C)
                            move(act, tab[:, j], tabv[bass.ds((2 * i + j) * P, P), :, :], d_tab[j], store=True)
                            move(act, tgt[:, j], tgtv[bass.ds((2 * i + j) * P, P), :, :], d_tgt[j], store=True)
                staggered(act, step, 1, UNITS, L)

            @blk.gpsimd
            def _(gp):
                def step(late):
                    for i, b, n in late(0):
                        if b == 0:
                            gp.wait_ge(d_xst, before(i))
                            gp.sem_inc(s.order, 1)
                            gp.tensor_copy(cur_src[0:P, :], idx[0:P, SRC, bass.ds(TG * i, TG)]).then_inc(s.cur, 1)
                            gp.wait_ge(s.cur, 2 * i + 1 + C)
                            gp.sem_inc(s.order, 1)
                        if b == 2:
                            gp.wait_ge(d_map, 16 * TG * i + 16)
                            gp.sem_inc(s.order, 1)
                            gp.tensor_copy(cur_map[0:P, :, :], idx[0:P, LAST:SLOT + 1, bass.ds(TG * i, TG)]).then_inc(s.cur, 1)
                            gp.wait_ge(s.cur, 2 * i + 2 + C)
                            gp.sem_inc(s.order, 1)
                        for t in range(2 * b % TG, 2 * b % TG + 2):
                            if b < 2:
                                gather(gp, xs[0:P, t, :], x_in, cur_src[0:P, t:t + 1], N - 1, d_xs)
                            else:
                                gp.indirect_dma_start(slot_of, bass.IndirectOffsetOnAxis(cur_map[0:P, 0, t:t + 1], 0),
                                                      cur_map[0:P, 1, t:t + 1], None, bounds_check=N - 1,
                                                      oob_is_err=False).then_inc(d_map, 16)
                    for i, b, n in late(1):
                        ln_power(gp, ln[b], s, n)
                count_one(gp, xs[0:P, 0, :], x_in, d_map)
                gp.wait_ge(d_map, 16)
                staggered(gp, step, 1, UNITS, L)
                gp.wait_ge(d_map, 16 * TG * NG + 16)

        CHAIN = 6

        def row_chain(ctx, prefix, src, groups, banks, first=0, dst=None, taps=None):
            NORMS, LAYERS = range(3), range(2 if taps else 3)
            W = SL if taps else 1
            xin = sb(prefix + "_xin", [128, SL, TG, D], ctx=ctx)
            res = sb(prefix + "_res", [128, SL, TG, D], ctx=ctx)
            xn = sb(prefix + "_xn", [128, W, len(NORMS), TG, D], ctx=ctx)
            hT = sb(prefix + "_hT", [128, len(LAYERS), GR], ctx=ctx)
            uT = sb(prefix + "_uT", [128, 4, GR], ctx=ctx)
            hid = sb(prefix + "_hid", [128, SL, TG, D], ctx=ctx) if taps else None
            ln = [ln_buffers(ctx, f"{prefix}{k}", SL) for k in NORMS]
            s = [counters(ctx, f"{prefix}{k}", "st mv var rstd order shift xn xa tr hT u uT leaky rows res") for k in NORMS]
            s_htr, s_hid = sem(prefix + "_hidden_transposed", ctx), sem(prefix + "_hidden", ctx)
            d_x = dma_counters(ctx, prefix + "_x_loaded", SL)
            d_out = dma_counters(ctx, prefix + "_out_stored", SL)
            d_xn = [dma_counters(ctx, f"{prefix}_xn{k}_stored", SL if taps else 0) for k in NORMS]
            d_hid = dma_counters(ctx, prefix + "_hid_stored", SL if taps else 0)
            W_COL = ((w1[:, :],), (wu1[:, 0, :],), (w31[:, 0:D], w31[:, D:2 * D]))
            W_ROW = ((w2g[:, :],), (wu2[:, :],), (w32[:, 0, :], w32[:, 1, :]))
            BIAS = (BIAS_OUT1, BIAS_U2, BIAS_32)
            FUNC = ((ACT.Identity, b1_col), (ACT.Silu, bu1_col), (ACT.Relu, b31_col))
            TR, COL, ROW, HID = banks

            def rows_in(k, b):
                return xin[:, b] if k == 0 else res[:, b]

            def load(sp, i, b, n):
                sp.wait_ge(s[0].res, reused(n))
                move(sp, xin[:, b], src[n + first], d_x[b])

            def tap_stores(sp, late):
                for k in NORMS:
                    for i, b, n in late(2 * k + 2):
                        sp.wait_ge(s[k].xn, n + 1 + C)
                        sp.wait_ge(s[k].xa, n + 1 + C)
                        move(sp, xn[:, b, k], taps[k][n], d_xn[k][b], store=True)
                for i, b, n in late(2):
                    sp.wait_ge(s_hid, n + 1 + C)
                    move(sp, hid[:, b], taps[3][n], d_hid[b], store=True)

            def stored(sp):
                for b in range(SL):
                    for one in ([d_xn[0][b], d_xn[1][b], d_xn[2][b], d_hid[b]] if taps else [d_out[b]]):
                        sp.wait_ge(one, before(groups // SL))

            def begin(v):
                for k in NORMS:
                    start(v, s[k], d_xn[k])
                start(v, [s_htr, s_hid], d_x, d_out, d_hid)

            def norms(v, late):
                for k in NORMS:
                    for i, b, n in late(2 * k + 1):
                        v.wait_ge(s[k].rstd, n + 1 + C)
                        if taps:
                            v.wait_ge(d_xn[k][b], before(i))
                        if k in LAYERS:
                            v.wait_ge(s[k].tr, n + C)
                        ln_apply_first(v, rows_in(k, b), ln[k][b], xn[:, b % W, k], s[k].xn, s[k].shift)
                for i, b, n in late(0):
                    v.wait_ge(d_x[b], landed(i))
                    ln_stats(v, xin[:, b], ln[0][b], s[0], n)

            def residuals(v, late):
                for k in LAYERS:
                    for i, b, n in late(2 * k + 2):
                        v.wait_ge(s[k].rows, n + 1 + C)
                        if k == 0 and taps:
                            v.wait_ge(s[2].xa, reused(n))
                        elif k == 0:
                            v.wait_ge(d_out[b], before(i))
                        v.tensor_tensor(flat(res[0:P, b]), flat(rows_in(k, b)[0:P]), bank(ROW[k])[0:P],
                                        ALU.add).then_inc(s[k].res, 1)
                        if k + 1 < len(NORMS):
                            v.wait_ge(s[k].res, n + 1 + C)
                            ln_stats(v, res[:, b], ln[k + 1][b], s[k + 1], n)

            def leaky(v, late):
                for i, b, n in late(1):
                    v.wait_ge(s[0].uT, n + 1 + C)
                    v.scalar_tensor_tensor(uT[:, 0, :], uT[:, 0, :], 0.2, uT[:, 0, :], ALU.mult, ALU.max).then_inc(s[0].leaky, 1)

            def powers(gp, late, which=NORMS):
                for k in which:
                    for i, b, n in late(2 * k):
                        ln_power(gp, ln[k][b], s[k], n)

            def free(pe, late, uses, banks, me, counter):
                for u, (k, half, per_group) in enumerate(uses):
                    if banks[u] == banks[me]:
                        for i, b, n in late(2 * k + (1 if u < me else 2)):
                            pe.wait_ge(counter[k], per_group * n + half + 1 + C)

            TR_USES = [(k, 0, 1) for k in LAYERS]
            COL_USES = [(k, half, len(W_COL[k])) for k in LAYERS for half in range(len(W_COL[k]))]

            def products(pe, late):
                for k in LAYERS:
                    for i, b, n in late(2 * k + 1):
                        pe.wait_ge(s[k].xn, n + 1 + C)
                        pe.wait_ge(s[k].xa, n + 1 + C)
                        free(pe, late, TR_USES, TR, k, [one.hT for one in s])
                        transposes(pe, bank(TR[k]), xn[:, b % W, k]).then_inc(s[k].tr, 1)
                for u, (k, half, per_group) in enumerate(COL_USES):
                    for i, b, n in late(2 * k + 1):
                        pe.wait_ge(s[k].hT, n + 1 + C)
                        free(pe, late, COL_USES, COL, u, [one.uT for one in s])
                        pe.matmul(bank(COL[u])[:, 0:GR], W_COL[k][half], hT[:, k, :], start=True, stop=True).then_inc(s[k].u, 1)
                for k in LAYERS:
                    for i, b, n in late(2 * k + 1):
                        pe.wait_ge(s[k].uT, len(W_COL[k]) * (n + 1) + C)
                        if k == 0:
                            pe.wait_ge(s[0].leaky, n + 1 + C)
                        pe.wait_ge(s[k].res, n + C)
                        bias_rows(pe, bank(ROW[k]), BIAS[k])
                        for half, w in enumerate(W_ROW[k]):
                            last = rows_times(pe, bank(ROW[k]), uT[:, k + half], w, start=False,
                                              stop=half == len(W_ROW[k]) - 1)
                        last.then_inc(s[k].rows, 1)
                        if taps and k == 0:
                            pe.wait_ge(s_hid, n + C)
                            for t in range(TG):
                                last = pe.transpose(bank(HID)[0:P, t * D:(t + 1) * D], uT[:, 0, t * P:(t + 1) * P], ident[:, :])
                            last.then_inc(s_htr, 1)

            def evacuations(act, late):
                for k in LAYERS:
                    for i, b, n in late(2 * k + 1):
                        act.wait_ge(s[k].tr, n + 1 + C)
                        act.activation(hT[:, k, :], bank(TR[k])[:, 0:GR], ACT.Relu).then_inc(s[k].hT, 1)
                for u, (k, half, per_group) in enumerate(COL_USES):
                    for i, b, n in late(2 * k + 1):
                        f, bias = FUNC[k]
                        act.wait_ge(s[k].u, per_group * n + half + 1 + C)
                        act.activation(uT[:, k + half, :], bank(COL[u])[:, 0:GR], f, bias=bias[:, half:half + 1]).then_inc(s[k].uT, 1)
                for i, b, n in late(CHAIN if dst is not None else 1):
                    if taps:
                        act.wait_ge(s_htr, n + 1 + C)
                        act.wait_ge(d_hid[b], before(i))
                        act.activation(flat(hid[0:P, b]), bank(HID)[0:P], ACT.Copy).then_inc(s_hid, 1)
                    else:
                        act.wait_ge(s[2].res, n + 1 + C)
                        move(act, res[:, b], dst[n + first], d_out[b], store=True)

            def norms_rest(act, late):
                for k in NORMS:
                    for i, b, n in late(2 * k):
                        act.wait_ge(s[k].shift, n + 1 + C)
                        ln_apply_rest(act, rows_in(k, b), ln[k][b], xn[:, b % W, k], s[k].xa)

            Chain = namedtuple("Chain", "load tap_stores stored begin norms residuals leaky powers products evacuations norms_rest")
            return Chain(load, tap_stores, stored, begin, norms, residuals, leaky, powers, products, evacuations, norms_rest)

        WITH_ATTENTION, ALONE = 0, NG

        with phase() as ctx:
            cur = sb("e_cur", [128, SL, 2, TG], i32, ctx=ctx)
            got = sb("e_got", [128, SL, 2, TG], i32, ctx=ctx)
            s = counters(ctx, "e", "cur order got")
            d_got = dma_counters(ctx, "e_slots_read", SL)
            chain = row_chain(ctx, "e", slots(xsrc_d), NG, banks=((0, 1), (2, 3), (4, 5), 6),
                              taps=[slots(xn0_src), slots(xn2_src), slots(xn3_src), slots(hid_src)])
            blk = ctx.enter_context(nc.Block())

            @blk.sync
            def _(sp):
                def step(late):
                    for i, b, n in late(0):
                        chain.load(sp, i, b, n)
                    chain.tap_stores(sp, late)
                staggered(sp, step, CHAIN)
                chain.stored(sp)

            @blk.vector
            def _(v):
                start(v, s)
                chain.begin(v)

                def step(late):
                    chain.norms(v, late)
                    chain.residuals(v, late)
                    chain.leaky(v, late)
                staggered(v, step, CHAIN)

            @blk.gpsimd
            def _(gp):
                def step(late):
                    for i, b, n in late(0):
                        gp.wait_ge(s.got, reused(n))
                        gp.sem_inc(s.order, 1)
                        stage_indices(gp, cur[0:P, b], slice(SRC, DST + 1), s, n)
                        for end in range(2):
                            for t in range(TG):
                                gather(gp, got[0:P, b, end, t:t + 1], slot_of, cur[0:P, b, end, t:t + 1], N - 1, d_got[b])
                    chain.powers(gp, late)
                    for i, b, n in late(1):
                        gp.wait_ge(d_got[b], 16 * 2 * TG * (i + 1))
                        gp.sem_inc(s.order, 1)
                        gp.tensor_copy(idx[0:P, SRC_SLOT:DST_SLOT + 1, tiles(n)], got[0:P, b]).then_inc(s.got, 1)
                staggered(gp, step, CHAIN)

            @blk.tensor
            def _(pe):
                staggered(pe, lambda late: chain.products(pe, late), CHAIN)

            @blk.scalar
            def _(act):
                def step(late):
                    chain.evacuations(act, late)
                    chain.norms_rest(act, late)
                staggered(act, step, CHAIN)

        with phase() as ctx:
            groups = ND - ALONE
            chain = row_chain(ctx, "n", rows(x_in), groups, banks=((0, 1, 7), (2, 3, 2, 3), (4, 5, 6), None),
                              first=ALONE, dst=rows(out))
            blk = ctx.enter_context(nc.Block())

            @blk.sync
            def _(sp):
                in_order(sp, lambda i, b, n: chain.load(sp, i, b, n), groups)
                chain.stored(sp)

            @blk.vector
            def _(v):
                chain.begin(v)

                def step(late):
                    chain.norms(v, late)
                    chain.residuals(v, late)
                    chain.leaky(v, late)
                staggered(v, step, CHAIN, groups)

            @blk.gpsimd
            def _(gp):
                staggered(gp, lambda late: chain.powers(gp, late), CHAIN, groups)

            @blk.tensor
            def _(pe):
                staggered(pe, lambda late: chain.products(pe, late), CHAIN, groups)

            @blk.scalar
            def _(act):
                def step(late):
                    chain.evacuations(act, late)
                    chain.norms_rest(act, late)
                staggered(act, step, CHAIN, groups)

        def select(v, which, out, n):
            return v.tensor_tensor(out[0:P].rearrange("p (t q) -> p t q", q=P),
                                   dst_bc[0:P, bass.ds(GR * n, GR)].rearrange("p (t q) -> p t q", q=P),
                                   which[0:P, tiles(n)].unsqueeze(2).broadcast_to((P, TG, P)), ALU.is_equal)

        def run_sums(pe, ps, m, sel):
            for t in range(TG):
                last = pe.matmul(ps[:, t * P:(t + 1) * P], m[0:P, t, :], sel[0:P, t * P:(t + 1) * P],
                                 start=True, stop=True)
            return last

        def run_carry(v, ps, sums, s, b, n, tiles=range(TG)):
            for t in tiles:
                before_it = sums[:, b, t * P - 1:t * P] if t else sums[:, (b - 1) % SL, GR - 1:GR]
                v.wait_ge(s.sum, TG * n + t + 1 + C)
                v.scalar_tensor_tensor(sums[:, b, t * P:(t + 1) * P],
                                       same_bc[:, bass.ds(GR * n + t * P, P)], before_it,
                                       ps[:, t * P:(t + 1) * P], ALU.mult, ALU.add).then_inc(s.sum, 1)

        with phase() as ctx:
            fs = sb("a_fs", [128, SL, TG, FW], ctx=ctx)
            fd = sb("a_fd", [128, SL, TG, H], ctx=ctx)
            xd = sb("a_xd", [128, SL, TG, D], ctx=ctx)
            cur = sb("a_cur", [128, SL, 2, TG], i32, ctx=ctx)
            z = sb("a_z", [128, SL, TG, H], ctx=ctx)
            zn = sb("a_zn", [128, SL, TG, H], ctx=ctx)
            ez = sb("a_ez", [128, SL, TG, H], ctx=ctx)
            msg = sb("a_msg", [128, SL, TG, MW], ctx=ctx)
            sel = sb("a_sel", [128, GR], ctx=ctx)
            selc = sb("a_selc", [128, GR], ctx=ctx)
            tot = sb("a_tot", [128, SL, TG, MW], ctx=ctx)
            rw = sb("a_rw", [128, SL, TG, H], ctx=ctx)
            agg = sb("a_agg", [128, SL, TG, D], ctx=ctx)
            deg = sb("a_deg", [128, SL, TG], ctx=ctx)
            dv = sb("a_dv", [128, SL, TG], ctx=ctx)
            sc = sb("a_sc", [128, SL, TG], ctx=ctx)
            ln = ln_buffers(ctx, "a", SL)
            s = counters(ctx, "a", "cur order z zn ez el w msg ones sel selc tot1 totc rw agg x1 deg dv dvs dvl st mv var rstd sc g1n g1")
            d_fs = dma_counters(ctx, "a_fs", SL)
            d_fd = dma_counters(ctx, "a_fd", SL)
            d_xd = dma_counters(ctx, "a_xd", SL)
            d_x1 = dma_counters(ctx, "a_x1_stored", SL)
            d_g1 = dma_counters(ctx, "a_g1_stored", SL)
            x1v, t1v = slots(x1_dst), slots(tab1)
            chain = row_chain(ctx, "o", rows(x_in), NG, banks=((2, 2, 2), (3, 4, 3, 4), (5, 6, 7), None),
                              first=WITH_ATTENTION, dst=rows(out))
            blk = ctx.enter_context(nc.Block())

            @blk.gpsimd
            def _(gp):
                def step(late):
                    for i, b, n in late(0):
                        gp.wait_ge(s.msg, reused(n))
                        gp.sem_inc(s.order, 1)
                        gp.wait_ge(d_xd[b], 16 * TG * i + 16)
                        gp.sem_inc(s.order, 1)
                        stage_indices(gp, cur[0:P, b], slice(SRC, DST + 1), s, n)
                        for t in range(TG):
                            gather(gp, fs[0:P, b, t, :], feat_tab, cur[0:P, b, 0, t:t + 1], N - 1, d_fs[b])
                        for t in range(TG):
                            gather(gp, fd[0:P, b, t, :], tgt_tab, cur[0:P, b, 1, t:t + 1], N - 1, d_fd[b])
                        gp.wait_ge(d_x1[b], before(i))
                        gp.sem_inc(s.order, 1)
                        gp.wait_ge(s.g1n, reused(n))
                        gp.sem_inc(s.order, 1)
                        for t in range(TG):
                            gather(gp, xd[0:P, b, t, :], x_in, cur[0:P, b, 1, t:t + 1], N - 1, d_xd[b])
                    chain.powers(gp, late, [0])
                    for i, b, n in late(3):
                        gp.wait_ge(s.deg, n + 1 + C)
                        gp.sem_inc(s.order, 1)
                        gp.tensor_tensor(dv[0:P, b], deg[0:P, b], neghalf[0:P, :], ALU.pow).then_inc(s.dv, 1)
                        ln_power(gp, ln[b], s, n)
                    chain.powers(gp, late, [1, 2])
                for b in range(SL):
                    count_one(gp, xd[0:P, b, 0, :], x_in, d_xd[b])
                    gp.wait_ge(d_xd[b], 16)
                staggered(gp, step, CHAIN)

            @blk.vector
            def _(v):
                start(v, s)
                for one in (*d_x1, *d_g1):
                    v.sem_inc(one, DONE)
                v.memset(msg[:, :, :, D + H:MW], 1.0).then_inc(s.ones, 1)
                v.memset(tot[:, :, :, :], 0.0).then_inc(s.ones, 1)
                v.wait_ge(s.ones, 2 + C)
                chain.begin(v)

                def step(late):
                    chain.norms(v, late)
                    chain.residuals(v, late)
                    for i, b, n in late(4):
                        v.wait_ge(s.dv, n + 1 + C)
                        v.tensor_copy(dinv[0:P, tiles(n)], dv[0:P, b]).then_inc(s.dvs, 1)
                        v.tensor_tensor(deg[0:P, b], dv[0:P, b], islast[0:P, tiles(n)], ALU.mult).then_inc(s.dvl, 1)
                        v.wait_ge(s.dvl, n + 1 + C)
                        v.tensor_copy(dinv_last[0:P, tiles(n)], deg[0:P, b]).then_inc(s.dvs, 1)
                        v.wait_ge(s.rstd, n + 1 + C)
                        v.tensor_tensor(sc[0:P, b], ln[b].rstd[0:P], deg[0:P, b], ALU.mult).then_inc(s.sc, 1)
                        v.wait_ge(s.sc, n + 1 + C)
                        ln_apply(v, xd[:, b], ln[b], sc[:, b], agg[:, b], s.g1n)
                    for i, b, n in late(0):
                        v.wait_ge(s.tot1, TG * n + C)
                        select(v, dst_f, sel, n).then_inc(s.sel, 1)
                        select(v, carry_f, selc, n).then_inc(s.selc, 1)
                        v.wait_ge(d_fs[b], 16 * TG * (i + 1))
                        v.wait_ge(d_fd[b], 16 * TG * (i + 1))
                        v.tensor_tensor(z[0:P, b], fs[0:P, b, :, 0:H], fd[0:P, b], ALU.add).then_inc(s.z, 1)
                        v.wait_ge(s.z, n + 1 + C)
                        v.tensor_scalar(zn[0:P, b], z[0:P, b], 0.0, None, ALU.min).then_inc(s.zn, 1)
                    chain.leaky(v, late)
                    for i, b, n in late(1):
                        v.wait_ge(s.totc, TG * (n + 1) + C)
                        v.reciprocal(rw[0:P, b], tot[0:P, b, :, D:D + H]).then_inc(s.rw, 1)
                        v.tensor_scalar(deg[0:P, b], tot[0:P, b, :, D + H], 1.0, 1.0, ALU.add, ALU.max).then_inc(s.deg, 1)
                        v.wait_ge(s.rw, n + 1 + C)
                        v.wait_ge(d_g1[b], before(i))
                        v.tensor_tensor(agg[0:P, b].rearrange("p t (h f) -> p t h f", f=F),
                                        tot[0:P, b, :, 0:D].rearrange("p t (h f) -> p t h f", f=F),
                                        rw[0:P, b].unsqueeze(3).broadcast_to((P, TG, H, F)), ALU.mult).then_inc(s.agg, 1)
                    for i, b, n in late(0):
                        v.wait_ge(s.ez, n + 1 + C)
                        v.tensor_scalar(ez[0:P, b], ez[0:P, b], 1.0, 0.2, ALU.subtract, ALU.mult).then_inc(s.el, 1)
                        v.wait_ge(s.el, 2 * n + 1 + C)
                        v.scalar_tensor_tensor(z[0:P, b], z[0:P, b], 0.0, ez[0:P, b], ALU.max, ALU.add).then_inc(s.el, 1)
                    for i, b, n in late(1):
                        v.wait_ge(s.agg, n + 1 + C)
                        v.wait_ge(d_xd[b], 16 * TG * (i + 1) + 16)
                        v.tensor_tensor(flat(xd[0:P, b]), flat(xd[0:P, b]), flat(agg[0:P, b]), ALU.add).then_inc(s.x1, 1)
                    for i, b, n in late(0):
                        v.wait_ge(s.w, n + 1 + C)
                        v.tensor_tensor(msg[0:P, b, :, 0:D].rearrange("p t (h f) -> p t h f", f=F),
                                        fs[0:P, b, :, H:FW].rearrange("p t (h f) -> p t h f", f=F),
                                        msg[0:P, b, :, D:D + H].unsqueeze(3).broadcast_to((P, TG, H, F)), ALU.mult).then_inc(s.msg, 1)
                    for i, b, n in late(1):
                        v.wait_ge(s.x1, n + 1 + C)
                        ln_stats(v, xd[:, b], ln[b], s, n)
                staggered(v, step, CHAIN)

            @blk.scalar
            def _(act):
                def step(late):
                    chain.evacuations(act, late)
                    for i, b, n in late(0):
                        act.wait_ge(s.zn, n + 1 + C)
                        act.activation(ez[0:P, b], zn[0:P, b], ACT.Exp).then_inc(s.ez, 1)
                    for i, b, n in late(4):
                        act.wait_ge(s.g1n, n + 1 + C)
                        act.activation(flat(agg[0:P, b]), flat(agg[0:P, b]), ACT.Relu).then_inc(s.g1, 1)
                    for i, b, n in late(0):
                        act.wait_ge(s.el, 2 * n + 2 + C)
                        act.activation(msg[0:P, b, :, D:D + H], z[0:P, b], ACT.Exp).then_inc(s.w, 1)
                        for t in range(TG):
                            act.wait_ge(s.tot1, TG * n + t + 1 + C)
                            act.activation(tot[0:P, b, t, :], bank(t % 2)[0:P, 0:MW], ACT.Copy).then_inc(s.totc, 1)
                    chain.norms_rest(act, late)
                staggered(act, step, CHAIN)

            @blk.tensor
            def _(pe):
                def step(late):
                    chain.products(pe, late)
                    for i, b, n in late(0):
                        pe.wait_ge(s.sel, n + 1 + C)
                        pe.wait_ge(s.selc, n + 1 + C)
                        pe.wait_ge(s.msg, n + 1 + C)
                        for t in range(TG):
                            ps = bank(t % 2)[0:P, 0:MW]
                            pe.wait_ge(s.totc, TG * n + t - 1 + C)
                            pe.matmul(ps, sel[0:P, t * P:(t + 1) * P], msg[0:P, b, t, :], start=True, stop=False)
                            pe.wait_ge(s.totc, TG * n + t + C)
                            prev = tot[0:P, b, t - 1, :] if t else tot[0:P, (b - 1) % SL, TG - 1, :]
                            pe.matmul(ps, selc[0:P, t * P:(t + 1) * P], prev, start=False, stop=True).then_inc(s.tot1, 1)
                staggered(pe, step, CHAIN)

            @blk.sync
            def _(sp):
                def step(late):
                    for i, b, n in late(0):
                        chain.load(sp, i, b, n)
                    for i, b, n in late(2):
                        sp.wait_ge(s.x1, n + 1 + C)
                        move(sp, xd[:, b], x1v[n], d_x1[b], store=True)
                    for i, b, n in late(4):
                        sp.wait_ge(s.g1, n + 1 + C)
                        move(sp, agg[:, b], t1v[n], d_g1[b], store=True)
                staggered(sp, step, 4)
                chain.stored(sp)
                for b in range(SL):
                    sp.wait_ge(d_x1[b], before(SI))
                    sp.wait_ge(d_g1[b], before(SI))

        def convolution(prefix, first, nb_view, self_view, over_tab, x_view, out_views):
            with phase() as ctx:
                hs = sb(prefix + "_hs", [128, SL, TG, D], ctx=ctx)
                gd = sb(prefix + "_gd", [128, SL, TG, D], ctx=ctx)
                xd = None if first else sb(prefix + "_xd", [128, SL, TG, D], ctx=ctx)
                m = sb(prefix + "_m", [128, SL, TG, D], ctx=ctx)
                sel = sb(prefix + "_sel", [128, SL, GR], ctx=ctx)
                sums = sb(prefix + "_sums", [128, SL, GR], ctx=ctx)
                cur = sb(prefix + "_cur", [128, SL, TG], i32, ctx=ctx)
                u = sb(prefix + "_u", [128, SL, TG, D], ctx=ctx)
                o = sb(prefix + "_o", [128, SL, TG, D], ctx=ctx)
                dl = sb(prefix + "_dl", [128, SL, TG], ctx=ctx)
                ln = ln_buffers(ctx, prefix, SL)
                s = counters(ctx, prefix, "cur order sel m ps sum rows u dl leaky o st mv var rstd x")
                d_hs = dma_counters(ctx, prefix + "_hs", SL)
                d_gd = dma_counters(ctx, prefix + "_gd", SL)
                d_xd = dma_counters(ctx, prefix + "_xd", SL)
                d_ov = dma_counters(ctx, prefix + "_ov", SL)
                d_o = dma_counters(ctx, prefix + "_o", SL)
                d_u = dma_counters(ctx, prefix + "_u", SL)
                PS_OUT = SL
                blk = ctx.enter_context(nc.Block())

                @blk.sync
                def _(sp):
                    def turn(i, b, n):
                        sp.wait_ge(s.m, reused(n))
                        move(sp, hs[:, b], nb_view[n], d_hs[b])
                        move(sp, gd[:, b], self_view[n], d_gd[b])
                        if not first:
                            sp.wait_ge(s.u, TG * (n - SL + 1) + C)
                            move(sp, xd[:, b], x_view[n], d_xd[b])
                    in_order(sp, turn)

                @blk.gpsimd
                def _(gp):
                    def step(late):
                        for i, b, n in late(0):
                            gp.wait_ge(d_hs[b], landed(i))
                            gp.sem_inc(s.order, 1)
                            stage_indices(gp, cur[0:P, b], SRC_SLOT, s, n)
                            for t in range(TG):
                                gather(gp, hs[0:P, b, t, :], over_tab, cur[0:P, b, t:t + 1], E - 1, d_ov[b])
                        if not first:
                            for i, b, n in late(5):
                                ln_power(gp, ln[b], s, n)
                    staggered(gp, step, 3 if first else 5)

                @blk.vector
                def _(v):
                    start(v, s, d_hs, d_gd, d_xd, d_o, d_u)
                    v.memset(sums[:, :, :], 0.0).then_inc(s.sum, 1)
                    v.wait_ge(s.sum, 1 + C)

                    def step(late):
                        for i, b, n in late(0):
                            v.wait_ge(s.ps, reused(n))
                            select(v, dst_f, sel[:, b], n).then_inc(s.sel, 1)
                            v.wait_ge(d_hs[b], landed(i))
                            v.wait_ge(d_gd[b], landed(i))
                            v.wait_ge(d_ov[b], 16 * TG * (i + 1))
                            v.scalar_tensor_tensor(flat(m[0:P, b]), flat(hs[0:P, b]), 0.0 if first else 1.0,
                                                   flat(gd[0:P, b]), ALU.max if first else ALU.mult,
                                                   ALU.add).then_inc(s.m, 1)
                        for i, b, n in late(3):
                            v.wait_ge(s.rows, n + 1 + C)
                            if first:
                                v.wait_ge(s.o, reused(n))
                                v.tensor_copy(dl[0:P, b], dinv_last[0:P, tiles(n)]).then_inc(s.dl, 1)
                            else:
                                v.wait_ge(d_xd[b], landed(i))
                                v.wait_ge(d_u[b], before(i))
                        for i, b, n in late(1):
                            v.wait_ge(s.ps, n + 1 + C)
                        for t in range(TG):
                            for i, b, n in late(1):
                                run_carry(v, bank(b), sums, s, b, n, [t])
                            for i, b, n in late(3):
                                v.scalar_tensor_tensor(u[0:P, b, t, :], bank(PS_OUT)[0:P, t * D:(t + 1) * D],
                                                       dinv[0:P, bass.ds(TG * n + t, 1)],
                                                       b1_bc[0:P, :] if first else xd[0:P, b, t, :],
                                                       ALU.mult, ALU.add).then_inc(s.u, 1)
                        for i, b, n in late(3):
                            v.wait_ge(s.u, TG * (n + 1) + C)
                            if first:
                                v.scalar_tensor_tensor(flat(u[0:P, b]), flat(u[0:P, b]), 0.2, flat(u[0:P, b]),
                                                       ALU.mult, ALU.max).then_inc(s.leaky, 1)
                            else:
                                v.tensor_tensor(u[0:P, b], u[0:P, b], out1_bc[0:P, :].unsqueeze(1).broadcast_to((P, TG, D)),
                                                ALU.add).then_inc(s.x, 1)
                                v.wait_ge(s.x, n + 1 + C)
                                ln_stats(v, u[:, b], ln[b], s, n)
                        if not first:
                            for i, b, n in late(6):
                                v.wait_ge(s.rstd, n + 1 + C)
                                v.wait_ge(d_o[b], before(i))
                                ln_apply(v, u[:, b], ln[b], ln[b].rstd, o[:, b], s.o)
                    staggered(v, step, 3 if first else 6)

                @blk.tensor
                def _(pe):
                    def step(late):
                        for i, b, n in late(0):
                            pe.wait_ge(s.sel, n + 1 + C)
                            pe.wait_ge(s.m, n + 1 + C)
                            pe.wait_ge(s.sum, TG * (n - SL + 1) + 1 + C)
                            run_sums(pe, bank(b), m[:, b], sel[:, b]).then_inc(s.ps, 1)
                        for i, b, n in late(2):
                            pe.wait_ge(s.sum, TG * (n + 1) + 1 + C)
                            pe.wait_ge(s.u, TG * n + C)
                            rows_times(pe, bank(PS_OUT), sums[:, b], w1[:, :] if first else w2g[:, :]).then_inc(s.rows, 1)
                    staggered(pe, step, 2)

                @blk.scalar
                def _(act):
                    def turn(i, b, n):
                        if first:
                            act.wait_ge(s.leaky, n + 1 + C)
                            act.wait_ge(s.dl, n + 1 + C)
                            act.wait_ge(d_o[b], before(i))
                            for t in range(TG):
                                last = act.activation(o[0:P, b, t, :], u[0:P, b, t, :], ACT.Copy,
                                                      scale=dl[0:P, b, t:t + 1])
                            last.then_inc(s.o, 1)
                        act.wait_ge(s.o, n + 1 + C)
                        move(act, o[:, b], out_views[0][n], d_o[b], store=True)
                        if not first:
                            move(act, u[:, b], out_views[1][n], d_u[b], store=True)
                    in_order(act, turn)
                    for b in range(SL):
                        act.wait_ge(d_o[b], before(SI))
                        if not first:
                            act.wait_ge(d_u[b], before(SI))

        def message_layer():
            with phase() as ctx:
                hs = sb("m_hs", [128, SL, TG, D], ctx=ctx)
                hd = sb("m_hd", [128, SL, TG, D], ctx=ctx)
                xd = sb("m_xd", [128, SL, TG, D], ctx=ctx)
                cur = sb("m_cur", [128, SL, 2, TG], i32, ctx=ctx)
                sT = sb("m_sT", [128, SL, GR], ctx=ctx)
                dT = sb("m_dT", [128, SL, GR], ctx=ctx)
                vT = sb("m_vT", [128, SL, GR], ctx=ctx)
                m = sb("m_m", [128, SL, TG, D], ctx=ctx)
                sel = sb("m_sel", [128, SL, GR], ctx=ctx)
                sums = sb("m_sums", [128, SL, GR], ctx=ctx)
                sc = sb("m_sc", [128, SL, TG], ctx=ctx)
                ln = ln_buffers(ctx, "m", SL)
                s = counters(ctx, "m", "cur order trs sT trd dT u v rows m sel ps sum u2 w rows2 x st mv var rstd sc gn g")
                d_hs = dma_counters(ctx, "m_hs", SL)
                d_xd = dma_counters(ctx, "m_xd", SL)
                d_ov = dma_counters(ctx, "m_ov", SL)
                d_hd = dma_counters(ctx, "m_hd", SL)
                d_x3 = dma_counters(ctx, "m_x3", SL)
                d_g = dma_counters(ctx, "m_g", SL)
                hsv, xdv, x3v, t4v = slots(xn2_src), slots(x2_dst), slots(x3_dst), slots(tab4)
                PS_S, PS_D, PS_U, PS_MSG, PS_SUM, PS_U2, PS_UPD = range(7)
                blk = ctx.enter_context(nc.Block())

                @blk.sync
                def _(sp):
                    def step(late):
                        for i, b, n in late(0):
                            sp.wait_ge(s.trs, reused(n))
                            move(sp, hs[:, b], hsv[n], d_hs[b])
                        for i, b, n in late(2):
                            sp.wait_ge(d_x3[b], before(i))
                            move(sp, xd[:, b], xdv[n], d_xd[b])
                    staggered(sp, step, 2)

                @blk.gpsimd
                def _(gp):
                    def step(late):
                        for i, b, n in late(0):
                            gp.wait_ge(d_hs[b], landed(i))
                            gp.sem_inc(s.order, 1)
                            gp.wait_ge(s.trd, reused(n))
                            gp.sem_inc(s.order, 1)
                            stage_indices(gp, cur[0:P, b], slice(SRC_SLOT, DST_SLOT + 1), s, n)
                            for t in range(TG):
                                gather(gp, hs[0:P, b, t, :], tab3, cur[0:P, b, 0, t:t + 1], E - 1, d_ov[b])
                            for t in range(TG):
                                gather(gp, hd[0:P, b, t, :], tab3, cur[0:P, b, 1, t:t + 1], E - 1, d_hd[b])
                        for i, b, n in late(4):
                            ln_power(gp, ln[b], s, n)
                    staggered(gp, step, 4)

                @blk.vector
                def _(v):
                    start(v, s, d_hs, d_xd, d_x3, d_g)
                    v.memset(sums[:, :, :], 0.0).then_inc(s.sum, 1)
                    v.wait_ge(s.sum, 1 + C)

                    def step(late):
                        for i, b, n in late(5):
                            v.wait_ge(s.rstd, n + 1 + C)
                            v.tensor_tensor(sc[0:P, b], ln[b].rstd[0:P], islast[0:P, tiles(n)], ALU.mult).then_inc(s.sc, 1)
                            v.wait_ge(s.sc, n + 1 + C)
                            ln_apply(v, xd[:, b], ln[b], sc[:, b], m[:, b], s.gn)
                        for i, b, n in late(0):
                            v.wait_ge(s.ps, reused(n))
                            select(v, dst_f, sel[:, b], n).then_inc(s.sel, 1)
                        for i, b, n in late(1):
                            v.wait_ge(s.rows, n + 1 + C)
                            v.wait_ge(d_g[b], before(i))
                            v.tensor_copy(flat(m[0:P, b]), bank(PS_MSG)[0:P]).then_inc(s.m, 1)
                        for i, b, n in late(2):
                            v.wait_ge(s.rows2, n + 1 + C)
                            v.wait_ge(d_xd[b], landed(i))
                            v.tensor_tensor(flat(xd[0:P, b]), flat(xd[0:P, b]), bank(PS_UPD)[0:P], ALU.add).then_inc(s.x, 1)
                        for i, b, n in late(1):
                            v.wait_ge(s.ps, n + 1 + C)
                            run_carry(v, bank(PS_SUM), sums, s, b, n)
                        for i, b, n in late(2):
                            v.wait_ge(s.x, n + 1 + C)
                            ln_stats(v, xd[:, b], ln[b], s, n)
                    staggered(v, step, 5)

                @blk.tensor
                def _(pe):
                    def step(late):
                        for i, b, n in late(2):
                            pe.wait_ge(s.w, n + C)
                            pe.matmul(bank(PS_U2)[:, 0:GR], wu1[:, 0, :], dT[:, b, :], start=True, stop=False)
                            pe.wait_ge(s.sum, TG * (n + 1) + 1 + C)
                            pe.matmul(bank(PS_U2)[:, 0:GR], wu1[:, 1, :], sums[:, b, :], start=False, stop=True).then_inc(s.u2, 1)
                        for i, b, n in late(1):
                            pe.wait_ge(s.v, n + 1 + C)
                            pe.wait_ge(s.m, n + C)
                            bias_rows(pe, bank(PS_MSG), BIAS_M2)
                            rows_times(pe, bank(PS_MSG), vT[:, b], wm2[:, :], start=False).then_inc(s.rows, 1)
                        for i, b, n in late(2):
                            pe.wait_ge(s.w, n + 1 + C)
                            pe.wait_ge(s.x, n + C)
                            bias_rows(pe, bank(PS_UPD), BIAS_U2)
                            rows_times(pe, bank(PS_UPD), vT[:, b], wu2[:, :], start=False).then_inc(s.rows2, 1)
                        for i, b, n in late(1):
                            pe.wait_ge(s.sel, n + 1 + C)
                            pe.wait_ge(s.m, n + 1 + C)
                            pe.wait_ge(s.sum, TG * n + 1 + C)
                            run_sums(pe, bank(PS_SUM), m[:, b], sel[:, b]).then_inc(s.ps, 1)
                        for i, b, n in late(0):
                            pe.wait_ge(d_hs[b], landed(i))
                            pe.wait_ge(d_ov[b], 16 * TG * (i + 1))
                            pe.wait_ge(s.sT, n + C)
                            transposes(pe, bank(PS_S), hs[:, b]).then_inc(s.trs, 1)
                            pe.wait_ge(d_hd[b], 16 * TG * (i + 1))
                            pe.wait_ge(s.dT, n + C)
                            transposes(pe, bank(PS_D), hd[:, b]).then_inc(s.trd, 1)
                            pe.wait_ge(s.sT, n + 1 + C)
                            pe.wait_ge(s.v, n + C)
                            pe.matmul(bank(PS_U)[:, 0:GR], wm1[:, 0, :], sT[:, b, :], start=True, stop=False)
                            pe.wait_ge(s.dT, n + 1 + C)
                            pe.matmul(bank(PS_U)[:, 0:GR], wm1[:, 1, :], dT[:, b, :], start=False, stop=True).then_inc(s.u, 1)
                    staggered(pe, step, 2)

                @blk.scalar
                def _(act):
                    def step(late):
                        for i, b, n in late(5):
                            act.wait_ge(s.gn, n + 1 + C)
                            act.activation(flat(m[0:P, b]), flat(m[0:P, b]), ACT.Relu).then_inc(s.g, 1)
                        for i, b, n in late(2):
                            act.wait_ge(s.u2, n + 1 + C)
                            act.activation(vT[:, b, :], bank(PS_U2)[:, 0:GR], ACT.Silu, bias=bu1_col[:, 0:1]).then_inc(s.w, 1)
                        for i, b, n in late(0):
                            act.wait_ge(s.trs, n + 1 + C)
                            act.activation(sT[:, b, :], bank(PS_S)[:, 0:GR], ACT.Relu).then_inc(s.sT, 1)
                            act.wait_ge(s.trd, n + 1 + C)
                            act.activation(dT[:, b, :], bank(PS_D)[:, 0:GR], ACT.Relu).then_inc(s.dT, 1)
                            act.wait_ge(s.u, n + 1 + C)
                            act.activation(vT[:, b, :], bank(PS_U)[:, 0:GR], ACT.Silu, bias=bm1_col[:, 0:1]).then_inc(s.v, 1)
                        for i, b, n in late(5):
                            act.wait_ge(s.g, n + 1 + C)
                            move(act, m[:, b], t4v[n], d_g[b], store=True)
                            move(act, xd[:, b], x3v[n], d_x3[b], store=True)
                    staggered(act, step, 5)
                    for b in range(SL):
                        act.wait_ge(d_g[b], before(SI))
                        act.wait_ge(d_x3[b], before(SI))

        def isomorphism_layer():
            with phase() as ctx:
                hs = sb("g_hs", [128, SL, TG, D], ctx=ctx)
                gd = sb("g_gd", [128, SL, TG, D], ctx=ctx)
                xd = sb("g_xd", [128, SL, TG, D], ctx=ctx)
                cur = sb("g_cur", [128, SL, TG], i32, ctx=ctx)
                at = sb("g_at", [128, SL, TG], i32, ctx=ctx)
                m = sb("g_m", [128, SL, TG, D], ctx=ctx)
                sel = sb("g_sel", [128, SL, GR], ctx=ctx)
                sums = sb("g_sums", [128, SL, GR], ctx=ctx)
                hT = sb("g_hT", [128, SL, 2, GR], ctx=ctx)
                s = counters(ctx, "g", "cur at order sel m ps sum u h rows x")
                d_hs = dma_counters(ctx, "g_hs", SL)
                d_gd = dma_counters(ctx, "g_gd", SL)
                d_xd = dma_counters(ctx, "g_xd", SL)
                d_ov = dma_counters(ctx, "g_ov", SL)
                d_out = dma_counters(ctx, "g_out", SL)
                hsv, xdv, gdv = slots(xn3_src), slots(x3_dst), slots(tab4)
                PS_SUM, PS_H, PS_OUT = 0, 2, 4
                blk = ctx.enter_context(nc.Block())

                @blk.sync
                def _(sp):
                    def turn(i, b, n):
                        sp.wait_ge(s.m, reused(n))
                        move(sp, hs[:, b], hsv[n], d_hs[b])
                        move(sp, gd[:, b], gdv[n], d_gd[b])
                        sp.wait_ge(d_out[b], 16 * TG * i + 16)
                        move(sp, xd[:, b], xdv[n], d_xd[b])
                    in_order(sp, turn)

                @blk.gpsimd
                def _(gp):
                    def step(late):
                        for i, b, n in late(0):
                            gp.wait_ge(d_hs[b], landed(i))
                            gp.sem_inc(s.order, 1)
                            stage_indices(gp, cur[0:P, b], SRC_SLOT, s, n)
                            for t in range(TG):
                                gather(gp, hs[0:P, b, t, :], tab4, cur[0:P, b, t:t + 1], E - 1, d_ov[b])
                        for i, b, n in late(3):
                            gp.wait_ge(d_out[b], 16 * TG * i + 16)
                            gp.sem_inc(s.order, 1)
                            gp.tensor_copy(at[0:P, b], idx[0:P, LAST, tiles(n)]).then_inc(s.at, 1)
                            gp.wait_ge(s.at, n + 1 + C)
                            gp.sem_inc(s.order, 1)
                            gp.wait_ge(s.x, n + 1 + C)
                            gp.sem_inc(s.order, 1)
                            for t in range(TG):
                                gp.indirect_dma_start(out, bass.IndirectOffsetOnAxis(at[0:P, b, t:t + 1], 0),
                                                      xd[0:P, b, t, :], None, bounds_check=N - 1,
                                                      oob_is_err=False).then_inc(d_out[b], 16)
                    for b in range(SL):
                        count_one(gp, xd[0:P, b, 0, :], tab4, d_out[b])
                    staggered(gp, step, 3)
                    for b in range(SL):
                        gp.wait_ge(d_out[b], 16 * TG * SI + 16)

                @blk.vector
                def _(v):
                    start(v, s, d_hs, d_gd, d_xd)
                    v.memset(sums[:, :, :], 0.0).then_inc(s.sum, 1)
                    v.wait_ge(s.sum, 1 + C)

                    def step(late):
                        for i, b, n in late(0):
                            v.wait_ge(s.ps, reused(n))
                            select(v, dst_f, sel[:, b], n).then_inc(s.sel, 1)
                            v.wait_ge(d_hs[b], landed(i))
                            v.wait_ge(d_gd[b], landed(i))
                            v.wait_ge(d_ov[b], 16 * TG * (i + 1))
                            v.scalar_tensor_tensor(flat(m[0:P, b]), flat(hs[0:P, b]), 0.0, flat(gd[0:P, b]),
                                                   ALU.max, ALU.add).then_inc(s.m, 1)
                            v.wait_ge(s.ps, n + 1 + C)
                            run_carry(v, bank(PS_SUM), sums, s, b, n)
                        for i, b, n in late(1):
                            v.wait_ge(s.rows, n + 1 + C)
                            v.wait_ge(d_xd[b], landed(i))
                            v.tensor_tensor(flat(xd[0:P, b]), flat(xd[0:P, b]), bank(PS_OUT)[0:P], ALU.add).then_inc(s.x, 1)
                    staggered(v, step, 1)

                @blk.tensor
                def _(pe):
                    def step(late):
                        for i, b, n in late(1):
                            pe.wait_ge(s.sum, TG * (n + 1) + 1 + C)
                            for half in range(2):
                                pe.wait_ge(s.h, 2 * n + half - 1 + C)
                                pe.matmul(bank(PS_H + half)[:, 0:GR], w31[:, half * D:(half + 1) * D], sums[:, b, :],
                                          start=True, stop=True).then_inc(s.u, 1)
                        for i, b, n in late(0):
                            pe.wait_ge(s.sel, n + 1 + C)
                            pe.wait_ge(s.m, n + 1 + C)
                            pe.wait_ge(s.sum, TG * n + 1 + C)
                            run_sums(pe, bank(PS_SUM), m[:, b], sel[:, b]).then_inc(s.ps, 1)
                        for i, b, n in late(1):
                            pe.wait_ge(s.x, n + C)
                            bias_rows(pe, bank(PS_OUT), BIAS_32)
                            for half in range(2):
                                pe.wait_ge(s.h, 2 * n + half + 1 + C)
                                last = rows_times(pe, bank(PS_OUT), hT[:, b, half], w32[:, half, :], start=False, stop=half == 1)
                            last.then_inc(s.rows, 1)
                    staggered(pe, step, 1)

                @blk.scalar
                def _(act):
                    def turn(i, b, n):
                        for half in range(2):
                            act.wait_ge(s.rows, reused(n))
                            act.wait_ge(s.u, 2 * n + half + 1 + C)
                            act.activation(hT[:, b, half, :], bank(PS_H + half)[:, 0:GR], ACT.Relu,
                                           bias=b31_col[:, half:half + 1]).then_inc(s.h, 1)
                    in_order(act, turn)

        convolution("c", True, slots(xn0_src), slots(tab1), tab1, None, [slots(tab2)])
        convolution("d", False, slots(hid_src), slots(tab2), tab2, slots(x1_dst), [slots(tab3), slots(x2_dst)])
        message_layer()
        isomorphism_layer()


_INS = ['x', 'src', 'dst', 'L0_gnn_W', 'L0_gnn_source_scorer', 'L0_gnn_target_scorer', 'L1_gnn_ctx', 'L1_gnn_W1',
        'L1_gnn_b1', 'L1_gnn_W2', 'L1_gnn_b2', 'L1_gnn_Wg', 'L1_gnn_bg', 'L1_gnn_Wb', 'L2_gnn_W_msg1',
        'L2_gnn_b_msg1', 'L2_gnn_W_msg2', 'L2_gnn_b_msg2', 'L2_gnn_W_upd1', 'L2_gnn_b_upd1', 'L2_gnn_W_upd2',
        'L2_gnn_b_upd2', 'L3_gnn_W1', 'L3_gnn_b1', 'L3_gnn_W2', 'L3_gnn_b2']


def kernel(**inputs):
    import numpy as _np
    import concourse.bacc as _bacc
    from concourse import mybir as _mybir
    from concourse.bass_utils import run_bass_kernel_spmd as _run

    nc = _bacc.Bacc("TRN2", target_bir_lowering=False, num_devices=1)
    arrays, tensors = {}, {}
    for name in _INS:
        a = _np.ascontiguousarray(inputs[name])
        arrays[f"in_{name}"] = a
        tensors[name] = nc.dram_tensor(f"in_{name}", a.shape, _mybir.dt.from_np(a.dtype), kind="ExternalInput").ap()
    shape = tuple(inputs["x"].shape)
    out = nc.dram_tensor("out_x", shape, _mybir.dt.float32, kind="ExternalOutput").ap()
    gnn_four_layers(nc, tensors, out)
    r = _run(nc, [arrays], core_ids=[0])
    return r.results[0]["out_x"]
```
